# Optimizing a Trainium2 kernel written in Bass

```python
import numpy as np
import jax
import jax.numpy as jnp

def _softmax(x, axis=-1):
    return jax.nn.softmax(x, axis=axis)

def _gelu(x):
    return jax.nn.gelu(x, approximate=True)

def _silu(x):
    return jax.nn.silu(x)

def _sigmoid(x):
    return jax.nn.sigmoid(x)

def _layernorm(x, axis=-1, eps=1e-05):
    m = jnp.mean(x, axis=axis, keepdims=True)
    v = jnp.var(x, axis=axis, keepdims=True)
    return (x - m) / jnp.sqrt(v + eps)

def _scatter_add(tgt, idx, src, axis=0):
    return tgt.at[idx].add(src)

def _segment_sum(src, seg, n):
    return jax.ops.segment_sum(src, seg, n)
kernel_name = 'mk_gps_d1_gnn_r8_06b73c'

def setup_inputs(seed: int=0):
    np.random.seed(seed)
    _w = jnp.asarray

    def _rec_inputs():
        import jax
        import jax.numpy as jnp
        _gk = jax.random.key(seed)
        x = -0.0002117 + 1 * jax.random.normal(jax.random.fold_in(_gk, 1), (12500, 256), jnp.float32)
        src = jax.random.randint(jax.random.fold_in(_gk, 2), (200000,), 0, 12500, jnp.int32)
        dst = jax.random.randint(jax.random.fold_in(_gk, 3), (200000,), 0, 12500, jnp.int32)
        _o = jnp.argsort(dst, stable=True)
        src = src[_o]
        dst = dst[_o]
        return (x, src, dst)
    x, src, dst = _rec_inputs()

    def _L0_gnn_setup():
        import jax, jax.numpy as jnp
        import numpy as np
        N = 12500
        E = 200000
        IN = 256
        H = 4
        C = 64
        key = jax.random.key(seed)
        k1, k2, k3, k4, k5, k6 = jax.random.split(key, 6)
        x = jax.random.normal(k1, (N, IN), dtype=jnp.float32)
        edge_index = jax.random.randint(k2, (2, E), 0, N, dtype=jnp.int64)
        W = jax.random.normal(k3, (IN, H * C), dtype=jnp.float32) * (1.0 / np.sqrt(IN))
        att_src = jax.random.normal(k4, (H, C), dtype=jnp.float32) * 0.1
        att_dst = jax.random.normal(k5, (H, C), dtype=jnp.float32) * 0.1
        bias = jax.random.normal(k6, (H * C,), dtype=jnp.float32) * 0.01
        return {'x': x, 'edge_index': edge_index, 'W': W, 'att_src': att_src, 'att_dst': att_dst, 'bias': bias}
    _L0_gnn_all = _L0_gnn_setup()
    _L0_gnn_in = {k: v for k, v in _L0_gnn_all.items() if k in ('W', 'att_src', 'att_dst', 'bias')}
    del _L0_gnn_all

    def _L0_mix_setup():
        import jax, jax.numpy as jnp
        import numpy as np
        MIDC = 256
        HEADS = 8
        HEADC = MIDC // HEADS
        EPS = 1e-05

        def _ln(x, gamma, beta):
            mu = jnp.mean(x, axis=-1, keepdims=True)
            var = jnp.var(x, axis=-1, keepdims=True)
            return (x - mu) * jax.lax.rsqrt(var + EPS) * gamma + beta
        key = jax.random.key(seed)
        ks = jax.random.split(key, 8)
        B, HW, C = (8, 512, MIDC)
        s = 1.0 / np.sqrt(C)
        return {'x': jax.random.normal(ks[0], (B, HW, C), jnp.float32), 'w_qkv': jax.random.normal(ks[1], (C, 3 * C), jnp.float32) * s, 'b_qkv': jnp.zeros((3 * C,), jnp.float32), 'kln_g': jnp.ones((HEADC,), jnp.float32), 'kln_b': jnp.zeros((HEADC,), jnp.float32), 'vln_g': jnp.ones((HEADC,), jnp.float32), 'vln_b': jnp.zeros((HEADC,), jnp.float32), 'w1': jax.random.normal(ks[2], (C, C), jnp.float32) * s, 'b1': jnp.zeros((C,), jnp.float32), 'w2': jax.random.normal(ks[3], (C, C), jnp.float32) * s, 'b2': jnp.zeros((C,), jnp.float32)}
    _L0_mix_all = _L0_mix_setup()
    _L0_mix_in = {k: v for k, v in _L0_mix_all.items() if k in ('w_qkv', 'b_qkv', 'kln_g', 'kln_b', 'vln_g', 'vln_b', 'w1', 'b1', 'w2', 'b2')}
    del _L0_mix_all

    def _L0_ffn_setup():
        import jax, jax.numpy as jnp
        import numpy as np
        B, S, D = (8, 512, 256)
        H = 4 * D
        CAPACITY = 0.5
        key = jax.random.key(seed)
        ks = jax.random.split(key, 6)
        x = jax.random.normal(ks[0], (B, S, D), dtype=jnp.float32)
        attention_mask = jnp.zeros((B, 1, 1, S), dtype=jnp.float32)
        wr = jax.random.normal(ks[1], (D, 1), dtype=jnp.float32) * 0.02
        br = jnp.zeros((1,), dtype=jnp.float32)
        w1 = jax.random.normal(ks[2], (D, H), dtype=jnp.float32) * 0.02
        b1 = jnp.zeros((H,), dtype=jnp.float32)
        w2 = jax.random.normal(ks[3], (H, D), dtype=jnp.float32) * 0.02
        b2 = jnp.zeros((D,), dtype=jnp.float32)
        return {'x': x, 'attention_mask': attention_mask, 'wr': wr, 'br': br, 'w1': w1, 'b1': b1, 'w2': w2, 'b2': b2}
    _L0_ffn_all = _L0_ffn_setup()
    _L0_ffn_in = {k: v for k, v in _L0_ffn_all.items() if k in ('attention_mask', 'wr', 'br', 'w1', 'b1', 'w2', 'b2')}
    del _L0_ffn_all
    return {'x': x, 'src': src, 'dst': dst, 'L0_gnn_W': _L0_gnn_in['W'], 'L0_gnn_att_src': _L0_gnn_in['att_src'], 'L0_gnn_att_dst': _L0_gnn_in['att_dst'], 'L0_gnn_bias': _L0_gnn_in['bias'], 'L0_mix_w_qkv': _L0_mix_in['w_qkv'], 'L0_mix_b_qkv': _L0_mix_in['b_qkv'], 'L0_mix_kln_g': _L0_mix_in['kln_g'], 'L0_mix_kln_b': _L0_mix_in['kln_b'], 'L0_mix_vln_g': _L0_mix_in['vln_g'], 'L0_mix_vln_b': _L0_mix_in['vln_b'], 'L0_mix_w1': _L0_mix_in['w1'], 'L0_mix_b1': _L0_mix_in['b1'], 'L0_mix_w2': _L0_mix_in['w2'], 'L0_mix_b2': _L0_mix_in['b2'], 'L0_ffn_attention_mask': _L0_ffn_in['attention_mask'], 'L0_ffn_wr': _L0_ffn_in['wr'], 'L0_ffn_br': _L0_ffn_in['br'], 'L0_ffn_w1': _L0_ffn_in['w1'], 'L0_ffn_b1': _L0_ffn_in['b1'], 'L0_ffn_w2': _L0_ffn_in['w2'], 'L0_ffn_b2': _L0_ffn_in['b2']}

def reference(x, src, dst, L0_gnn_W, L0_gnn_att_src, L0_gnn_att_dst, L0_gnn_bias, L0_mix_w_qkv, L0_mix_b_qkv, L0_mix_kln_g, L0_mix_kln_b, L0_mix_vln_g, L0_mix_vln_b, L0_mix_w1, L0_mix_b1, L0_mix_w2, L0_mix_b2, L0_ffn_attention_mask, L0_ffn_wr, L0_ffn_br, L0_ffn_w1, L0_ffn_b1, L0_ffn_w2, L0_ffn_b2):
    import jax
    import jax.numpy as jnp

    def _L0_gnn_ref(x, edge_index, W, att_src, att_dst, bias):
        import jax, jax.numpy as jnp
        import numpy as np
        N = 12500
        E = 200000
        IN = 256
        H = 4
        C = 64
        n = x.shape[0]
        loops = jnp.arange(n, dtype=edge_index.dtype)
        src = jnp.concatenate([edge_index[0], loops])
        dst = jnp.concatenate([edge_index[1], loops])
        xp = (x @ W).reshape(n, H, C)
        a_src = jnp.einsum('nhc,hc->nh', xp, att_src)
        a_dst = jnp.einsum('nhc,hc->nh', xp, att_dst)
        alpha = jax.nn.leaky_relu(a_src[src] + a_dst[dst], negative_slope=0.2)
        amax = jax.ops.segment_max(alpha, dst, num_segments=n)
        amax = jnp.where(jnp.isfinite(amax), amax, 0.0)
        ex = jnp.exp(alpha - amax[dst])
        denom = jax.ops.segment_sum(ex, dst, num_segments=n)
        w = ex / denom[dst]
        msg = xp[src] * w[..., None]
        agg = jax.ops.segment_sum(msg, dst, num_segments=n)
        out = agg.reshape(n, H * C) + bias
        return jax.nn.elu(out)

    def _L0_mix_ref(x, w_qkv, b_qkv, kln_g, kln_b, vln_g, vln_b, w1, b1, w2, b2):
        import jax, jax.numpy as jnp
        import numpy as np
        MIDC = 256
        HEADS = 8
        HEADC = MIDC // HEADS
        EPS = 1e-05

        def _ln(x, gamma, beta):
            mu = jnp.mean(x, axis=-1, keepdims=True)
            var = jnp.var(x, axis=-1, keepdims=True)
            return (x - mu) * jax.lax.rsqrt(var + EPS) * gamma + beta
        B, HW, C = x.shape
        bias = x
        qkv = (x @ w_qkv + b_qkv).reshape(B, HW, HEADS, 3 * HEADC)
        qkv = qkv.transpose(0, 2, 1, 3)
        q, k, v = jnp.split(qkv, 3, axis=-1)
        k = _ln(k, kln_g, kln_b)
        v = _ln(v, vln_g, vln_b)
        kv = jnp.einsum('bhnd,bhne->bhde', k, v) / HW
        out = jnp.einsum('bhnd,bhde->bhne', q, kv)
        out = out.transpose(0, 2, 1, 3).reshape(B, HW, C)
        ret = out + bias
        h = jax.nn.gelu(ret @ w1 + b1, approximate=False)
        return h @ w2 + b2 + bias

    def _L0_ffn_ref(x, attention_mask, wr, br, w1, b1, w2, b2):
        import jax, jax.numpy as jnp
        import numpy as np
        B, S, D = (8, 512, 256)
        H = 4 * D
        CAPACITY = 0.5
        b, s, d = x.shape
        weights = (jnp.einsum('bsd,do->bso', x, wr) + br)[..., 0]
        k = max(1, int(CAPACITY * s))
        kk = k - 1 if k > 1 else 1
        _, idx = jax.lax.top_k(weights, k)
        sel_idx = idx[:, :kk]
        sel = jnp.take_along_axis(x, sel_idx[:, :, None], axis=1)
        h = jax.nn.gelu(jnp.einsum('bkd,dh->bkh', sel, w1) + b1)
        y = jnp.einsum('bkh,hd->bkd', h, w2) + b2
        w_sel = jnp.take_along_axis(weights, sel_idx, axis=1)
        y = y * w_sel[..., None]
        batch_idx = jnp.arange(b)[:, None]
        processed = jnp.zeros_like(x).at[batch_idx, sel_idx].set(y)
        return processed + x
    edge_index = jnp.stack([src, dst])
    xn = _layernorm(x, axis=-1)
    x = x + _L0_gnn_ref(xn, edge_index, L0_gnn_W, L0_gnn_att_src, L0_gnn_att_dst, L0_gnn_bias) + _L0_mix_ref(xn[None], L0_mix_w_qkv, L0_mix_b_qkv, L0_mix_kln_g, L0_mix_kln_b, L0_mix_vln_g, L0_mix_vln_b, L0_mix_w1, L0_mix_b1, L0_mix_w2, L0_mix_b2)[0]
    x = x + _L0_ffn_ref(_layernorm(x, axis=-1)[None], L0_ffn_attention_mask, L0_ffn_wr, L0_ffn_br, L0_ffn_w1, L0_ffn_b1, L0_ffn_w2, L0_ffn_b2)[0]
    return x

_drawn_inputs = setup_inputs


def setup_inputs(seed=0):
    import zlib

    import numpy as np

    out = dict(_drawn_inputs(seed))
    spreads = {'L0_mix_b_qkv': (0.0, 0.1),
     'L0_mix_kln_g': (1.0, 0.6),
     'L0_mix_kln_b': (0.0, 0.446),
     'L0_mix_vln_g': (1.0, 0.6),
     'L0_mix_vln_b': (0.0, 0.401),
     'L0_mix_b1': (0.0, 0.1),
     'L0_mix_b2': (0.0, 0.1),
     'L0_ffn_b1': (0.0, 0.8),
     'L0_ffn_b2': (0.0, 0.8)}
    factors = {'L0_gnn_bias': 8.0, 'L0_ffn_wr': 5.584, 'L0_ffn_w1': 6.265, 'L0_ffn_w2': 5.89}
    for name, (base, spread) in spreads.items():
        noise = np.random.default_rng([zlib.crc32(name.encode()), seed]).standard_normal(out[name].shape)
        drawn = base * np.exp(spread * noise) if base else spread * noise
        out[name] = jnp.asarray(drawn.astype(out[name].dtype))
    for name, factor in factors.items():
        out[name] = (out[name] * factor).astype(out[name].dtype)
    return out
```

```python
import numpy as np
import concourse.bass as bass
from concourse import mybir
from contextlib import ExitStack

FP32 = mybir.dt.float32
BF16 = mybir.dt.bfloat16
I32 = mybir.dt.int32
I16 = mybir.dt.int16
ALU = mybir.AluOpType
ACT = mybir.ActivationFunctionType
AX = mybir.AxisListType.X
P = 128
CT = 32
ST_T = 4
BIG = 1e38


def ds(start, size):
    return bass.ds(start, size)


class Chain:

    def __init__(self, eng, sem, base=0):
        self.eng, self.sem, self.base, self.n = eng, sem, base, 0

    def __call__(self, ins):
        ins.then_inc(self.sem, 1)
        self.n += 1
        self.eng.wait_ge(self.sem, self.base + self.n)


def gps_kernel(nc, n_nodes, n_edges, x, src, dst, Wg, att_src, att_dst, g_bias, w_qkv, b_qkv, kln_g, kln_b,
               vln_g, vln_b, m_w1, m_b1, m_w2, m_b2, f_wr, f_br, f_w1, f_b1, f_w2, f_b2, out):
    D, HG, HM = 256, 4, 8
    CG, CM = D // HG, D // HM
    FH = 4 * D
    FC = FH // P
    NPAD = x.shape[0]
    NB = NPAD // P
    NP = NB // 2
    EP = src.shape[0]
    NT = EP // P
    NST = NT // ST_T
    SC = CT // ST_T
    NCH = NT // CT
    NI = NST + NB - 1
    ROW = D + 2 * HG
    K_SEL = max(1, int(0.5 * n_nodes)) - 1
    EPS = 1e-5
    TAIL = n_nodes - (NB - 1) * P
    assert NB == 2 * NP and NP == NCH and NP % 2 == 1 and NI <= 512 and n_edges <= EP

    ctx = ExitStack()
    with ctx:
        def sb(name, shape, dt=FP32):
            return ctx.enter_context(nc.sbuf_tensor(name, shape, dt))

        def sem(name):
            return ctx.enter_context(nc.semaphore(name))

        tab_d = nc.dram_tensor("tab_d", [NPAD, ROW], FP32).ap()
        xnT_d = nc.dram_tensor("xnT_d", [NP, P, 2 * 2 * P], FP32).ap()
        srcE_d = nc.dram_tensor("srcE_d", [P, NT], I32).ap()
        dstE_d = nc.dram_tensor("dstE_d", [P, NT], FP32).ap()
        dst16_d = nc.dram_tensor("dst16_d", [P, NT], I16).ap()
        base_d = nc.dram_tensor("base_d", [NPAD, D], FP32).ap()

        bank = [ctx.enter_context(nc.psum_tensor(f"bank{i}", [P, 512], FP32)) for i in range(3)]
        two = ctx.enter_context(nc.psum_tensor("two", [P, 2, 512], FP32))
        bank += [two[:, 0, :], two[:, 1, :]]
        bank += [ctx.enter_context(nc.psum_tensor(f"bank{i}", [P, 512], FP32)) for i in range(5, 8)]

        def sums(i):
            return two[:, ds(i % 2, 1), 0:ROW].rearrange("p a r -> p (a r)")

        accf = sb("acc", [P, max(NB * ROW, 6400)])[:, :]
        acc = accf[:, 0:NB * ROW].rearrange("p (b r) -> p b r", r=ROW)
        iota_f = sb("iota_f", [P, P])
        pcol = sb("pcol", [P, 1])
        ident = sb("ident", [P, P])
        ones = sb("ones", [P, P])
        stat = sb("stat", [P, NB, 2])
        wnode = sb("wnode", [P, NB])
        kvw = sb("kvw", [P, 2, 2 * D])
        bkv = sb("bkv", [P, 2 * D])
        valid_last = sb("valid_last", [P, 1])
        item_base = sb("item_base", [P, NI])
        nodeval = sb("nodeval", [P, NB, 3, 2 * HG], BF16)

        G = sb("G", [P, 2, CT, ROW])
        sidx = sb("sidx", [P, 2, CT], I32)
        dstE = sb("dstE", [P, 2, CT])
        drow = sb("drow", [P, 2, P + 2], I32)
        shared = sb("shared", [P, CT * P // 2])
        dbc = shared[:, :].bitcast(I16)
        kv = shared[:, 0:4 * D].rearrange("p (a n) -> p a n", a=2)
        sq = shared[:, 4 * D:6 * D]
        oneT = sb("oneT", [P, ST_T * P], BF16)
        zb = sb("zb", [P, 512], BF16)
        oneE = sb("oneE", [P, ST_T, P])
        xtk = oneE[:, :, :].rearrange("p (k b) n -> p k (b n)", k=2)
        work = sb("work", [P, 2356])
        o = [0]

        def piece(n, p=P):
            a = work[0:p, o[0]:o[0] + n]
            o[0] += n
            return a

        dn = piece(CT * 8)
        U = piece(3 * P)
        s_e, sT, bw = (U[:, k * P:(k + 1) * P] for k in range(3))
        pn = piece(2 * (P + 1))
        We = pn[:, 0:2 * P]
        pen, neq = pn[:, 0:P + 1], pn[:, P + 1:]
        sng = piece(1)
        x4 = piece(4)
        first = piece(P)
        fw = piece(P)
        c2 = piece(2)
        fac = piece(HG)
        g0 = o[0]
        gh = piece(6 * HG * (CT + 1), 1)
        item_block = work[32:33, g0:g0 + NI].bitcast(I32)
        item_tile = work[64:65, g0:g0 + NI].bitcast(I32)
        chunk_item = work[96:97, g0:g0 + NCH + 1].bitcast(I32)
        cin = piece(2 * P, 1)
        rl = piece(HG, 1)
        r8 = piece(2 * HG, 1)
        one0 = piece(P, 1)
        rs = sb("rs", [P, 2, 16])

        Gf = G[:, :, :, :].rearrange("p a t r -> p (a t r)")
        go = [0]

        def gpiece(n):
            a = Gf[:, go[0]:go[0] + n]
            go[0] += n
            return a

        bar = sem("bar")
        phase = [0]
        d32_in = sem("d32_in")
        ld_w, ld_i, iota_done = sem("ld_w"), sem("ld_i"), sem("iota_done")
        prep_mm, prep_dve, vch = sem("prep_mm"), sem("prep_dve"), sem("vch")
        idx_in = [sem("idx_in0"), sem("idx_in1")]
        idx_f, idx_t, idx_out = sem("idx_f"), sem("idx_t"), sem("idx_out")
        idx_stored = [sem("idx_stored0"), sem("idx_stored1")]
        d16_ready, d16_stored = sem("d16_ready"), sem("d16_stored")
        x_in = [sem("x_in0"), sem("x_in1")]
        x_var, x_std, xn_ready, xn_T, xt_ready, xp_ready, row_ready = (
            sem("x_var"), sem("x_std"), sem("xn_ready"), sem("xn_T"), sem("xt_ready"), sem("xp_ready"), sem("row_ready"))
        row_split, vln = sem("row_split"), sem("vln")
        tab_out = [sem("tab_out0"), sem("tab_out1")]
        xt_out = [sem("xt_out0"), sem("xt_out1")]
        idx_ld = [sem("idx_ld0"), sem("idx_ld1")]
        rows_in = [sem("rows_in0"), sem("rows_in1")]
        drow_in = [sem("drow_in0"), sem("drow_in1")]
        dbc_in, xtk_in = sem("dbc_in"), sem("xtk_in")
        dz, ot_ready, ot_used, d_read, s_ready, sT_ready = (
            sem("dz"), sem("ot_ready"), sem("ot_used"), sem("d_read"), sem("s_ready"), sem("sT_ready"))
        x4_ready, r_ready, gh_ready, c_ready, mm_ready, m_ready = (
            sem("x4_ready"), sem("r_ready"), sem("gh_ready"), sem("c_ready"), sem("mm_ready"), sem("m_ready"))
        u_ready, w_ready, one0_ready, fac_ready = sem("u_ready"), sem("w_ready"), sem("one0_ready"), sem("fac_ready")
        oe_ready, oe_used, sum_added = sem("oe_ready"), sem("oe_used"), sem("sum_added")
        chunk_done, vck = sem("chunk_done"), sem("vck")
        kv_mm, kv_biased, kv_sq, kv_var, kv_std, kv_norm, kv_acc = (
            sem("kv_mm"), sem("kv_biased"), sem("kv_sq"), sem("kv_var"), sem("kv_std"), sem("kv_norm"), sem("kv_acc"))
        pace = sem("pace")
        mw_in, mw_pe, mw_dve = sem("mw_in"), sem("mw_pe"), sem("mw_dve")
        n_in = [sem("n_in0"), sem("n_in1")]
        h_mm, h_act, o_mm, e_in, e_out, v_var, v_std = (
            sem("h_mm"), sem("h_act"), sem("o_mm"), sem("e_in"), sem("e_out"), sem("v_var"), sem("v_std"))
        z_ready, zT_ready, zT_stored, b_ready, n_read, vnp = (
            sem("z_ready"), sem("zT_ready"), sem("zT_stored"), sem("b_ready"), sem("n_read"), sem("vnp"))
        b_out = [sem("b_out0"), sem("b_out1")]
        vth, cnt_ready, cnt_sum = sem("vth"), sem("cnt_ready"), sem("cnt_sum")
        f_in = sem("f_in")
        b_in = [sem("b_in0"), sem("b_in1")]
        f_up, f_act, f_down, f_y, f_out, vff = (
            sem("f_up"), sem("f_act"), sem("f_down"), sem("f_y"), [sem("f_out0"), sem("f_out1")], sem("vff"))

        block = ctx.enter_context(nc.Block())

        def settled(eng, semaphore, value):
            eng.wait_ge(semaphore, value)
            eng.sem_inc(pace, 1)

        def barrier(eng, n):
            eng.drain().then_inc(bar, 1)
            eng.wait_ge(bar, 5 * n)

        go[0] = 0
        wcat = gpiece(2 * ROW).rearrange("p (c n) -> p c n", c=2)
        attb = gpiece(2 * D).rearrange("p (a n) -> p a n", a=2)
        wtmp = gpiece(2 * D).rearrange("p (a n) -> p a n", a=2)
        wraw = gpiece(2 * 3 * D).rearrange("p (c n) -> p c n", c=2)
        braw = gpiece(3 * D)
        wmean = gpiece(48)
        iotaI = gpiece(512).bitcast(I32)
        pcolI = gpiece(1).bitcast(I32)
        iota_w = gpiece(512)
        samp = gpiece(NST)
        sampF = gpiece(NST)
        tmp512 = gpiece(512)
        small = gpiece(16)
        cmp2 = gpiece(64)
        go[0] += go[0] % 2
        idxI = gpiece(2 * 2 * P).bitcast(I32).rearrange("p (a k n) -> p a k n", a=2, k=2)
        idxF = gpiece(2 * P).rearrange("p (k n) -> p k n", k=2)
        idxO = gpiece(2 * 2 * P).rearrange("p (a k n) -> p a k n", a=2, k=2)
        ao = [0]

        def apiece(n):
            a = accf[:, ao[0]:ao[0] + n]
            ao[0] += n
            return a

        d32 = gpiece(1024).bitcast(I32)
        d16 = dbc[:, 0:NT]
        xin = apiece(2 * 2 * D).rearrange("p (a t n) -> p a t n", a=2, t=2)
        xn = apiece(2 * 2 * D).rearrange("p (a t n) -> p a t n", a=2, t=2)
        xt = apiece(2 * 4 * P).rearrange("p (a k n) -> p a k n", a=2, k=2)
        xrow = apiece(2 * 2 * ROW).rearrange("p (a t n) -> p a t n", a=2, t=2)
        bst = apiece(16)
        var = apiece(4)
        mv = apiece(4).rearrange("p (t k) -> p t k", t=2)
        res = apiece(2 * 2 * 8).rearrange("p (a t n) -> p a t n", a=2, t=2)
        DQ = (NT + 1023) // 1024

        x_v = x.rearrange("(q t p) n -> q p t n", t=2, p=P)
        tab_v = tab_d.rearrange("(q t p) n -> q p t n", t=2, p=P)
        base_v = base_d.rearrange("(q t p) n -> q p t n", t=2, p=P)
        out_v = out.rearrange("(q t p) n -> q p t n", t=2, p=P)
        src_t = src.rearrange("(t e) -> t e", e=P)
        dst_t = dst[1:1 + EP].rearrange("(t e) -> t e", e=P)
        NG = (NT + P - 1) // P

        def grp(g):
            return min(P, NT - g * P)

        R2 = (NP - 1) // 2

        def paired(eng, body):
            with eng.Fori(0, R2) as r:
                body(2 * r, 0, r)
                body(2 * r + 1, 1, r)
            body(NP - 1, 0, R2)

        go[0] = 0
        wq = gpiece(2 * D).rearrange("p (c n) -> p c n", c=2)
        wqT = gpiece(2 * D).rearrange("p (c n) -> p c n", c=2)
        kvd = gpiece(2 * P).rearrange("p (c n) -> p c n", c=2)
        m1T = gpiece(2 * D).rearrange("p (c n) -> p c n", c=2)
        w1m = gpiece(2 * D).rearrange("p (c n) -> p c n", c=2)
        wm = gpiece(2 * D).rearrange("p (c n) -> p c n", c=2)
        w2m = gpiece(2 * D).rearrange("p (c n) -> p c n", c=2)
        b1m = gpiece(2)
        bm = gpiece(2)
        bq = gpiece(2)
        kqb = gpiece(2)
        kcol = gpiece(2)
        vrow = gpiece(2 * CM).rearrange("p (k n) -> p k n", k=2)
        svk = gpiece(4)
        mt1 = gpiece(P)
        mt2 = gpiece(P)
        gbr = gpiece(D)
        b2r = gpiece(D)
        wrr = gpiece(D)
        brc = gpiece(1)
        go[0] += go[0] % 2
        xl = gpiece(2 * 2 * D).rearrange("p (s t n) -> p s t n", s=2, t=2)
        xtl = gpiece(2 * 2 * D).rearrange("p (s k n) -> p s k n", s=2, k=2)
        xpl = gpiece(2 * 2 * D).rearrange("p (s t n) -> p s t n", s=2, t=2)
        t1, t2, t3, x2, zz = (gpiece(2 * D).rearrange("p (t n) -> p t n", t=2) for _ in range(5))
        hT = gpiece(2 * D).rearrange("p (k n) -> p k n", k=2)
        bb = gpiece(2 * 2 * D).rearrange("p (s t n) -> p s t n", s=2, t=2)
        bst2 = gpiece(12)
        mv2 = gpiece(4).rearrange("p (t k) -> p t k", t=2)
        var2 = gpiece(4)
        dsum, flg, wsp, rec = (gpiece(2 * HG).rearrange("p (t h) -> p t h", t=2) for _ in range(4))
        assert go[0] <= 2 * CT * ROW

        def load_mix(sp):
            wv = w_qkv.rearrange("(c p) (h n) -> p c h n", p=P, h=HM)
            for c in (0, 1):
                sp.dma_start(wq[:, c, :].rearrange("p (h n) -> p h n", h=HM), wv[:, c, :, 0:CM]).then_inc(mw_in, 16)
            sp.dma_start(w1m, m_w1.rearrange("(c p) n -> p c n", p=P)).then_inc(mw_in, 16)
            sp.dma_start(w2m, m_w2.rearrange("(c p) n -> p c n", p=P)).then_inc(mw_in, 16)
            bqv = b_qkv.rearrange("(c h n) -> c h n", c=2, n=3 * CM)[:, :, 0:CM]
            for c in (0, 1):
                sp.dma_start(b1m[:, c:c + 1], m_b1[c * P:(c + 1) * P][:, None]).then_inc(mw_in, 16)
                for h in range(P // CM):
                    sp.dma_start(bq[h * CM:(h + 1) * CM, c:c + 1], bqv[c, h][:, None]).then_inc(mw_in, 16)
            for k, a in ((0, kln_g), (1, kln_b)):
                for h in range(P // CM):
                    sp.dma_start(kcol[h * CM:(h + 1) * CM, k:k + 1], a[:, None]).then_inc(mw_in, 16)
            for k, a in ((0, vln_g), (1, vln_b)):
                sp.dma_start(vrow[:, k, :], a[None, :].to_broadcast([P, CM])).then_inc(mw_in, 16)
            sp.dma_start(gbr, g_bias[None, :].to_broadcast([P, D])).then_inc(mw_in, 16)
            sp.dma_start(b2r, m_b2[None, :].to_broadcast([P, D])).then_inc(mw_in, 16)
            sp.dma_start(wrr, f_wr.rearrange("d o -> o d").to_broadcast([P, D])).then_inc(mw_in, 16)
            sp.dma_start(brc, f_br[None, :].to_broadcast([P, 1])).then_inc(mw_in, 16)

        MW = 16 * (4 + 2 * (1 + P // CM) + 2 * (P // CM) + 2 + 4)

        def mix_weights_dve(dve, lk):
            v = nc.vector
            dve.wait_ge(mw_in, MW)
            lk(v.tensor_scalar(b2r, b2r, -1.0, None, ALU.add))
            lk(v.memset(kvd, 0.0))
            v.sem_inc(mw_dve, 1)
            gain = vrow[:, None, 0, :].to_broadcast([P, P // CM, CM])
            bias = vrow[:, None, 1, :].to_broadcast([P, P // CM, CM])

            def hv(a):
                return a.rearrange("p (h n) -> p h n", n=CM)

            for c in (0, 1):
                lk(v.tensor_scalar(mt1, bank[5][:, c * P:c * P + P], kcol[:, 0:1], None, ALU.mult))
                lk(v.tensor_tensor(hv(mt1), hv(mt1), gain, ALU.mult))
                lk(v.tensor_scalar(mt2, bank[6][:, c * P:c * P + P], kcol[:, 1:2], None, ALU.mult))
                lk(v.tensor_tensor(hv(mt2), hv(mt2), gain, ALU.mult))
                lk(v.tensor_tensor(mt1, mt1, mt2, ALU.add))
                lk(v.tensor_scalar(svk[:, 0:1], bank[5][:, 256 + c:257 + c], kcol[:, 0:1], None, ALU.mult))
                lk(v.scalar_tensor_tensor(svk[:, 0:1], kcol[:, 1:2], float(n_nodes), svk[:, 0:1], ALU.mult, ALU.add))
                lk(v.tensor_scalar(hv(mt2), bias, svk[:, 0:1], None, ALU.mult))
                lk(v.tensor_tensor(mt1, mt1, mt2, ALU.add))
                for h in range(P // CM):
                    r = slice(h * CM, (h + 1) * CM)
                    lk(v.tensor_scalar(kvd[r, c, r], mt1[r, r], 1.0 / n_nodes, None, ALU.mult))
            v.sem_inc(mw_dve, 1)
            dve.wait_ge(mw_pe, 1)
            for c in (0, 1):
                lk(v.tensor_copy(wqT[:, c, :], bank[c][:, 0:D]))
            v.sem_inc(mw_dve, 1)
            dve.wait_ge(mw_pe, 2)
            for c in (0, 1):
                lk(v.tensor_copy(m1T[:, c, :], bank[3 + c][:, 0:D]))
                lk(v.tensor_tensor(m1T[:, c, c * P:c * P + P], m1T[:, c, c * P:c * P + P], ident[:, :], ALU.add))
                lk(v.tensor_copy(kqb[:, c:c + 1], bank[2][:, c:c + 1]))
            v.sem_inc(mw_dve, 1)
            dve.wait_ge(mw_pe, 3)
            for c in (0, 1):
                lk(v.tensor_copy(wm[:, c, :], bank[c][:, 0:D]))
                lk(v.tensor_tensor(bm[:, c:c + 1], bank[2][:, 4 + c:5 + c], b1m[:, c:c + 1], ALU.add))

        def mix_weights_pe(pe):
            te = nc.tensor
            pe.wait_ge(mw_dve, 1)
            for c in (0, 1):
                for k in (0, 1):
                    last = te.transpose(bank[c][:, k * P:k * P + P], wq[:, k, c * P:c * P + P], ident[:, :])
            last.then_inc(mw_pe, 1)
            pe.wait_ge(mw_dve, 3)
            for c in (0, 1):
                te.matmul(bank[3 + c][:, 0:D], kvd[:, c, :], wqT[:, c, :], start=True, stop=True)
                last = te.matmul(bank[2][:, c:c + 1], kvd[:, c, :], bq[:, c:c + 1], start=True, stop=True)
            last.then_inc(mw_pe, 1)
            pe.wait_ge(mw_dve, 4)
            for c in (0, 1):
                for k in (0, 1):
                    te.matmul(bank[c][:, 0:D], m1T[:, k, c * P:c * P + P], w1m[:, k, :], start=(k == 0), stop=(k == 1))
            for c in (0, 1):
                for k in (0, 1):
                    last = te.matmul(bank[2][:, 4 + c:5 + c], w1m[:, k, c * P:c * P + P], kqb[:, k:k + 1], start=(k == 0), stop=(k == 1))
            last.then_inc(mw_pe, 1)

        def node_loads(sp):
            def load(q, s):
                sp.dma_start(xl[:, s, :, :], x_v[ds(q, 1)].rearrange("a p t n -> p (a t) n")).then_inc(n_in[s], 16)
                sp.dma_start(xpl[:, s, :, :], tab_v[ds(q, 1)].rearrange("a p t n -> p (a t) n")[:, :, 0:D]).then_inc(n_in[s], 16)
                sp.dma_start(xtl[:, s, :, :], xnT_d[ds(q, 1)].rearrange("a p (k n) -> p (a k) n", k=2)).then_inc(n_in[s], 16)

            def step(q, s, more=True):
                if more:
                    settled(sp, n_read, q + 1)
                    load(q + 2, s)
                settled(sp, b_ready, q + 1)
                sp.dma_start(base_v[ds(q, 1)].rearrange("a p t n -> p (a t) n"), bb[:, s, :, :]).then_inc(b_out[s], 16)

            load(0, 0)
            load(1, 1)
            with sp.Fori(0, R2 - 1) as r:
                step(2 * r, 0)
                step(2 * r + 1, 1)
            step(NP - 3, 0)
            step(NP - 2, 1, False)
            step(NP - 1, 0, False)
            for s in (0, 1):
                sp.wait_ge(b_out[s], 16 * (R2 + 1 - s))

        def node_dve(dve):
            v = nc.vector
            KNP = 24

            def body(q, s, r, first):
                ck = Chain(dve, vnp, KNP * q)
                aq = acc[:, ds(2 * q, 2), :]
                dve.wait_ge(n_in[s], 48 * r + 48)
                ck(v.tensor_tensor(dsum, aq[:, :, D:D + HG], aq[:, :, D + HG:ROW], ALU.add))
                ck(v.tensor_scalar(flg, dsum, 0.5, None, ALU.is_lt))
                v.tensor_tensor(wsp, aq[:, :, D + HG:ROW], flg, ALU.add)
                ck(v.tensor_tensor(dsum, dsum, flg, ALU.add))
                ck(v.reciprocal(rec, dsum))

                def heads(a):
                    return a.rearrange("p t (h n) -> p t h n", h=HG)

                def wide(a):
                    return a[:, :, :, None].to_broadcast([P, 2, HG, CG])

                ck(v.tensor_tensor(heads(t1), heads(xpl[:, s]), wide(wsp), ALU.mult))
                ck(v.tensor_tensor(t1, t1, aq[:, :, 0:D], ALU.add))
                ck(v.tensor_tensor(heads(t1), heads(t1), wide(rec), ALU.mult))
                ck(v.tensor_tensor(t1, t1, gbr[:, None, :].to_broadcast([P, 2, D]), ALU.add))
                ck(v.tensor_scalar(t2, t1, 0.0, None, ALU.min))
                v.sem_inc(e_in, 1)
                ck(v.tensor_copy(mv2, stat[:, ds(2 * q, 2), :]))
                for t in (0, 1):
                    last = v.tensor_scalar(t3[:, t, :], xl[:, s, t, :], mv2[:, t, 0:1], mv2[:, t, 1:2], ALU.subtract, ALU.mult)
                ck(last)
                ck(v.tensor_tensor(t3, t3, b2r[:, None, :].to_broadcast([P, 2, D]), ALU.add))
                ck(v.tensor_tensor(t3, t3, xl[:, s], ALU.add))
                dve.wait_ge(o_mm, q + 1)
                ck(v.tensor_tensor(t3, t3, bank[1][:, :].rearrange("p (t n) -> p t n", t=2), ALU.add))
                v.sem_inc(n_read, 1)
                dve.wait_ge(e_out, q + 1)
                ck(v.scalar_tensor_tensor(t1, t1, 0.0, t2, ALU.max, ALU.add))
                ck(v.tensor_tensor(x2, t1, t3, ALU.add))
                for t in (0, 1):
                    last = v.bn_stats(bst2[:, 6 * t:6 * t + 6], x2[:, t, :])
                ck(last)
                v.sem_inc(pace, 1)
                for t in (0, 1):
                    last = v.bn_aggr(mv2[:, t, :], bst2[:, 6 * t:6 * t + 6])
                ck(last)
                ck(v.tensor_scalar(var2[:, 0:2], mv2[:, :, 1], EPS, None, ALU.add))
                v.sem_inc(v_var, 1)
                dve.wait_ge(v_std, q + 1)
                ck(v.reciprocal(mv2[:, :, 1], var2[:, 2:4]))
                dve.wait_ge(zT_ready, q + 1)
                for t in (0, 1):
                    last = v.tensor_scalar(zz[:, t, :], x2[:, t, :], mv2[:, t, 0:1], mv2[:, t, 1:2], ALU.subtract, ALU.mult)
                ck(last)
                v.sem_inc(z_ready, 1)
                ck(v.tensor_tensor(t1, zz, wrr[:, None, :].to_broadcast([P, 2, D]), ALU.mult))
                ck(v.tensor_reduce(wnode[:, ds(2 * q, 2)], t1, AX, ALU.add))
                if not first:
                    dve.wait_ge(b_out[s], 16 * r)
                ck(v.tensor_tensor(bb[:, s], x2, zz, ALU.add))
                v.sem_inc(b_ready, 1)
                assert ck.n == KNP, ck.n

            body(0, 0, 0, True)
            body(1, 1, 0, True)
            with dve.Fori(1, R2) as r:
                body(2 * r, 0, r, False)
                body(2 * r + 1, 1, r, False)
            body(NP - 1, 0, R2, False)

        def node_act(act):
            a = nc.scalar

            def body(q, s, r):
                act.wait_ge(h_mm, q + 1)
                for k in (0, 1):
                    last = a.activation(hT[:, k, :], bank[0][:, k * D:k * D + D], ACT.Gelu, bias=bm[:, k:k + 1])
                last.then_inc(h_act, 1)
                act.wait_ge(e_in, q + 1)
                a.activation(t2, t2, ACT.Exp).then_inc(e_out, 1)
                act.wait_ge(v_var, q + 1)
                a.activation(var2[:, 2:4], var2[:, 0:2], ACT.Sqrt).then_inc(v_std, 1)
                act.wait_ge(zT_ready, q + 2)
                a.copy(accf[:, ds(2 * ROW * q, 2 * D)], bank[2][:, :]).then_inc(zT_stored, 1)

            paired(act, body)

        def node_pe(pe):
            te = nc.tensor
            pe.sem_inc(zT_ready, 1)
            pe.sem_inc(zT_stored, 1)

            def body(q, s, r):
                pe.wait_ge(n_in[s], 48 * r + 48)
                for f in (0, 1):
                    for k in (0, 1):
                        last = te.matmul(bank[0][:, f * D:f * D + D], wm[:, k, f * P:f * P + P], xtl[:, s, k, :], start=(k == 0), stop=(k == 1))
                last.then_inc(h_mm, 1)
                pe.wait_ge(h_act, q + 1)
                for t in (0, 1):
                    for k in (0, 1):
                        last = te.matmul(bank[1][:, t * D:t * D + D], hT[:, k, t * P:t * P + P], w2m[:, k, :], start=(k == 0), stop=(k == 1))
                last.then_inc(o_mm, 1)
                pe.wait_ge(z_ready, q + 1)
                pe.wait_ge(zT_stored, q + 1)
                for k in (0, 1):
                    for t in (0, 1):
                        last = te.transpose(bank[2][:, k * D + t * P:k * D + t * P + P], zz[:, t, k * P:k * P + P], ident[:, :])
                last.then_inc(zT_ready, 1)

            paired(pe, body)

        o[0] = 0
        wp, cmpb, rank, sel, eqm = (piece(NB) for _ in range(5))
        wcnt = piece(8)
        lower = piece(P)
        bits = piece(4)
        bits_i = piece(4).bitcast(I32)

        def threshold_dve(dve, lk):
            v = nc.vector
            cnt, c0, sg, kp, pen_l, need = (wcnt[:, i:i + 1] for i in range(6))
            cur, cand, bi = bits_i[:, 0:1], bits_i[:, 1:2], bits_i[:, 2:3]
            bit, keep, thr = bits[:, 0:1], bits[:, 1:2], bits[:, 2:3]
            lastcol = slice(NB - 1, NB)
            lk(v.tensor_scalar(wnode[:, :], wnode[:, :], brc, None, ALU.add))
            lk(v.tensor_scalar(pen_l, valid_last[:, :], -1.0, 3.0 * BIG, ALU.add, ALU.mult))
            lk(v.tensor_scalar(wnode[:, lastcol], wnode[:, lastcol], valid_last[:, :], pen_l, ALU.mult, ALU.add))
            lk(v.tensor_scalar(lower, iota_f[:, 0:P], pcol[:, :], None, ALU.is_gt))
            lk(v.tensor_scalar(cmpb, wnode[:, :], 0.0, None, ALU.is_ge))
            lk(v.tensor_reduce(cnt, cmpb, AX, ALU.add))
            v.sem_inc(cnt_ready, 1)
            dve.wait_ge(cnt_sum, 1)
            lk(v.tensor_scalar(c0, bank[3][:, 0:1], float(K_SEL), None, ALU.is_ge))
            lk(v.tensor_scalar(sg, c0, 2.0, -1.0, ALU.mult, ALU.add))
            lk(v.tensor_scalar(kp, c0, float(2 * K_SEL - n_nodes - 1), float(n_nodes - K_SEL + 1), ALU.mult, ALU.add))
            lk(v.tensor_scalar(wp, wnode[:, :], sg, None, ALU.mult))
            lk(v.tensor_scalar(wp[:, lastcol], wp[:, lastcol], valid_last[:, :], pen_l, ALU.mult, ALU.add))
            lk(v.memset(bits_i, 0))
            lk(v.memset(bit, float(2 ** 30)))
            KTH = 8
            with dve.Fori(0, 31) as j:
                ck = Chain(dve, vth, KTH * j)
                ck(v.tensor_copy(bi, bit))
                ck(v.tensor_tensor(cand, cur, bi, ALU.bitwise_or))
                ck(v.tensor_scalar(cmpb, wp, cand.bitcast(FP32), None, ALU.is_ge))
                ck(v.tensor_reduce(cnt, cmpb, AX, ALU.add))
                v.sem_inc(cnt_ready, 1)
                dve.wait_ge(cnt_sum, j + 2)
                ck(v.tensor_tensor(keep, bank[3][:, 0:1], kp, ALU.is_ge))
                ck(v.tensor_tensor(bi, keep, bit, ALU.mult))
                ck(v.tensor_tensor(cur, cur, bi, ALU.bitwise_or))
                ck(v.tensor_scalar(bit, bit, 0.5, None, ALU.mult))
                assert ck.n == KTH
            lk(v.tensor_tensor(thr, cur.bitcast(FP32), sg, ALU.mult))
            lk(v.tensor_scalar(sel, wnode[:, :], thr, None, ALU.is_gt))
            lk(v.tensor_scalar(eqm, wnode[:, :], thr, None, ALU.is_equal))
            lk(v.tensor_reduce(cnt, sel, AX, ALU.add))
            v.sem_inc(cnt_ready, 1)
            dve.wait_ge(cnt_sum, 33)
            lk(v.tensor_scalar(need, bank[3][:, 0:1], -1.0, float(K_SEL), ALU.mult, ALU.add))
            tot = bank[4][:, 0:NB]
            lk(v.tensor_copy(cmpb, tot))
            lk(v.memset(wp, 0.0))
            lk(v.tensor_tensor_scan(rank, cmpb, wp, 0.0, ALU.add, ALU.add))
            lk(v.tensor_tensor(rank, rank, cmpb, ALU.subtract))
            lk(v.tensor_tensor(rank, rank, bank[5][:, 0:NB], ALU.add))
            lk(v.tensor_scalar(rank, rank, need, None, ALU.is_lt))
            lk(v.tensor_tensor(eqm, eqm, rank, ALU.mult))
            lk(v.tensor_tensor(sel, sel, eqm, ALU.add))
            lk(v.tensor_tensor(wnode[:, :], wnode[:, :], sel, ALU.mult))

        def threshold_pe(pe):
            te = nc.tensor
            pe.wait_ge(cnt_ready, 1)
            te.matmul(bank[3][:, 0:1], ones[:, :], wcnt[:, 0:1], start=True, stop=True).then_inc(cnt_sum, 1)
            with pe.Fori(0, 31) as j:
                pe.wait_ge(cnt_ready, j + 2)
                te.matmul(bank[3][:, 0:1], ones[:, :], wcnt[:, 0:1], start=True, stop=True).then_inc(cnt_sum, 1)
            pe.wait_ge(cnt_ready, 33)
            te.matmul(bank[4][:, 0:NB], ones[:, :], eqm, start=True, stop=True)
            te.matmul(bank[5][:, 0:NB], lower, eqm, start=True, stop=True)
            te.matmul(bank[3][:, 0:1], ones[:, :], wcnt[:, 0:1], start=True, stop=True).then_inc(cnt_sum, 1)

        go[0] = 0
        w1f = gpiece(2 * FH).rearrange("p (k n) -> p k n", k=2)
        w2f = gpiece(FC * D).rearrange("p (k n) -> p k n", k=FC)
        b1f = gpiece(FC)
        b2f = gpiece(D)
        hf = gpiece(2 * FC * D).rearrange("p (s f n) -> p s f n", s=2, f=FC)
        bl = gpiece(2 * 2 * D).rearrange("p (s t n) -> p s t n", s=2, t=2)
        yo = gpiece(2 * 2 * D).rearrange("p (s t n) -> p s t n", s=2, t=2)
        ty = gpiece(2 * D).rearrange("p (t n) -> p t n", t=2)
        assert go[0] <= 2 * CT * ROW

        def ffn_dma(sp):
            sp.dma_start(w1f, f_w1.rearrange("(k p) n -> p k n", p=P)).then_inc(f_in, 16)
            sp.dma_start(w2f, f_w2.rearrange("(k p) n -> p k n", p=P)).then_inc(f_in, 16)
            sp.dma_start(b1f, f_b1.rearrange("(k p) -> p k", p=P), allow_slow_non_contiguous=True).then_inc(f_in, 16)
            sp.dma_start(b2f, f_b2[None, :].to_broadcast([P, D])).then_inc(f_in, 16)

            def load(q, s):
                sp.dma_start(bl[:, s, :, :], base_v[ds(q, 1)].rearrange("a p t n -> p (a t) n")).then_inc(b_in[s], 16)

            def step(q, s, more=True):
                settled(sp, f_y, q + 1)
                sp.dma_start(out_v[ds(q, 1)].rearrange("a p t n -> p (a t) n"), yo[:, s, :, :]).then_inc(f_out[s], 16)
                if more:
                    load(q + 2, s)

            load(0, 0)
            load(1, 1)
            with sp.Fori(0, R2 - 1) as r:
                step(2 * r, 0)
                step(2 * r + 1, 1)
            step(NP - 3, 0)
            step(NP - 2, 1, False)
            step(NP - 1, 0, False)
            for s in (0, 1):
                sp.wait_ge(f_out[s], 16 * (R2 + 1 - s))

        def ffn_pe(pe):
            te = nc.tensor
            pe.wait_ge(f_in, 64)

            def up(q, s, first=False):
                zt = accf[:, ds(2 * ROW * q, 2 * D)].rearrange("p (k n) -> p k n", k=2)
                for j in range(FC // 2):
                    if not first:
                        pe.wait_ge(f_act, 4 * q - 3 + j)
                    for f in (2 * j, 2 * j + 1):
                        for k in (0, 1):
                            last = te.matmul(bank[j][:, (f % 2) * D:(f % 2) * D + D], w1f[:, k, f * P:f * P + P], zt[:, k, :],
                                             start=(k == 0), stop=(k == 1))
                    last.then_inc(f_up, 1)

            def down(q, s, first=False):
                pe.wait_ge(f_act, 4 * q + 4)
                if not first:
                    pe.wait_ge(f_y, q - 1)
                for t in (0, 1):
                    for f in range(FC):
                        last = te.matmul(bank[5 + s][:, t * D:t * D + D], hf[:, s, f, t * P:t * P + P], w2f[:, f, :],
                                         start=(f == 0), stop=(f == FC - 1))
                last.then_inc(f_down, 1)

            up(0, 0, True)
            up(1, 1)
            down(0, 0, True)
            up(2, 0)
            down(1, 1, True)
            with pe.Fori(1, R2) as r:
                up(2 * r + 1, 1)
                down(2 * r, 0)
                up(2 * r + 2, 0)
                down(2 * r + 1, 1)
            down(NP - 1, 0)

        def ffn_act(act):
            a = nc.scalar
            act.wait_ge(f_in, 64)

            def body(q, s, first):
                for j in range(FC // 2):
                    act.wait_ge(f_up, 4 * q + j + 1)
                    if j == 0 and not first:
                        act.wait_ge(f_down, q - 1)
                    for f in (2 * j, 2 * j + 1):
                        last = a.activation(hf[:, s, f, :], bank[j][:, (f % 2) * D:(f % 2) * D + D], ACT.Gelu_apprx_tanh,
                                            bias=b1f[:, f:f + 1])
                    last.then_inc(f_act, 1)

            body(0, 0, True)
            body(1, 1, True)
            with act.Fori(1, R2) as r:
                body(2 * r, 0, False)
                body(2 * r + 1, 1, False)
            body(NP - 1, 0, False)

        def ffn_dve(dve, lk):
            v = nc.vector
            dve.wait_ge(f_in, 64)
            KFF = 3

            def body(q, s, r, first):
                ck = Chain(dve, vff, KFF * q)
                dve.wait_ge(f_down, q + 1)
                ck(v.tensor_tensor(ty, bank[5 + s][:, :].rearrange("p (t n) -> p t n", t=2),
                                   b2f[:, None, :].to_broadcast([P, 2, D]), ALU.add))
                dve.wait_ge(b_in[s], 16 * r + 16)
                if not first:
                    dve.wait_ge(f_out[s], 16 * r)
                for t in (0, 1):
                    ck(v.scalar_tensor_tensor(yo[:, s, t, :], ty[:, t, :], wnode[:, ds(2 * q + t, 1)], bl[:, s, t, :], ALU.mult, ALU.add))
                v.sem_inc(f_y, 1)
                assert ck.n == KFF

            body(0, 0, 0, True)
            body(1, 1, 0, True)
            with dve.Fori(1, R2) as r:
                body(2 * r, 0, r, False)
                body(2 * r + 1, 1, r, False)
            body(NP - 1, 0, R2, False)

        @block.sync
        def _(sp):
            sp.dma_start(wcat[:, :, 0:D], Wg.rearrange("(c p) n -> p c n", p=P)).then_inc(ld_w, 16)
            sp.dma_start(attb[:, 0, :], att_src.rearrange("h c -> (h c)")[None, :].to_broadcast([P, D])).then_inc(ld_w, 16)
            sp.dma_start(attb[:, 1, :], att_dst.rearrange("h c -> (h c)")[None, :].to_broadcast([P, D])).then_inc(ld_w, 16)
            sp.dma_start(wraw, w_qkv.rearrange("(c p) n -> p c n", p=P)).then_inc(ld_w, 16)
            sp.dma_start(braw, b_qkv[None, :].to_broadcast([P, 3 * D])).then_inc(ld_w, 16)
            sp.dma_start(samp[0:1, 0:NST - 1].bitcast(I32),
                         dst[0:EP].rearrange("(a t s) -> a t s", a=1, s=ST_T * P)[:, 1:, 0],
                         allow_slow_non_contiguous=True).then_inc(ld_i, 16)
            def load_group(g):
                n = grp(g)
                sp.dma_start(idxI[0:n, g % 2, 0, :], src_t[g * P:g * P + n, :]).then_inc(idx_in[g % 2], 16)
                sp.dma_start(idxI[0:n, g % 2, 1, :], dst_t[g * P:g * P + n, :]).then_inc(idx_in[g % 2], 16)

            for g in range(min(2, NG)):
                load_group(g)
            for g in range(NG):
                n = grp(g)
                if g + 2 < NG:
                    sp.wait_ge(idx_f, g + 1)
                    load_group(g + 2)
                sp.wait_ge(idx_out, g + 1)
                sp.dma_start(srcE_d[:, g * P:g * P + n], idxO[:, g % 2, 0, 0:n].bitcast(I32)).then_inc(idx_stored[g % 2], 16)
                sp.dma_start(dstE_d[:, g * P:g * P + n], idxO[:, g % 2, 1, 0:n]).then_inc(idx_stored[g % 2], 16)
            for k in range(DQ):
                n = min(1024, NT - k * 1024)
                if k:
                    sp.wait_ge(d16_ready, k)
                sp.dma_start(d32[:, 0:n], dst[1:1 + EP].rearrange("(p t) -> p t", p=P)[:, k * 1024:k * 1024 + n]).then_inc(d32_in, 16)
            sp.wait_ge(d16_ready, DQ)
            sp.dma_start(dst16_d, d16).then_inc(d16_stored, 16)
            def load_x(q, s):
                sp.dma_start(xin[:, s, :, :], x_v[q]).then_inc(x_in[s], 16)

            def store(q, s, tick):
                settled(sp, row_ready, tick + 1)
                sp.dma_start(tab_v[q], xrow[:, s, :, :]).then_inc(tab_out[s], 16)
                sp.dma_start(xnT_d[q].rearrange("p (k n) -> p k n", k=2), xt[:, s, :, :]).then_inc(xt_out[s], 16)

            load_x(0, 0)
            load_x(1, 1)
            with sp.Fori(0, R2 - 1) as r:
                for u in (0, 1):
                    q = 2 * r + u
                    settled(sp, xn_ready, q + 1)
                    load_x(q + 2, u)
                    store(q, u, q)
            for q in range(NP - 3, NP):
                if q + 2 < NP:
                    settled(sp, xn_ready, q + 1)
                    load_x(q + 2, q % 2)
                store(q, q % 2, q)
            for s in (0, 1):
                sp.wait_ge(tab_out[s], 16 * (R2 + 1 - s))
                sp.wait_ge(xt_out[s], 16 * (R2 + 1 - s))
                sp.wait_ge(idx_stored[s], 32 * ((NG + 1 - s) // 2))
            sp.wait_ge(d16_stored, 16)
            barrier(sp, 1)
            def chunk_loads(c, s, tick):
                sp.dma_start(sidx[:, s, :], srcE_d[:, ds(c * CT, CT)]).then_inc(idx_ld[s], 16)
                sp.dma_start(dstE[:, s, :], dstE_d[:, ds(c * CT, CT)]).then_inc(drow_in[s], 16)
                for h in range(HG):
                    win = dst[ds(c * (CT * P), CT * P)]
                    rowap = bass.AP(tensor=win.tensor, offset=win.offset, ap=[[P, CT], [1, P + 2]])
                    sp.dma_start(drow[h * CT:(h + 1) * CT, s, :], rowap).then_inc(drow_in[s], 16)

            def chunk_bc(c):
                sp.dma_start(dbc, dst16_d.rearrange("p t -> (p t)")[ds(c * (CT * P), CT * P)][None, :].to_broadcast([P, CT * P])).then_inc(dbc_in, 16)

            def chunk_xt(c):
                sp.dma_start(xtk, xnT_d[ds(c, 1)].rearrange("a p (k n) -> p (a k) n", k=2)).then_inc(xtk_in, 16)

            chunk_loads(0, 0, 0)
            chunk_loads(1, 1, 1)
            chunk_bc(0)
            chunk_xt(0)

            def chunk_sp(c, s, more2=True, more1=True):
                if more1:
                    settled(sp, kv_acc, c + 2)
                    chunk_bc(c + 1)
                    settled(sp, chunk_done, c + 1)
                    chunk_xt(c + 1)
                if more2:
                    chunk_loads(c + 2, s, c)

            with sp.Fori(0, R2 - 1) as r:
                chunk_sp(2 * r, 0)
                chunk_sp(2 * r + 1, 1)
            chunk_sp(NCH - 3, 0)
            chunk_sp(NCH - 2, 1, more2=False)
            barrier(sp, 2)
            load_mix(sp)
            barrier(sp, 3)
            node_loads(sp)
            barrier(sp, 4)
            ffn_dma(sp)

        @block.gpsimd
        def _(pool):
            nc.gpsimd.iota(iotaI, [[1, 512]], base=0, channel_multiplier=0).then_inc(iota_done, 1)
            nc.gpsimd.iota(pcolI, [[0, 1]], base=0, channel_multiplier=1).then_inc(iota_done, 1)
            barrier(pool, 1)
            def gather(c, s, users, wait_free):
                if wait_free:
                    pool.wait_ge(chunk_done, c - 1)
                    pool.sem_inc(pace, 1)
                pool.wait_ge(idx_ld[s], 16 * users)
                pool.sem_inc(pace, 1)
                for t in range(CT):
                    nc.gpsimd.indirect_dma_start(
                        out=G[:, s, t, :], out_offset=None, in_=tab_d,
                        in_offset=bass.IndirectOffsetOnAxis(ap=sidx[:, s, t:t + 1], axis=0)).then_inc(rows_in[s], 16)

            gather(0, 0, 1, False)
            gather(1, 1, 1, False)
            with pool.Fori(1, R2) as r:
                gather(2 * r, 0, r + 1, True)
                gather(2 * r + 1, 1, r + 1, True)
            gather(NCH - 1, 0, R2 + 1, True)
            barrier(pool, 2)
            barrier(pool, 3)
            barrier(pool, 4)

        @block.vector
        def _(dve):
            v = nc.vector
            lk = Chain(dve, vch)
            dve.wait_ge(iota_done, 2)
            lk(v.tensor_copy(iota_w, iotaI))
            lk(v.tensor_copy(iota_f[:, :], iotaI[:, 0:P]))
            lk(v.tensor_copy(pcol[:, :], pcolI))
            v.memset(ones[:, :], 1.0)
            v.memset(zb[:, :], 0.0)
            lk(v.tensor_scalar(ident[:, :], iota_f[:, 0:P], pcol[:, :], None, ALU.is_equal))
            lk(v.tensor_scalar(valid_last[:, :], pcol[:, :], float(TAIL), None, ALU.is_lt))
            dve.wait_ge(ld_i, 16)
            lk(v.tensor_copy(sampF[0:1, 0:NST - 1], samp[0:1, 0:NST - 1].bitcast(I32)))
            v.sem_inc(prep_dve, 1)
            T, pos, inv, p128 = (small[:, i:i + 1] for i in range(4))
            lk(v.tensor_scalar(p128, pcol[:, :], float(P), None, ALU.mult))
            lk(v.tensor_scalar(inv, pcol[:, :], 1.0, None, ALU.is_lt))
            lk(v.tensor_scalar(pos, pcol[:, :], float(NB - 1), None, ALU.is_gt))
            lk(v.tensor_tensor(inv, inv, pos, ALU.add))
            dve.wait_ge(prep_mm, 1)
            lk(v.tensor_scalar(tmp512[:, 0:NST - 1], bank[0][:, 0:NST - 1], p128, None, ALU.is_lt))
            lk(v.tensor_reduce(T, tmp512[:, 0:NST - 1], AX, ALU.add))
            lk(v.scalar_tensor_tensor(T, inv, 1e6, T, ALU.mult, ALU.add))
            lk(v.tensor_tensor(pos, T, pcol[:, :], ALU.add))
            lk(v.tensor_scalar(tmp512[:, 0:NI], iota_w[:, 0:NI], pos, None, ALU.is_ge))
            lk(v.tensor_scalar(cmp2[:, 0:NCH + 1], iota_w[:, 0:NCH + 1], float(SC), T, ALU.mult, ALU.is_gt))
            v.sem_inc(prep_dve, 1)
            dve.wait_ge(prep_mm, 2)
            lk(v.tensor_scalar(item_base[:, :], bank[0][:, 0:NI], float(P), None, ALU.mult))
            lk(v.tensor_copy(item_block, bank[0][32:33, 0:NI]))
            lk(v.tensor_tensor(item_tile, iota_w[64:65, 0:NI], bank[0][64:65, 0:NI], ALU.subtract))
            lk(v.tensor_scalar(item_tile, item_tile, SC - 1, None, ALU.bitwise_and))
            lk(v.scalar_tensor_tensor(chunk_item, iota_w[96:97, 0:NCH + 1], float(SC), bank[1][96:97, 0:NCH + 1], ALU.mult, ALU.add))
            dve.wait_ge(ld_w, 80)
            for c in range(2):
                for a in range(2):
                    lk(v.tensor_tensor(wtmp[:, a, :], wcat[:, c, 0:D], attb[:, a, :], ALU.mult))
                lk(v.tensor_reduce(wcat[:, c, D:ROW], wtmp.rearrange("p a (h n) -> p (a h) n", h=HG), AX, ALU.add))

            def centre(dst_ap, raw):
                parts = raw.rearrange("p (h n) -> p h n", h=HM)
                for kind in (0, 1):
                    a = parts[:, :, CM * (1 + kind):CM * (2 + kind)]
                    m = wmean[:, 8 * kind:8 * kind + 8]
                    lk(v.tensor_reduce(m, a, AX, ALU.add))
                    lk(v.tensor_scalar(m, m, 1.0 / CM, None, ALU.mult))
                    lk(v.tensor_tensor(dst_ap[:, D * kind:D * (kind + 1)].rearrange("p (h n) -> p h n", h=HM), a,
                                       m[:, :, None].to_broadcast([P, HM, CM]), ALU.subtract))

            centre(kvw[:, 0, :], wraw[:, 0, :])
            centre(kvw[:, 1, :], wraw[:, 1, :])
            centre(bkv[:, :], braw)
            for g in range(NG):
                n = grp(g)
                dve.wait_ge(idx_in[g % 2], 32 * (g // 2 + 1))
                if g:
                    dve.wait_ge(idx_t, g)
                lk(v.tensor_copy(idxF[0:n, :, :], idxI[0:n, g % 2, :, :]))
                v.sem_inc(idx_f, 1)
                dve.wait_ge(idx_t, g + 1)
                if g >= 2:
                    dve.wait_ge(idx_stored[g % 2], 32 * (g // 2))
                v.tensor_copy(idxO[:, g % 2, 0, 0:n].bitcast(I32), bank[2][:, 0:n])
                lk(v.tensor_copy(idxO[:, g % 2, 1, 0:n], bank[2][:, P:P + n]))
                v.sem_inc(idx_out, 1)
            for k in range(DQ):
                n = min(1024, NT - k * 1024)
                dve.wait_ge(d32_in, 16 * (k + 1))
                lk(v.tensor_copy(d16[:, k * 1024:k * 1024 + n], d32[:, 0:n]))
                v.sem_inc(d16_ready, 1)
            KLN, KSP = 7, 7

            def ln1(q, s, r, first=False):
                ln = Chain(dve, vln, KLN * q)
                dve.wait_ge(x_in[s], 16 * r + 16)
                for t in (0, 1):
                    last = v.bn_stats(bst[:, 6 * t:6 * t + 6], xin[:, s, t, :])
                ln(last)
                v.sem_inc(pace, 1)
                for t in (0, 1):
                    last = v.bn_aggr(mv[:, t, :], bst[:, 6 * t:6 * t + 6])
                ln(last)
                ln(v.tensor_scalar(var[:, 0:2], mv[:, :, 1], EPS, None, ALU.add))
                v.sem_inc(x_var, 1)
                dve.wait_ge(x_std, q + 1)
                ln(v.reciprocal(mv[:, :, 1], var[:, 2:4]))
                if not first:
                    dve.wait_ge(xn_T, q - 1)
                for t in (0, 1):
                    ln(v.tensor_scalar(xn[:, s, t, :], xin[:, s, t, :], mv[:, t, 0:1], mv[:, t, 1:2],
                                       ALU.subtract, ALU.mult))
                ln(v.tensor_copy(stat[:, ds(2 * q, 2), :], mv))
                v.sem_inc(xn_ready, 1)
                assert ln.n == KLN

            def split(q, s):
                ln = Chain(dve, row_split, KSP * q)
                dve.wait_ge(row_ready, q + 1)
                r0, r1 = res[:, 0, :, :], res[:, 1, :, :]
                ln(v.tensor_copy(r0[:, :, 0:HG], xrow[:, s, :, D + HG:ROW]))
                ln(v.tensor_copy(r0[:, :, HG:2 * HG], xrow[:, s, :, D:D + HG]))
                for k in range(3):
                    part = nodeval[:, ds(2 * q, 2), k, :]
                    ln(v.tensor_copy(part, r0))
                    if k < 2:
                        ln(v.tensor_tensor(r0, r0, part, ALU.subtract))
                assert ln.n == KSP

            ln1(0, 0, 0, first=True)
            ln1(1, 1, 0, first=True)
            split(0, 0)
            ln1(2, 0, 1)
            split(1, 1)
            with dve.Fori(1, R2) as r:
                ln1(2 * r + 1, 1, r)
                split(2 * r, 0)
                ln1(2 * r + 2, 0, r + 1)
                split(2 * r + 1, 1)
            split(NP - 1, 0)
            barrier(dve, 1)

            GW = HG * (CT + 1)

            def ghv(i):
                return gh[:, i * GW:(i + 1) * GW]

            def ghh(i):
                return ghv(i).rearrange("p (h t) -> p h t", h=HG)

            lk(v.memset(accf, 0.0))
            lk(v.memset(gh, -BIG))
            for i in (0, 3):
                lk(v.memset(ghv(i), -3.0 * BIG))
            lk(v.memset(r8, 1.0))
            s3 = s_e.rearrange("p (h t) -> p t h", h=HG)
            dn3 = dn.rearrange("p (t k) -> p t k", k=8)
            U3 = U.rearrange("p (a t h) -> p a t h", a=3, h=HG)
            UA = U.rearrange("p (a n) -> p a n", a=3)
            W3 = We.rearrange("p (a t h) -> p a t h", a=2, h=HG)
            KCHUNK = 37
            v.sem_inc(d_read, 1)
            v.sem_inc(kv_var, 1)

            def edge_chunk(c, s, r):
                ck = Chain(dve, vck, c * KCHUNK)
                lo = dve.value_load(chunk_item[0:1, ds(c, 1)], min_val=0, max_val=NI - 1)
                hi = dve.value_load(chunk_item[0:1, ds(c + 1, 1)], min_val=1, max_val=NI)
                dve.wait_ge(dbc_in, 16 * c + 16)
                v.sem_inc(pace, 1)
                with dve.Fori(lo, hi) as i:
                    tl = dve.value_load(item_tile[0:1, ds(i, 1)], min_val=0, max_val=SC - 1)
                    for hf in (0, 1):
                        dve.wait_ge(ot_used, 2 * i + hf + 1)
                        v.tensor_scalar(oneT[:, hf * 256:hf * 256 + 256], dbc[:, ds(tl * 512 + hf * 256, 256)],
                                        item_base[:, ds(i, 1)], pcol[:, :], ALU.subtract, ALU.is_equal).then_inc(ot_ready, 1)
                dve.wait_ge(ot_used, 2 * hi + 2)
                ck(v.tensor_copy(dn, bank[0][:, 0:CT * 8]))
                v.sem_inc(d_read, 1)
                dve.wait_ge(drow_in[s], 80 * r + 80)
                ck(v.tensor_tensor(neq, drow[:, s, 0:P + 1], drow[:, s, 1:P + 2], ALU.not_equal))
                ck(v.tensor_tensor(sng, drow[:, s, 1:2], drow[:, s, P:P + 1], ALU.not_equal))
                dve.wait_ge(rows_in[s], 16 * CT * r + 16 * CT)
                ck(v.tensor_tensor(s3, G[:, s, :, D:D + HG], dn3[:, :, HG:2 * HG], ALU.max))
                v.sem_inc(s_ready, 1)
                v.tensor_scalar(pen, neq, -BIG, None, ALU.mult)
                ck(v.tensor_scalar(sng, sng, -BIG, None, ALU.mult))
                ck(v.tensor_scalar(x4[:, 2:3], pen[:, 0:1], sng, None, ALU.add))
                ck(v.tensor_scalar(x4[:, 3:4], pen[:, P:P + 1], sng, None, ALU.add))
                dve.wait_ge(kv_mm, 2 * c + 1)
                dve.wait_ge(kv_acc, c + 1)
                ck(v.tensor_tensor(kv[:, 0, :], bank[7][:, :], bkv[:, :], ALU.add))
                v.sem_inc(kv_biased, 1)
                dve.wait_ge(sT_ready, c + 1)
                v.tensor_copy(sT, bank[1][:, 0:P])
                ck(v.tensor_copy(first, bank[1][:, P:2 * P]))
                ck(v.tensor_tensor_scan(fw, pen[:, 0:P], sT, -BIG, ALU.add, ALU.max))
                ck(v.tensor_tensor_scan(bw[:, ::-1], pen[:, 1:P + 1][:, ::-1], sT[:, ::-1], -BIG, ALU.add, ALU.max))
                v.tensor_copy(x4[:, 0:1], fw[:, P - 1:P])
                ck(v.tensor_copy(x4[:, 1:2], bw[:, 0:1]))
                v.sem_inc(x4_ready, 1)
                dve.wait_ge(kv_mm, 2 * c + 2)
                ck(v.tensor_tensor(kv[:, 1, :], bank[7][:, :], bkv[:, :], ALU.add))
                v.sem_inc(kv_biased, 1)
                dve.wait_ge(r_ready, c + 1)
                pr = bank[2][0:1, :].rearrange("p (k h t) -> p k h t", k=4, h=HG)
                v.tensor_copy(ghh(0)[:, :, 1:CT + 1], pr[:, 2])
                v.tensor_copy(ghh(1)[:, :, 1:CT + 1], pr[:, 0])
                v.tensor_copy(ghh(3)[:, :, 0:CT], pr[:, 3])
                ck(v.tensor_copy(ghh(4)[:, :, 0:CT], pr[:, 1]))
                ck(v.tensor_tensor_scan(ghv(2), ghv(0), ghv(1), -BIG, ALU.add, ALU.max))
                ck(v.tensor_tensor_scan(ghv(5)[:, ::-1], ghv(3)[:, ::-1], ghv(4)[:, ::-1], -BIG, ALU.add, ALU.max))
                v.tensor_copy(cin[:, 0:P].rearrange("p (h t) -> p h t", h=HG), ghh(2)[:, :, 0:CT])
                ck(v.tensor_copy(cin[:, P:2 * P].rearrange("p (h t) -> p h t", h=HG), ghh(5)[:, :, 1:CT + 1]))
                v.sem_inc(gh_ready, 1)
                for t in (0, 1):
                    dve.wait_ge(kv_sq, 2 * c + t + 1)
                    ck(v.tensor_reduce(rs[:, t, :], sq.rearrange("p (g n) -> p g n", n=CM), AX, ALU.add))
                    v.sem_inc(kv_var, 1)
                ck(v.tensor_scalar(rs[:, :, :], rs[:, :, :], 1.0 / CM, EPS, ALU.mult, ALU.add))
                v.sem_inc(kv_var, 1)
                dve.wait_ge(c_ready, c + 1)
                ck(v.tensor_copy(c2, bank[1][:, 2 * P:2 * P + 2]))
                v.tensor_tensor_scan(fw, pen[:, 0:P], sT, c2[:, 0:1], ALU.add, ALU.max)
                ck(v.tensor_tensor_scan(bw[:, ::-1], pen[:, 1:P + 1][:, ::-1], sT[:, ::-1], c2[:, 1:2], ALU.add, ALU.max))
                ck(v.tensor_tensor(fw, fw, bw, ALU.max))
                v.sem_inc(mm_ready, 1)
                dve.wait_ge(kv_std, c + 1)
                ck(v.reciprocal(rs[:, :, :], rs[:, :, :]))
                last_pair = isinstance(c, int)
                if last_pair:
                    ck(v.tensor_scalar(rs[:, 1, :], rs[:, 1, :], valid_last[:, :], None, ALU.mult))
                for t in (0, 1):
                    last = v.tensor_tensor(kv[:, t, :].rearrange("p (g n) -> p g n", n=CM), kv[:, t, :].rearrange("p (g n) -> p g n", n=CM),
                                           rs[:, t, :][:, :, None].to_broadcast([P, 16, CM]), ALU.mult)
                ck(last)
                v.sem_inc(kv_norm, 1)
                v.tensor_tensor(U3[:, 0], G[:, s, :, D:D + HG], dn3[:, :, 0:HG], ALU.add)
                v.tensor_tensor(U3[:, 1], dn3[:, :, HG:2 * HG], dn3[:, :, 0:HG], ALU.add)
                dve.wait_ge(m_ready, c + 1)
                ck(v.tensor_tensor(U3[:, 2], bank[1][:, 272:272 + P].rearrange("p (h t) -> p t h", h=HG), dn3[:, :, 0:HG], ALU.add))
                ck(v.scalar_tensor_tensor(U, U, 0.2, U, ALU.mult, ALU.max))
                ck(v.tensor_tensor(UA[:, 0:2], UA[:, 0:2],
                                   U[:, None, 2 * P:3 * P].to_broadcast([P, 2, P]), ALU.subtract))
                ck(v.tensor_tensor(rl, ghh(1)[:, :, 0], dn3[0:1, 0, 0:HG], ALU.add))
                ck(v.scalar_tensor_tensor(rl, rl, 0.2, rl, ALU.mult, ALU.max))
                ck(v.tensor_tensor(rl, rl, U3[0:1, 2, 0, :], ALU.subtract))
                ck(v.tensor_scalar(rl, rl, 0.0, None, ALU.min))
                v.sem_inc(u_ready, 1)
                v.tensor_copy(ghh(1)[:, :, 0], ghh(2)[:, :, CT])
                ck(v.tensor_scalar(one0, iota_f[0:1, 0:P], item_base[0:1, ds(lo, 1)], dstE[0:1, s, 0:1], ALU.add, ALU.is_equal))
                v.sem_inc(one0_ready, 1)
                dve.wait_ge(w_ready, c + 1)
                gm = G[:, s, :, 0:D].rearrange("p t (h n) -> p t h n", h=HG)
                for k in range(4):
                    q8 = slice(k * 8, k * 8 + 8)
                    v.tensor_tensor(gm[:, q8], gm[:, q8], W3[:, 0, q8][:, :, :, None].to_broadcast([P, 8, HG, CG]), ALU.mult)
                v.tensor_copy(G[:, s, :, D:D + HG], W3[:, 0])
                ck(v.tensor_tensor(G[:, s, :, D + HG:ROW], W3[:, 1], first.rearrange("p (h t) -> p t h", h=HG), ALU.mult))
                dve.wait_ge(fac_ready, c + 1)
                ck(v.tensor_scalar(fac, bank[1][:, 400 + HG:400 + 2 * HG], -1.0, 1.0, ALU.mult, ALU.add))
                ck(v.tensor_tensor(fac, fac, bank[1][:, 400:400 + HG], ALU.add))
                b0 = dve.value_load(item_block[0:1, ds(lo, 1)], min_val=0, max_val=NB - 1)
                am = acc[:, ds(b0, 1), 0:D].rearrange("p a (h n) -> p (a h) n", h=HG)
                at = acc[:, ds(b0, 1), D:ROW].rearrange("p a (k h) -> p (a k) h", h=HG)
                v.tensor_tensor(am, am, fac[:, :, None].to_broadcast([P, HG, CG]), ALU.mult)
                ck(v.tensor_tensor(at, at, fac[:, None, :].to_broadcast([P, 2, HG]), ALU.mult))

                def onehots(i):
                    tl = dve.value_load(item_tile[0:1, ds(i, 1)], min_val=0, max_val=SC - 1)
                    for k in range(ST_T):
                        dve.wait_ge(oe_used, 4 * i + k + 1)
                        v.tensor_scalar(oneE[:, k, :], iota_f[:, 0:P], item_base[:, ds(i, 1)],
                                        dstE[:, s, ds(tl * ST_T + k, 1)], ALU.add, ALU.is_equal).then_inc(oe_ready, 1)

                def add(i):
                    b = dve.value_load(item_block[0:1, ds(i, 1)], min_val=0, max_val=NB - 1)
                    dve.wait_ge(oe_used, 4 * i + 8)
                    dve.wait_ge(sum_added, i + 2)
                    a = acc[:, ds(b, 1), :].rearrange("p a r -> p (a r)")
                    v.tensor_tensor(a, a, sums(i), ALU.add).then_inc(sum_added, 1)

                onehots(lo)
                with dve.Fori(lo + 1, hi) as i:
                    onehots(i)
                    add(i - 1)
                add(hi - 1)
                dve.wait_ge(sum_added, hi + 2)
                v.sem_inc(chunk_done, 1)
                assert ck.n == KCHUNK + last_pair, ck.n

            paired(dve, edge_chunk)
            barrier(dve, 2)
            mix_weights_dve(dve, lk)
            barrier(dve, 3)
            node_dve(dve)
            threshold_dve(dve, lk)
            barrier(dve, 4)
            ffn_dve(dve, lk)

        @block.scalar
        def _(act):
            a = nc.scalar

            def std1(q):
                act.wait_ge(x_var, q + 1)
                a.activation(var[:, 2:4], var[:, 0:2], ACT.Sqrt).then_inc(x_std, 1)

            def rows1(q, s, r):
                act.wait_ge(xn_T, q + 1)
                if r is not None:
                    act.wait_ge(xt_out[s], 16 * r)
                    act.wait_ge(tab_out[s], 16 * r)
                    act.wait_ge(row_split, 7 * (q - 1))
                a.copy(xt[:, s, :, :], bank[3][:, :].rearrange("p (k n) -> p k n", k=2)).then_inc(xt_ready, 1)
                for t in (0, 1):
                    act.wait_ge(xp_ready, 2 * q + t + 1)
                    last = a.copy(xrow[:, s, t, :], bank[4 + t][:, 0:ROW])
                last.then_inc(row_ready, 1)

            std1(0)
            std1(1)
            rows1(0, 0, None)
            std1(2)
            rows1(1, 1, None)
            with act.Fori(1, R2) as r:
                for u in (0, 1):
                    q = 2 * r + u
                    std1(q + 1)
                    rows1(q, u, r)
            rows1(NP - 1, 0, R2)
            barrier(act, 1)

            def edge_act(c, s, r):
                for t in (0, 1):
                    act.wait_ge(kv_biased, 2 * c + t + 1)
                    act.wait_ge(kv_var, 3 * c + t + 1)
                    a.activation(sq, kv[:, t, :], ACT.Square).then_inc(kv_sq, 1)
                act.wait_ge(kv_var, 3 * c + 4)
                a.activation(rs[:, :, :], rs[:, :, :], ACT.Sqrt).then_inc(kv_std, 1)
                act.wait_ge(u_ready, c + 1)
                a.activation(We, U[:, 0:2 * P], ACT.Exp)
                a.activation(r8[:, 0:HG], rl, ACT.Exp).then_inc(w_ready, 1)

            paired(act, edge_act)
            barrier(act, 2)
            barrier(act, 3)
            node_act(act)
            barrier(act, 4)
            ffn_act(act)

        @block.tensor
        def _(pe):
            te = nc.tensor
            pe.wait_ge(prep_dve, 1)
            te.matmul(bank[0][:, 0:NST - 1], ones[0:1, :], sampF[0:1, 0:NST - 1], start=True, stop=True).then_inc(prep_mm, 1)
            pe.wait_ge(prep_dve, 2)
            te.matmul(bank[0][:, 0:NI], ones[:, :], tmp512[:, 0:NI], start=True, stop=True)
            te.matmul(bank[1][:, 0:NCH + 1], ones[:, :], cmp2[:, 0:NCH + 1], start=True, stop=True).then_inc(prep_mm, 1)
            for g in range(NG):
                n = grp(g)
                pe.wait_ge(idx_f, g + 1)
                if g:
                    pe.wait_ge(idx_out, g)
                te.transpose(bank[2][:, 0:n], idxF[0:n, 0, :], ident[0:n, 0:n])
                te.transpose(bank[2][:, P:P + n], idxF[0:n, 1, :], ident[0:n, 0:n]).then_inc(idx_t, 1)

            def turn(q, s):
                pe.wait_ge(xn_ready, q + 1)
                for k in (0, 1):
                    for t in (0, 1):
                        last = te.transpose(bank[3][:, k * 256 + t * P:k * 256 + t * P + P], xn[:, s, t, k * P:k * P + P], ident[:, :])
                last.then_inc(xn_T, 1)

            def project(q, s):
                pe.wait_ge(xt_ready, q + 1)
                for t in (0, 1):
                    for k in (0, 1):
                        last = te.matmul(bank[4 + t][:, 0:ROW], xt[:, s, k, t * P:t * P + P], wcat[:, k, :], start=(k == 0), stop=(k == 1))
                    last.then_inc(xp_ready, 1)

            turn(0, 0)
            project(0, 0)
            turn(1, 1)
            pe.wait_ge(row_ready, 1)
            project(1, 1)
            with pe.Fori(1, R2) as r:
                for u in (0, 1):
                    q = 2 * r + u
                    turn(q, u)
                    pe.wait_ge(row_ready, q)
                    project(q, u)
            turn(NP - 1, 0)
            pe.wait_ge(row_ready, NP - 1)
            project(NP - 1, 0)
            barrier(pe, 1)

            pe.sem_inc(ot_used, 2)
            pe.sem_inc(oe_used, 4)
            pe.sem_inc(sum_added, 2)
            pe.sem_inc(kv_acc, 1)
            for kbank in (5, 6):
                last = te.matmul(bank[kbank][:, :], zb[:, 0:P], zb[:, :], start=True, stop=False, skip_group_check=True)

            def edge_pe(c, s, r):
                lo = pe.value_load(chunk_item[0:1, ds(c, 1)], min_val=0, max_val=NI - 1)
                hi = pe.value_load(chunk_item[0:1, ds(c + 1, 1)], min_val=1, max_val=NI)
                pe.wait_ge(d_read, c + 1)
                te.matmul(bank[0][:, 0:CT * 8], zb[:, 0:P], zb[:, 0:CT * 8], start=True, stop=False, skip_group_check=True)
                with pe.Fori(lo, hi) as i:
                    b = pe.value_load(item_block[0:1, ds(i, 1)], min_val=0, max_val=NB - 1)
                    tl = pe.value_load(item_tile[0:1, ds(i, 1)], min_val=0, max_val=SC - 1)
                    for k in range(ST_T):
                        if k % 2 == 0:
                            pe.wait_ge(ot_ready, 2 * i + k // 2 + 1)
                        for part in range(3):
                            last = te.matmul(bank[0][:, ds(tl * 32 + k * 8, 8)], oneT[:, k * P:k * P + P],
                                             nodeval[:, ds(b, 1), part, :].rearrange("p a k -> p (a k)"),
                                             start=False, stop=False, skip_group_check=True)
                        if k % 2:
                            last.then_inc(ot_used, 1)
                def kv_product(t):
                    for k in (0, 1):
                        last = te.matmul(bank[7][:, :], xtk[:, k, t * P:t * P + P], kvw[:, k, :], start=(k == 0), stop=(k == 1))
                    last.then_inc(kv_mm, 1)

                pe.wait_ge(xtk_in, 16 * c + 16)
                kv_product(0)
                pe.wait_ge(s_ready, c + 1)
                te.transpose(bank[1][:, 0:P], s_e, ident[:, :])
                te.transpose(bank[1][:, P:2 * P], neq[:, 0:P], ident[:, :]).then_inc(sT_ready, 1)
                pe.wait_ge(kv_biased, 2 * c + 1)
                kv_product(1)
                pe.wait_ge(x4_ready, c + 1)
                for k in range(4):
                    last = te.transpose(bank[2][0:1, k * P:k * P + P], x4[:, k:k + 1], ident[:, :])
                last.then_inc(r_ready, 1)
                pe.wait_ge(gh_ready, c + 1)
                pe.sem_inc(pace, 1)
                te.transpose(bank[1][:, 2 * P:2 * P + 1], cin[:, 0:P], ident[0:1, 0:1])
                te.transpose(bank[1][:, 2 * P + 1:2 * P + 2], cin[:, P:2 * P], ident[0:1, 0:1]).then_inc(c_ready, 1)
                pe.wait_ge(mm_ready, c + 1)
                te.transpose(bank[1][:, 272:272 + P], fw, ident[:, :]).then_inc(m_ready, 1)
                pe.wait_ge(kv_norm, c + 1)
                for t in (0, 1):
                    for h2 in (0, 1):
                        te.matmul(bank[5][:, h2 * P:h2 * P + P], kv[:, t, h2 * P:h2 * P + P], kv[:, t, D + h2 * P:D + h2 * P + P],
                                  start=False, stop=False, skip_group_check=True)
                        te.matmul(bank[5][:, 256 + h2:257 + h2], kv[:, t, h2 * P:h2 * P + P], ones[:, 0:1],
                                  start=False, stop=False, skip_group_check=True)
                    last = te.matmul(bank[6][:, 0:D], ones[:, :], kv[:, t, D:2 * D], start=False, stop=False, skip_group_check=True)
                last.then_inc(kv_acc, 1)
                pe.wait_ge(w_ready, c + 1)
                pe.wait_ge(one0_ready, c + 1)
                te.matmul(bank[1][:, 400:400 + 2 * HG], one0, r8, start=True, stop=True).then_inc(fac_ready, 1)
                with pe.Fori(lo, hi) as i:
                    tl = pe.value_load(item_tile[0:1, ds(i, 1)], min_val=0, max_val=SC - 1)
                    pe.wait_ge(sum_added, i + 1)
                    for k in range(ST_T):
                        pe.wait_ge(oe_ready, 4 * i + k + 1)
                        last = te.matmul(sums(i), oneE[:, k, :], G[:, s, ds(tl * ST_T + k, 1), :].rearrange("p a r -> p (a r)"),
                                         start=(k == 0), stop=(k == ST_T - 1))
                        last.then_inc(oe_used, 1)

            paired(pe, edge_pe)
            barrier(pe, 2)
            mix_weights_pe(pe)
            barrier(pe, 3)
            node_pe(pe)
            threshold_pe(pe)
            barrier(pe, 4)
            ffn_pe(pe)


_F32 = ["L0_gnn_W", "L0_gnn_att_src", "L0_gnn_att_dst", "L0_gnn_bias", "L0_mix_w_qkv", "L0_mix_b_qkv", "L0_mix_kln_g",
        "L0_mix_kln_b", "L0_mix_vln_g", "L0_mix_vln_b", "L0_mix_w1", "L0_mix_b1", "L0_mix_w2", "L0_mix_b2", "L0_ffn_wr",
        "L0_ffn_br", "L0_ffn_w1", "L0_ffn_b1", "L0_ffn_w2", "L0_ffn_b2"]


def kernel(**inputs):
    import concourse.bacc as bacc
    from concourse.bass_utils import run_bass_kernel_spmd

    nc = bacc.Bacc("TRN2", target_bir_lowering=False, num_devices=1)
    x = np.asarray(inputs["x"])
    src, dst = np.asarray(inputs["src"]), np.asarray(inputs["dst"])
    n, e = x.shape[0], src.shape[0]
    npad = -(-n // P) * P
    ep = -(-e // (P * CT)) * (P * CT)
    arrays = {"x_in": np.zeros((npad, x.shape[1]), x.dtype), "src_in": np.zeros((ep,), src.dtype),
              "dst_in": np.full((ep + 2,), npad - 1, dst.dtype)}
    arrays["x_in"][:n] = x
    arrays["src_in"][:e] = src
    arrays["dst_in"][1:1 + e] = dst
    arrays["dst_in"][0] = -1
    for name in _F32:
        arrays[name] = np.ascontiguousarray(inputs[name])
    args = [nc.dram_tensor(k, a.shape, mybir.dt.from_np(a.dtype), kind="ExternalInput").ap() for k, a in arrays.items()]
    out = nc.dram_tensor("out", (npad, x.shape[1]), FP32, kind="ExternalOutput").ap()
    gps_kernel(nc, n, e, *args, out)
    r = run_bass_kernel_spmd(nc, [arrays], core_ids=[0])
    return r.results[0]["out"][:n]
```

```python
import numpy as np
import concourse.bass as bass
from concourse import mybir
from contextlib import ExitStack

FP32 = mybir.dt.float32
BF16 = mybir.dt.bfloat16
I32 = mybir.dt.int32
I16 = mybir.dt.int16
ALU = mybir.AluOpType
ACT = mybir.ActivationFunctionType
AX = mybir.AxisListType.X
P = 128
CT = 32
ST_T = 4
ACT_ST = 3
BIG = 1e38


def ds(start, size):
    return bass.ds(start, size)


class Chain:

    def __init__(self, eng, sem, base=0):
        self.eng, self.sem, self.base, self.n = eng, sem, base, 0

    def __call__(self, ins):
        ins.then_inc(self.sem, 1)
        self.n += 1
        self.eng.wait_ge(self.sem, self.base + self.n)


def gps_kernel(nc, n_nodes, n_edges, x, src, dst, Wg, att_src, att_dst, g_bias, w_qkv, b_qkv, kln_g, kln_b,
               vln_g, vln_b, m_w1, m_b1, m_w2, m_b2, f_wr, f_br, f_w1, f_b1, f_w2, f_b2, out):
    D, HG, HM = 256, 4, 8
    CG, CM = D // HG, D // HM
    FH = 4 * D
    FC = FH // P
    NPAD = x.shape[0]
    NB = NPAD // P
    NP = NB // 2
    EP = src.shape[0]
    NT = EP // P
    NST = NT // ST_T
    SC = CT // ST_T
    NCH = NT // CT
    ROW = D + 2 * HG
    K_SEL = max(1, int(0.5 * n_nodes)) - 1
    EPS = 1e-5
    TAIL = n_nodes - (NB - 1) * P
    assert NB == 2 * NP and NP == NCH and NP % 2 == 1 and NST < 512 and n_edges <= EP

    ctx = ExitStack()
    with ctx:
        def sb(name, shape, dt=FP32):
            return ctx.enter_context(nc.sbuf_tensor(name, shape, dt))

        def sem(name):
            return ctx.enter_context(nc.semaphore(name))

        tab_d = nc.dram_tensor("tab_d", [NPAD, ROW], FP32).ap()
        xnT_d = nc.dram_tensor("xnT_d", [NP, P, 2 * 2 * P], FP32).ap()
        srcE_d = nc.dram_tensor("srcE_d", [P, NT], I32).ap()
        dstE_d = nc.dram_tensor("dstE_d", [P, NT], FP32).ap()
        dst16_d = nc.dram_tensor("dst16_d", [P, NT], I16).ap()
        base_d = nc.dram_tensor("base_d", [NPAD, D], FP32).ap()

        one = ctx.enter_context(nc.psum_tensor("values", [P, 2, 512], FP32))
        bank = [ctx.enter_context(nc.psum_tensor(f"bank{i}", [P, 512], FP32)) for i in range(1, 7)]
        bank = [one[:, 0, :], bank[0], one[:, 1, :]] + bank[1:]
        onef = one[:, :, :].rearrange("p a n -> p (a n)")

        accf = sb("acc", [P, max(NB * ROW, 6400)])[:, :]
        acc = accf[:, 0:NB * ROW].rearrange("p (b r) -> p b r", r=ROW)
        iota_f = sb("iota_f", [P, P])
        pcol = sb("pcol", [P, 1])
        ident = sb("ident", [P, P])
        ones = sb("ones", [P, P])
        stat = sb("stat", [P, NB, 2])
        wnode = sb("wnode", [P, NB])
        kvw = sb("kvw", [P, 2, 2 * D])
        bkv = sb("bkv", [P, 2 * D])
        valid_last = sb("valid_last", [P, 1])
        first_base = sb("first_base", [P, NST + 1])
        block_base = sb("block_base", [P, NB])
        nodeval = sb("nodeval", [P, NB, 3, 2 * HG], BF16)

        G = sb("G", [P, 2, CT, ROW])
        sidx = sb("sidx", [P, 2, CT], I32)
        dstE = sb("dstE", [P, 2, CT])
        drow = sb("drow", [P, 2, P + 2], I32)
        shared = sb("shared", [P, CT * P // 2])
        dbc = shared[:, :].bitcast(I16)
        kv = shared[:, 0:4 * D].rearrange("p (a n) -> p a n", a=2)
        sq = shared[:, 4 * D:6 * D]
        xtk = shared[:, 6 * D:8 * D].rearrange("p (k n) -> p k n", k=2)
        oneT2 = sb("oneT2", [P, 2, ST_T * P], BF16)
        zb = sb("zb", [P, P], BF16)
        oneE = sb("oneE", [P, 2, ST_T, P])
        NV = 3 * 2 * HG
        nv = sb("nv", [P, SC, NV], BF16)
        cb = sb("cb", [P, SC])
        dl = sb("dl", [P, 2, SC, ST_T])
        work = sb("work", [P, 2236])
        o = [0]

        def piece(n, p=P):
            a = work[0:p, o[0]:o[0] + n]
            o[0] += n
            return a

        dn = piece(CT * 8)
        U = piece(3 * P)
        s_e, sT, bw = (U[:, k * P:(k + 1) * P] for k in range(3))
        pn = piece(2 * (P + 1))
        We = pn[:, 0:2 * P]
        oneT = [oneT2[:, 0, :], oneT2[:, 1, :], U[:, 0:2 * P].bitcast(BF16), We.bitcast(BF16)]
        pen, neq = pn[:, 0:P + 1], pn[:, P + 1:]
        sng = piece(1)
        x4 = piece(4)
        first = piece(P)
        fw = piece(P)
        c2 = piece(2)
        fac = piece(HG)
        g0 = o[0]
        gh = piece(6 * HG * (CT + 1), 1)
        first_block = work[32:33, g0:g0 + NST + 1].bitcast(I32)
        extra_tile = work[64:65, g0:g0 + NB - 1].bitcast(I32)
        extra_at = work[96:97, g0:g0 + NB - 1].bitcast(I32)
        cin = piece(2 * P, 1)
        rl = piece(HG, 1)
        r8 = piece(2 * HG, 1)
        one0 = cin[:, 0:P]
        rs = sb("rs", [P, 2, 16])

        Gf = G[:, :, :, :].rearrange("p a t r -> p (a t r)")
        go = [0]

        def gpiece(n):
            a = Gf[:, go[0]:go[0] + n]
            go[0] += n
            return a

        bar = sem("bar")
        phase = [0]
        d32_in = sem("d32_in")
        ld_w, ld_i, iota_done = sem("ld_w"), sem("ld_i"), sem("iota_done")
        prep_mm, prep_dve, vch = sem("prep_mm"), sem("prep_dve"), sem("vch")
        idx_in = [sem("idx_in0"), sem("idx_in1")]
        idx_f, idx_t, idx_out = sem("idx_f"), sem("idx_t"), sem("idx_out")
        idx_stored = [sem("idx_stored0"), sem("idx_stored1")]
        d16_ready, d16_stored = sem("d16_ready"), sem("d16_stored")
        x_in = [sem("x_in0"), sem("x_in1")]
        x_var, x_std, xn_ready, xn_T, xt_ready, xp_ready, row_ready = (
            sem("x_var"), sem("x_std"), sem("xn_ready"), sem("xn_T"), sem("xt_ready"), sem("xp_ready"), sem("row_ready"))
        row_split, vln = sem("row_split"), sem("vln")
        tab_out = [sem("tab_out0"), sem("tab_out1")]
        xt_out = [sem("xt_out0"), sem("xt_out1")]
        idx_ld = [sem("idx_ld0"), sem("idx_ld1")]
        rows_in = [sem("rows_in0"), sem("rows_in1")]
        drow_in = [sem("drow_in0"), sem("drow_in1")]
        dste_in = [sem("dste_in0"), sem("dste_in1")]
        nv_ready, xo_ready, xo_used = sem("nv_ready"), sem("xo_ready"), sem("xo_used")
        g_ready, a_scaled, vfac = sem("g_ready"), sem("a_scaled"), sem("vfac")
        xe_ready, xe_done, vx, dste_used = sem("xe_ready"), sem("xe_done"), sem("vx"), sem("dste_used")
        dbc_in, xtk_in = sem("dbc_in"), sem("xtk_in")
        ot_ready, ot_used, d_read, s_ready, sT_ready = (
            sem("ot_ready"), sem("ot_used"), sem("d_read"), sem("s_ready"), sem("sT_ready"))
        x4_ready, r_ready, gh_ready, c_ready, mm_ready, m_ready = (
            sem("x4_ready"), sem("r_ready"), sem("gh_ready"), sem("c_ready"), sem("mm_ready"), sem("m_ready"))
        u_ready, w_ready, one0_ready, fac_ready = sem("u_ready"), sem("w_ready"), sem("one0_ready"), sem("fac_ready")
        oe_ready, oe_used, sum_added = sem("oe_ready"), sem("oe_used"), sem("sum_added")
        vck = sem("vck")
        kv_mm, kv_biased, kv_sq, kv_var, kv_std, kv_norm, kv_acc = (
            sem("kv_mm"), sem("kv_biased"), sem("kv_sq"), sem("kv_var"), sem("kv_std"), sem("kv_norm"), sem("kv_acc"))
        pace = sem("pace")
        mw_in, mw_pe, mw_dve = sem("mw_in"), sem("mw_pe"), sem("mw_dve")
        n_in = [sem("n_in0"), sem("n_in1")]
        h_mm, h_act, o_mm, e_out, rec_ready, u_scaled, t_ready, sc_ready, x_scaled, x_read = (
            sem("h_mm"), sem("h_act"), sem("o_mm"), sem("e_out"), sem("rec_ready"), sem("u_scaled"), sem("t_ready"),
            sem("sc_ready"), sem("x_scaled"), sem("x_read"))
        x_ready = sem("x_ready")
        v_var, v_std = sem("v_var"), sem("v_std")
        z_ready, zT_ready, zT_stored, b_ready, vna, vnp, vns, vpl = (
            sem("z_ready"), sem("zT_ready"), sem("zT_stored"), sem("b_ready"), sem("vna"), sem("vnp"), sem("vns"), sem("vpl"))
        b_out = [sem("b_out0"), sem("b_out1")]
        vth, cnt_ready, cnt_sum = sem("vth"), sem("cnt_ready"), sem("cnt_sum")
        f_in = sem("f_in")
        b_in = [sem("b_in0"), sem("b_in1")]
        f_up, f_act, f_down, f_y, f_out, vff = (
            sem("f_up"), sem("f_act"), sem("f_down"), sem("f_y"), [sem("f_out0"), sem("f_out1")], sem("vff"))

        block = ctx.enter_context(nc.Block())

        def settled(eng, semaphore, value):
            eng.wait_ge(semaphore, value)
            eng.sem_inc(pace, 1)

        def barrier(eng, n):
            eng.drain().then_inc(bar, 1)
            eng.wait_ge(bar, 5 * n)

        go[0] = 0
        wcat = gpiece(2 * ROW).rearrange("p (c n) -> p c n", c=2)
        attb = gpiece(2 * D).rearrange("p (a n) -> p a n", a=2)
        wtmp = gpiece(2 * D).rearrange("p (a n) -> p a n", a=2)
        wraw = gpiece(2 * 3 * D).rearrange("p (c n) -> p c n", c=2)
        braw = gpiece(3 * D)
        wmean = gpiece(48)
        iotaI = gpiece(512).bitcast(I32)
        pcolI = gpiece(1).bitcast(I32)
        iota_w = gpiece(512)
        samp = gpiece(NST)
        sampF = gpiece(NST)
        tmp512 = gpiece(512)
        small = gpiece(16)
        diagT = gpiece(P)
        go[0] += go[0] % 2
        idxI = gpiece(2 * 2 * P).bitcast(I32).rearrange("p (a k n) -> p a k n", a=2, k=2)
        idxF = gpiece(2 * P).rearrange("p (k n) -> p k n", k=2)
        idxO = gpiece(2 * 2 * P).rearrange("p (a k n) -> p a k n", a=2, k=2)
        ao = [0]

        def apiece(n):
            a = accf[:, ao[0]:ao[0] + n]
            ao[0] += n
            return a

        d32 = gpiece(1024).bitcast(I32)
        d16 = dbc[:, 0:NT]
        xin = apiece(2 * 2 * D).rearrange("p (a t n) -> p a t n", a=2, t=2)
        xn = apiece(2 * 2 * D).rearrange("p (a t n) -> p a t n", a=2, t=2)
        xt = apiece(2 * 4 * P).rearrange("p (a k n) -> p a k n", a=2, k=2)
        xrow = apiece(2 * 2 * ROW).rearrange("p (a t n) -> p a t n", a=2, t=2)
        bst = apiece(16)
        var = apiece(4)
        mv = apiece(4).rearrange("p (t k) -> p t k", t=2)
        res = apiece(2 * 2 * 8).rearrange("p (a t n) -> p a t n", a=2, t=2)
        DQ = (NT + 1023) // 1024

        x_v = x.rearrange("(q t p) n -> q p t n", t=2, p=P)
        tab_v = tab_d.rearrange("(q t p) n -> q p t n", t=2, p=P)
        base_v = base_d.rearrange("(q t p) n -> q p t n", t=2, p=P)
        out_v = out.rearrange("(q t p) n -> q p t n", t=2, p=P)
        src_t = src.rearrange("(t e) -> t e", e=P)
        dst_t = dst[1:1 + EP].rearrange("(t e) -> t e", e=P)
        NG = (NT + P - 1) // P

        def grp(g):
            return min(P, NT - g * P)

        R2 = (NP - 1) // 2

        def paired(eng, body):
            with eng.Fori(0, R2) as r:
                body(2 * r, 0, r)
                body(2 * r + 1, 1, r)
            body(NP - 1, 0, R2)

        go[0] = 0
        wq = gpiece(2 * D).rearrange("p (c n) -> p c n", c=2)
        wqT = gpiece(2 * D).rearrange("p (c n) -> p c n", c=2)
        kvd = gpiece(2 * P).rearrange("p (c n) -> p c n", c=2)
        m1T = gpiece(2 * D).rearrange("p (c n) -> p c n", c=2)
        w1m = gpiece(2 * D).rearrange("p (c n) -> p c n", c=2)
        wm = gpiece(2 * D).rearrange("p (c n) -> p c n", c=2)
        w2m = gpiece(2 * D).rearrange("p (c n) -> p c n", c=2)
        b1m = gpiece(2)
        bm = gpiece(2)
        bq = gpiece(2)
        kqb = gpiece(2)
        kcol = gpiece(2)
        vrow = gpiece(2 * CM).rearrange("p (k n) -> p k n", k=2)
        svk = gpiece(4)
        mt1 = gpiece(P)
        mt2 = gpiece(P)
        gbr = gpiece(D)
        b2r = gpiece(D)
        wrr = gpiece(D)
        brc = gpiece(1)
        go[0] += go[0] % 2

        def two_slots():
            return gpiece(2 * 2 * D).rearrange("p (s t n) -> p s t n", s=2, t=2)

        xl, xpl, t1, t2, t3, uu, x2, zz, bb = (two_slots() for _ in range(9))
        xtl = gpiece(2 * 2 * D).rearrange("p (s k n) -> p s k n", s=2, k=2)
        hT = gpiece(2 * D).rearrange("p (k n) -> p k n", k=2)
        junk = gpiece(D)
        var2 = gpiece(4)
        bst2 = gpiece(12)
        mv2 = gpiece(4).rearrange("p (t k) -> p t k", t=2)
        sc1 = gpiece(8).rearrange("p (s t k) -> p s t k", s=2, t=2)
        dsum, flg, wsp = (gpiece(2 * HG).rearrange("p (t h) -> p t h", t=2) for _ in range(3))
        rec, wrc = (gpiece(4 * HG).rearrange("p (s t h) -> p s t h", s=2, t=2) for _ in range(2))
        assert go[0] <= 2 * CT * ROW

        def load_mix(sp):
            wv = w_qkv.rearrange("(c p) (h n) -> p c h n", p=P, h=HM)
            for c in (0, 1):
                sp.dma_start(wq[:, c, :].rearrange("p (h n) -> p h n", h=HM), wv[:, c, :, 0:CM]).then_inc(mw_in, 16)
            sp.dma_start(w1m, m_w1.rearrange("(c p) n -> p c n", p=P)).then_inc(mw_in, 16)
            sp.dma_start(w2m, m_w2.rearrange("(c p) n -> p c n", p=P)).then_inc(mw_in, 16)
            bqv = b_qkv.rearrange("(c h n) -> c h n", c=2, n=3 * CM)[:, :, 0:CM]
            for c in (0, 1):
                sp.dma_start(b1m[:, c:c + 1], m_b1[c * P:(c + 1) * P][:, None]).then_inc(mw_in, 16)
                for h in range(P // CM):
                    sp.dma_start(bq[h * CM:(h + 1) * CM, c:c + 1], bqv[c, h][:, None]).then_inc(mw_in, 16)
            for k, a in ((0, kln_g), (1, kln_b)):
                for h in range(P // CM):
                    sp.dma_start(kcol[h * CM:(h + 1) * CM, k:k + 1], a[:, None]).then_inc(mw_in, 16)
            for k, a in ((0, vln_g), (1, vln_b)):
                sp.dma_start(vrow[:, k, :], a[None, :].to_broadcast([P, CM])).then_inc(mw_in, 16)
            sp.dma_start(gbr, g_bias[None, :].to_broadcast([P, D])).then_inc(mw_in, 16)
            sp.dma_start(b2r, m_b2[None, :].to_broadcast([P, D])).then_inc(mw_in, 16)
            sp.dma_start(wrr, f_wr.rearrange("d o -> o d").to_broadcast([P, D])).then_inc(mw_in, 16)
            sp.dma_start(brc, f_br[None, :].to_broadcast([P, 1])).then_inc(mw_in, 16)

        MW = 16 * (4 + 2 * (1 + P // CM) + 2 * (P // CM) + 2 + 4)

        def mix_weights_dve(dve, lk):
            v = nc.vector
            dve.wait_ge(mw_in, MW)
            lk(v.tensor_scalar(b2r, b2r, -1.0, None, ALU.add))
            lk(v.memset(kvd, 0.0))
            v.sem_inc(mw_dve, 1)
            gain = vrow[:, None, 0, :].to_broadcast([P, P // CM, CM])
            bias = vrow[:, None, 1, :].to_broadcast([P, P // CM, CM])

            def hv(a):
                return a.rearrange("p (h n) -> p h n", n=CM)

            for c in (0, 1):
                lk(v.tensor_scalar(mt1, bank[5][:, c * P:c * P + P], kcol[:, 0:1], None, ALU.mult))
                lk(v.tensor_tensor(hv(mt1), hv(mt1), gain, ALU.mult))
                lk(v.tensor_scalar(mt2, bank[6][:, c * P:c * P + P], kcol[:, 1:2], None, ALU.mult))
                lk(v.tensor_tensor(hv(mt2), hv(mt2), gain, ALU.mult))
                lk(v.tensor_tensor(mt1, mt1, mt2, ALU.add))
                lk(v.tensor_scalar(svk[:, 0:1], bank[5][:, 256 + c:257 + c], kcol[:, 0:1], None, ALU.mult))
                lk(v.scalar_tensor_tensor(svk[:, 0:1], kcol[:, 1:2], float(n_nodes), svk[:, 0:1], ALU.mult, ALU.add))
                lk(v.tensor_scalar(hv(mt2), bias, svk[:, 0:1], None, ALU.mult))
                lk(v.tensor_tensor(mt1, mt1, mt2, ALU.add))
                for h in range(P // CM):
                    r = slice(h * CM, (h + 1) * CM)
                    lk(v.tensor_scalar(kvd[r, c, r], mt1[r, r], 1.0 / n_nodes, None, ALU.mult))
            v.sem_inc(mw_dve, 1)
            dve.wait_ge(mw_pe, 1)
            for c in (0, 1):
                lk(v.tensor_copy(wqT[:, c, :], bank[c][:, 0:D]))
            v.sem_inc(mw_dve, 1)
            dve.wait_ge(mw_pe, 2)
            for c in (0, 1):
                lk(v.tensor_copy(m1T[:, c, :], bank[3 + c][:, 0:D]))
                lk(v.tensor_tensor(m1T[:, c, c * P:c * P + P], m1T[:, c, c * P:c * P + P], ident[:, :], ALU.add))
                lk(v.tensor_copy(kqb[:, c:c + 1], bank[2][:, c:c + 1]))
            v.sem_inc(mw_dve, 1)
            dve.wait_ge(mw_pe, 3)
            for c in (0, 1):
                lk(v.tensor_copy(wm[:, c, :], bank[c][:, 0:D]))
                lk(v.tensor_tensor(bm[:, c:c + 1], bank[2][:, 4 + c:5 + c], b1m[:, c:c + 1], ALU.add))

        def mix_weights_pe(pe):
            te = nc.tensor
            pe.wait_ge(mw_dve, 1)
            for c in (0, 1):
                for k in (0, 1):
                    last = te.transpose(bank[c][:, k * P:k * P + P], wq[:, k, c * P:c * P + P], ident[:, :])
            last.then_inc(mw_pe, 1)
            pe.wait_ge(mw_dve, 3)
            for c in (0, 1):
                te.matmul(bank[3 + c][:, 0:D], kvd[:, c, :], wqT[:, c, :], start=True, stop=True)
                last = te.matmul(bank[2][:, c:c + 1], kvd[:, c, :], bq[:, c:c + 1], start=True, stop=True)
            last.then_inc(mw_pe, 1)
            pe.wait_ge(mw_dve, 4)
            for c in (0, 1):
                for k in (0, 1):
                    te.matmul(bank[c][:, 0:D], m1T[:, k, c * P:c * P + P], w1m[:, k, :], start=(k == 0), stop=(k == 1))
            for c in (0, 1):
                for k in (0, 1):
                    last = te.matmul(bank[2][:, 4 + c:5 + c], w1m[:, k, c * P:c * P + P], kqb[:, k:k + 1], start=(k == 0), stop=(k == 1))
            last.then_inc(mw_pe, 1)

        def node_loads(sp):
            def load(q, s):
                sp.dma_start(xl[:, s, :, :], x_v[ds(q, 1)].rearrange("a p t n -> p (a t) n")).then_inc(n_in[s], 16)
                sp.dma_start(xpl[:, s, :, :], tab_v[ds(q, 1)].rearrange("a p t n -> p (a t) n")[:, :, 0:D]).then_inc(n_in[s], 16)
                sp.dma_start(xtl[:, s, :, :], xnT_d[ds(q, 1)].rearrange("a p (k n) -> p (a k) n", k=2)).then_inc(n_in[s], 16)

            def store(q, s):
                settled(sp, b_ready, q + 3)
                sp.dma_start(base_v[ds(q, 1)].rearrange("a p t n -> p (a t) n"), bb[:, s, :, :]).then_inc(b_out[s], 16)

            def step(q, s):
                settled(sp, h_mm, q + 1)
                settled(sp, t_ready, q + 1)
                settled(sp, x_scaled, q + 1)
                load(q + 2, s)
                store(q, s)

            load(0, 0)
            load(1, 1)
            with sp.Fori(0, R2 - 1) as r:
                step(2 * r, 0)
                step(2 * r + 1, 1)
            step(NP - 3, 0)
            store(NP - 2, 1)
            store(NP - 1, 0)
            for s in (0, 1):
                sp.wait_ge(b_out[s], 16 * (R2 + 2 - s))

        def node_steps(eng, step):
            with eng.Fori(0, R2 - 1) as r:
                step(2 * r, 0, r, True)
                step(2 * r + 1, 1, r, True)
            step(NP - 3, 0, R2 - 1, True)
            step(NP - 2, 1, R2 - 1, True, False)
            step(NP - 1, 0, R2, False, False)

        def heads(a):
            return a.rearrange("p t (h n) -> p t h n", h=HG)

        def wide(a):
            return a[:, :, :, None].to_broadcast([P, 2, HG, CG])

        def node_dve(dve):
            v = nc.vector
            KNA, KNB = 7, 9

            def weights_of(q, s, r):
                ck = Chain(dve, vna, KNA * q)
                aq = acc[:, ds(2 * q, 2), D:ROW]
                ck(v.tensor_tensor(dsum, aq[:, :, 0:HG], aq[:, :, HG:2 * HG], ALU.add))
                ck(v.tensor_scalar(flg, dsum, 0.5, None, ALU.is_lt))
                v.tensor_tensor(wsp, aq[:, :, HG:2 * HG], flg, ALU.add)
                ck(v.tensor_tensor(dsum, dsum, flg, ALU.add))
                v.tensor_copy(sc1[:, s], stat[:, ds(2 * q, 2), :]).then_inc(sc_ready, 1)
                ck(v.reciprocal(rec[:, s], dsum))
                v.sem_inc(rec_ready, 1)
                ck(v.tensor_tensor(wrc[:, s], wsp, rec[:, s], ALU.mult))
                return ck

            def attention_of(q, s, r, ck):
                dve.wait_ge(n_in[s], 48 * r + 48)
                ck(v.tensor_tensor(heads(t1[:, s]), heads(xpl[:, s]), wide(wrc[:, s]), ALU.mult))
                dve.wait_ge(u_scaled, q + 1)
                ck(v.tensor_tensor(t1[:, s], t1[:, s], uu[:, s], ALU.add))
                v.sem_inc(t_ready, 1)
                assert ck.n == KNA, ck.n

            def step(q, s, r, more, more2=True):
                if more:
                    nxt = (q + 1, 1 - s, r + s)
                    na = weights_of(*nxt)
                ck = Chain(dve, vnp, KNB * q)
                dve.wait_ge(e_out, q + 1)
                dve.wait_ge(o_mm, q + 1)
                dve.wait_ge(b_ready, q + 1)
                ck(v.scalar_tensor_tensor(x2[:, s], t2[:, s], 1.0, bank[3 + s][:, :].rearrange("p (t n) -> p t n", t=2), ALU.min, ALU.add))
                ck(v.scalar_tensor_tensor(x2[:, s], t1[:, s], 0.0, x2[:, s], ALU.max, ALU.add))
                dve.wait_ge(x_ready, q + 1)
                ck(v.tensor_tensor(x2[:, s], x2[:, s], t3[:, s], ALU.add))
                v.sem_inc(x_read, 1)
                for t in (0, 1):
                    last = v.bn_stats(bst2[:, 6 * t:6 * t + 6], x2[:, s, t, :])
                ck(last)
                v.sem_inc(pace, 1)
                for t in (0, 1):
                    last = v.bn_aggr(mv2[:, t, :], bst2[:, 6 * t:6 * t + 6])
                ck(last)
                v.tensor_scalar(var2[:, 0:2], mv2[:, :, 1], EPS, None, ALU.add).then_inc(v_var, 1)
                if more:
                    attention_of(*nxt, na)
                dve.wait_ge(v_std, q + 1)
                ck(v.reciprocal(mv2[:, :, 1], var2[:, 2:4]))
                dve.wait_ge(zT_ready, q + 1)
                for t in (0, 1):
                    last = v.tensor_scalar(zz[:, s, t, :], x2[:, s, t, :], mv2[:, t, 0:1], mv2[:, t, 1:2], ALU.subtract, ALU.mult)
                ck(last)
                v.sem_inc(z_ready, 1)
                for t in (0, 1):
                    ck(v.scalar_tensor_tensor(junk, zz[:, s, t, :], 1.0, wrr, ALU.mult, ALU.mult, accum_out=wnode[:, ds(2 * q + t, 1)]))
                assert ck.n == KNB, ck.n

            lk = Chain(dve, vns)
            lk(v.scalar_tensor_tensor(stat[:, :, 0], stat[:, :, 0], -1.0, stat[:, :, 1], ALU.mult, ALU.mult))
            lk(v.tensor_scalar(stat[:, :, 1], stat[:, :, 1], 1.0, None, ALU.add))
            attention_of(0, 0, 0, weights_of(0, 0, 0))
            node_steps(dve, step)

        def node_pool(pool):
            g = nc.gpsimd
            pool.sem_inc(b_ready, 2)

            def scale_sums(q, s):
                pool.wait_ge(rec_ready, q + 1)
                g.tensor_tensor(heads(uu[:, s]), heads(acc[:, ds(2 * q, 2), 0:D]), wide(rec[:, s]), ALU.mult).then_inc(vpl, 1)
                pool.wait_ge(vpl, q + 1)
                g.tensor_tensor(uu[:, s], uu[:, s], gbr[:, None, :].to_broadcast([P, 2, D]), ALU.add).then_inc(u_scaled, 1)

            def add_b2(q, s):
                pool.wait_ge(x_scaled, q + 1)
                g.tensor_tensor(t3[:, s], t3[:, s], b2r[:, None, :].to_broadcast([P, 2, D]), ALU.add).then_inc(x_ready, 1)

            def step(q, s, r, more, more2=True):
                if more:
                    scale_sums(q + 1, 1 - s)
                    add_b2(q + 1, 1 - s)
                pool.wait_ge(z_ready, q + 1)
                pool.wait_ge(b_out[s], 16 * r + 16)
                g.tensor_tensor(bb[:, s], x2[:, s], zz[:, s], ALU.add).then_inc(b_ready, 1)

            scale_sums(0, 0)
            add_b2(0, 0)
            node_steps(pool, step)

        def node_act(act):
            a = nc.scalar
            act.sem_inc(b_out[0], 16)
            act.sem_inc(b_out[1], 16)

            def scale_x(q, s, r):
                act.wait_ge(n_in[s], 48 * r + 48)
                act.wait_ge(sc_ready, q + 1)
                act.wait_ge(x_read, q + 1)
                for t in (0, 1):
                    last = a.activation(t3[:, s, t, :], xl[:, s, t, :], ACT.Identity, bias=sc1[:, s, t, 0:1], scale=sc1[:, s, t, 1:2])
                last.then_inc(x_scaled, 1)

            def hidden(q):
                act.wait_ge(h_mm, q + 1)
                for k in (0, 1):
                    last = a.activation(hT[:, k, :], bank[0][:, k * D:k * D + D], ACT.Gelu, bias=bm[:, k:k + 1])
                last.then_inc(h_act, 1)

            def step(q, s, r, more, more2=True):
                if more:
                    hidden(q + 1)
                act.wait_ge(v_var, q + 1)
                a.activation(var2[:, 2:4], var2[:, 0:2], ACT.Sqrt).then_inc(v_std, 1)
                if more:
                    scale_x(q + 1, 1 - s, r + s)
                    exponent(q + 1, 1 - s)
                act.wait_ge(zT_ready, q + 3)
                a.copy(accf[:, ds(2 * ROW * q, 2 * D)], bank[2][:, :]).then_inc(zT_stored, 1)

            def exponent(q, s):
                act.wait_ge(t_ready, q + 1)
                a.activation(t2[:, s], t1[:, s], ACT.Exp).then_inc(e_out, 1)

            scale_x(0, 0, 0)
            hidden(0)
            exponent(0, 0)
            node_steps(act, step)

        def node_pe(pe):
            te = nc.tensor
            pe.sem_inc(zT_ready, 2)
            pe.sem_inc(zT_stored, 1)
            pe.sem_inc(x_read, 2)

            def up(q, s, r):
                pe.wait_ge(n_in[s], 48 * r + 48)
                for f in (0, 1):
                    for k in (0, 1):
                        last = te.matmul(bank[0][:, f * D:f * D + D], wm[:, k, f * P:f * P + P], xtl[:, s, k, :], start=(k == 0), stop=(k == 1))
                last.then_inc(h_mm, 1)

            def down(q, s):
                pe.wait_ge(x_read, q + 1)
                pe.wait_ge(h_act, q + 1)
                for t in (0, 1):
                    for k in (0, 1):
                        last = te.matmul(bank[3 + s][:, t * D:t * D + D], hT[:, k, t * P:t * P + P], w2m[:, k, :], start=(k == 0), stop=(k == 1))
                last.then_inc(o_mm, 1)

            def step(q, s, r, more, more2=True):
                if more:
                    down(q + 1, 1 - s)
                    if more2:
                        up(q + 2, s, r + 1)
                pe.wait_ge(z_ready, q + 1)
                pe.wait_ge(zT_stored, q + 1)
                for k in (0, 1):
                    for t in (0, 1):
                        last = te.transpose(bank[2][:, k * D + t * P:k * D + t * P + P], zz[:, s, t, k * P:k * P + P], ident[:, :])
                last.then_inc(zT_ready, 1)

            up(0, 0, 0)
            down(0, 0)
            up(1, 1, 0)
            node_steps(pe, step)

        o[0] = 0
        wp, cmpb, rank, sel, eqm = (piece(NB) for _ in range(5))
        wcnt = piece(8)
        lower = piece(P)
        bits = piece(4)
        bits_i = piece(4).bitcast(I32)

        def threshold_dve(dve, lk):
            v = nc.vector
            cnt, c0, sg, kp, pen_l, need = (wcnt[:, i:i + 1] for i in range(6))
            cur, cand, bi = bits_i[:, 0:1], bits_i[:, 1:2], bits_i[:, 2:3]
            bit, keep, thr = bits[:, 0:1], bits[:, 1:2], bits[:, 2:3]
            lastcol = slice(NB - 1, NB)
            lk(v.tensor_scalar(wnode[:, :], wnode[:, :], brc, None, ALU.add))
            lk(v.tensor_scalar(pen_l, valid_last[:, :], -1.0, 3.0 * BIG, ALU.add, ALU.mult))
            lk(v.tensor_scalar(wnode[:, lastcol], wnode[:, lastcol], valid_last[:, :], pen_l, ALU.mult, ALU.add))
            lk(v.tensor_scalar(lower, iota_f[:, 0:P], pcol[:, :], None, ALU.is_gt))
            lk(v.tensor_scalar(cmpb, wnode[:, :], 0.0, None, ALU.is_ge))
            lk(v.tensor_reduce(cnt, cmpb, AX, ALU.add))
            v.sem_inc(cnt_ready, 1)
            dve.wait_ge(cnt_sum, 1)
            lk(v.tensor_scalar(c0, bank[3][:, 0:1], float(K_SEL), None, ALU.is_ge))
            lk(v.tensor_scalar(sg, c0, 2.0, -1.0, ALU.mult, ALU.add))
            lk(v.tensor_scalar(kp, c0, float(2 * K_SEL - n_nodes - 1), float(n_nodes - K_SEL + 1), ALU.mult, ALU.add))
            lk(v.tensor_scalar(wp, wnode[:, :], sg, None, ALU.mult))
            lk(v.tensor_scalar(wp[:, lastcol], wp[:, lastcol], valid_last[:, :], pen_l, ALU.mult, ALU.add))
            lk(v.memset(bits_i, 0))
            lk(v.memset(bit, float(2 ** 30)))
            KTH = 8
            with dve.Fori(0, 31) as j:
                ck = Chain(dve, vth, KTH * j)
                ck(v.tensor_copy(bi, bit))
                ck(v.tensor_tensor(cand, cur, bi, ALU.bitwise_or))
                ck(v.tensor_scalar(cmpb, wp, cand.bitcast(FP32), None, ALU.is_ge))
                ck(v.tensor_reduce(cnt, cmpb, AX, ALU.add))
                v.sem_inc(cnt_ready, 1)
                dve.wait_ge(cnt_sum, j + 2)
                ck(v.tensor_tensor(keep, bank[3][:, 0:1], kp, ALU.is_ge))
                ck(v.tensor_tensor(bi, keep, bit, ALU.mult))
                ck(v.tensor_tensor(cur, cur, bi, ALU.bitwise_or))
                ck(v.tensor_scalar(bit, bit, 0.5, None, ALU.mult))
                assert ck.n == KTH
            lk(v.tensor_tensor(thr, cur.bitcast(FP32), sg, ALU.mult))
            lk(v.tensor_scalar(sel, wnode[:, :], thr, None, ALU.is_gt))
            lk(v.tensor_scalar(eqm, wnode[:, :], thr, None, ALU.is_equal))
            lk(v.tensor_reduce(cnt, sel, AX, ALU.add))
            v.sem_inc(cnt_ready, 1)
            dve.wait_ge(cnt_sum, 33)
            lk(v.tensor_scalar(need, bank[3][:, 0:1], -1.0, float(K_SEL), ALU.mult, ALU.add))
            tot = bank[4][:, 0:NB]
            lk(v.tensor_copy(cmpb, tot))
            lk(v.memset(wp, 0.0))
            lk(v.tensor_tensor_scan(rank, cmpb, wp, 0.0, ALU.add, ALU.add))
            lk(v.tensor_tensor(rank, rank, cmpb, ALU.subtract))
            lk(v.tensor_tensor(rank, rank, bank[5][:, 0:NB], ALU.add))
            lk(v.tensor_scalar(rank, rank, need, None, ALU.is_lt))
            lk(v.tensor_tensor(eqm, eqm, rank, ALU.mult))
            lk(v.tensor_tensor(sel, sel, eqm, ALU.add))
            lk(v.tensor_tensor(wnode[:, :], wnode[:, :], sel, ALU.mult))

        def threshold_pe(pe):
            te = nc.tensor
            pe.wait_ge(cnt_ready, 1)
            te.matmul(bank[3][:, 0:1], ones[:, :], wcnt[:, 0:1], start=True, stop=True).then_inc(cnt_sum, 1)
            with pe.Fori(0, 31) as j:
                pe.wait_ge(cnt_ready, j + 2)
                te.matmul(bank[3][:, 0:1], ones[:, :], wcnt[:, 0:1], start=True, stop=True).then_inc(cnt_sum, 1)
            pe.wait_ge(cnt_ready, 33)
            te.matmul(bank[4][:, 0:NB], ones[:, :], eqm, start=True, stop=True)
            te.matmul(bank[5][:, 0:NB], lower, eqm, start=True, stop=True)
            te.matmul(bank[3][:, 0:1], ones[:, :], wcnt[:, 0:1], start=True, stop=True).then_inc(cnt_sum, 1)

        go[0] = 0
        w1f = gpiece(2 * FH).rearrange("p (k n) -> p k n", k=2)
        w2f = gpiece(FC * D).rearrange("p (k n) -> p k n", k=FC)
        b1f = gpiece(FC)
        b2f = gpiece(D)
        hf = gpiece(2 * FC * D).rearrange("p (s f n) -> p s f n", s=2, f=FC)
        bl = gpiece(2 * 2 * D).rearrange("p (s t n) -> p s t n", s=2, t=2)
        yo = gpiece(2 * 2 * D).rearrange("p (s t n) -> p s t n", s=2, t=2)
        ty = gpiece(2 * D).rearrange("p (t n) -> p t n", t=2)
        assert go[0] <= 2 * CT * ROW

        def ffn_dma(sp):
            sp.dma_start(w1f, f_w1.rearrange("(k p) n -> p k n", p=P)).then_inc(f_in, 16)
            sp.dma_start(w2f, f_w2.rearrange("(k p) n -> p k n", p=P)).then_inc(f_in, 16)
            sp.dma_start(b1f, f_b1.rearrange("(k p) -> p k", p=P), allow_slow_non_contiguous=True).then_inc(f_in, 16)
            sp.dma_start(b2f, f_b2[None, :].to_broadcast([P, D])).then_inc(f_in, 16)

            def load(q, s):
                sp.dma_start(bl[:, s, :, :], base_v[ds(q, 1)].rearrange("a p t n -> p (a t) n")).then_inc(b_in[s], 16)

            def step(q, s, more=True):
                settled(sp, f_y, q + 1)
                sp.dma_start(out_v[ds(q, 1)].rearrange("a p t n -> p (a t) n"), yo[:, s, :, :]).then_inc(f_out[s], 16)
                if more:
                    load(q + 2, s)

            load(0, 0)
            load(1, 1)
            with sp.Fori(0, R2 - 1) as r:
                step(2 * r, 0)
                step(2 * r + 1, 1)
            step(NP - 3, 0)
            step(NP - 2, 1, False)
            step(NP - 1, 0, False)
            for s in (0, 1):
                sp.wait_ge(f_out[s], 16 * (R2 + 1 - s))

        def ffn_pe(pe):
            te = nc.tensor
            pe.wait_ge(f_in, 64)

            def up(q, s, first=False):
                zt = accf[:, ds(2 * ROW * q, 2 * D)].rearrange("p (k n) -> p k n", k=2)
                for j in range(FC // 2):
                    if not first:
                        pe.wait_ge(f_act, 4 * q - 3 + j)
                    for f in (2 * j, 2 * j + 1):
                        for k in (0, 1):
                            last = te.matmul(bank[j][:, (f % 2) * D:(f % 2) * D + D], w1f[:, k, f * P:f * P + P], zt[:, k, :],
                                             start=(k == 0), stop=(k == 1))
                    last.then_inc(f_up, 1)

            def down(q, s, first=False):
                pe.wait_ge(f_act, 4 * q + 4)
                if not first:
                    pe.wait_ge(f_y, q - 1)
                for t in (0, 1):
                    for f in range(FC):
                        last = te.matmul(bank[5 + s][:, t * D:t * D + D], hf[:, s, f, t * P:t * P + P], w2f[:, f, :],
                                         start=(f == 0), stop=(f == FC - 1))
                last.then_inc(f_down, 1)

            up(0, 0, True)
            up(1, 1)
            down(0, 0, True)
            up(2, 0)
            down(1, 1, True)
            with pe.Fori(1, R2) as r:
                up(2 * r + 1, 1)
                down(2 * r, 0)
                up(2 * r + 2, 0)
                down(2 * r + 1, 1)
            down(NP - 1, 0)

        def ffn_act(act):
            a = nc.scalar
            act.wait_ge(f_in, 64)

            def body(q, s, first):
                for j in range(FC // 2):
                    act.wait_ge(f_up, 4 * q + j + 1)
                    if j == 0 and not first:
                        act.wait_ge(f_down, q - 1)
                    for f in (2 * j, 2 * j + 1):
                        last = a.activation(hf[:, s, f, :], bank[j][:, (f % 2) * D:(f % 2) * D + D], ACT.Gelu_apprx_tanh,
                                            bias=b1f[:, f:f + 1])
                    last.then_inc(f_act, 1)

            body(0, 0, True)
            body(1, 1, True)
            with act.Fori(1, R2) as r:
                body(2 * r, 0, False)
                body(2 * r + 1, 1, False)
            body(NP - 1, 0, False)

        def ffn_dve(dve, lk):
            v = nc.vector
            dve.wait_ge(f_in, 64)
            KFF = 3

            def body(q, s, r, first):
                ck = Chain(dve, vff, KFF * q)
                dve.wait_ge(f_down, q + 1)
                ck(v.tensor_tensor(ty, bank[5 + s][:, :].rearrange("p (t n) -> p t n", t=2),
                                   b2f[:, None, :].to_broadcast([P, 2, D]), ALU.add))
                dve.wait_ge(b_in[s], 16 * r + 16)
                if not first:
                    dve.wait_ge(f_out[s], 16 * r)
                for t in (0, 1):
                    ck(v.scalar_tensor_tensor(yo[:, s, t, :], ty[:, t, :], wnode[:, ds(2 * q + t, 1)], bl[:, s, t, :], ALU.mult, ALU.add))
                v.sem_inc(f_y, 1)
                assert ck.n == KFF

            body(0, 0, 0, True)
            body(1, 1, 0, True)
            with dve.Fori(1, R2) as r:
                body(2 * r, 0, r, False)
                body(2 * r + 1, 1, r, False)
            body(NP - 1, 0, R2, False)

        @block.sync
        def _(sp):
            sp.dma_start(wcat[:, :, 0:D], Wg.rearrange("(c p) n -> p c n", p=P)).then_inc(ld_w, 16)
            sp.dma_start(attb[:, 0, :], att_src.rearrange("h c -> (h c)")[None, :].to_broadcast([P, D])).then_inc(ld_w, 16)
            sp.dma_start(attb[:, 1, :], att_dst.rearrange("h c -> (h c)")[None, :].to_broadcast([P, D])).then_inc(ld_w, 16)
            sp.dma_start(wraw, w_qkv.rearrange("(c p) n -> p c n", p=P)).then_inc(ld_w, 16)
            sp.dma_start(braw, b_qkv[None, :].to_broadcast([P, 3 * D])).then_inc(ld_w, 16)
            sp.dma_start(samp[0:1, 0:NST - 1].bitcast(I32),
                         dst[0:EP].rearrange("(a t s) -> a t s", a=1, s=ST_T * P)[:, 1:, 0],
                         allow_slow_non_contiguous=True).then_inc(ld_i, 16)
            def load_group(g):
                n = grp(g)
                sp.dma_start(idxI[0:n, g % 2, 0, :], src_t[g * P:g * P + n, :]).then_inc(idx_in[g % 2], 16)
                sp.dma_start(idxI[0:n, g % 2, 1, :], dst_t[g * P:g * P + n, :]).then_inc(idx_in[g % 2], 16)

            for g in range(min(2, NG)):
                load_group(g)
            for g in range(NG):
                n = grp(g)
                if g + 2 < NG:
                    sp.wait_ge(idx_f, g + 1)
                    load_group(g + 2)
                sp.wait_ge(idx_out, g + 1)
                sp.dma_start(srcE_d[:, g * P:g * P + n], idxO[:, g % 2, 0, 0:n].bitcast(I32)).then_inc(idx_stored[g % 2], 16)
                sp.dma_start(dstE_d[:, g * P:g * P + n], idxO[:, g % 2, 1, 0:n]).then_inc(idx_stored[g % 2], 16)
            for k in range(DQ):
                n = min(1024, NT - k * 1024)
                if k:
                    sp.wait_ge(d16_ready, k)
                sp.dma_start(d32[:, 0:n], dst[1:1 + EP].rearrange("(p t) -> p t", p=P)[:, k * 1024:k * 1024 + n]).then_inc(d32_in, 16)
            sp.wait_ge(d16_ready, DQ)
            sp.dma_start(dst16_d, d16).then_inc(d16_stored, 16)
            def load_x(q, s):
                sp.dma_start(xin[:, s, :, :], x_v[q]).then_inc(x_in[s], 16)

            def store(q, s, tick):
                settled(sp, row_ready, tick + 1)
                sp.dma_start(tab_v[q], xrow[:, s, :, :]).then_inc(tab_out[s], 16)
                sp.dma_start(xnT_d[q].rearrange("p (k n) -> p k n", k=2), xt[:, s, :, :]).then_inc(xt_out[s], 16)

            load_x(0, 0)
            load_x(1, 1)
            with sp.Fori(0, R2 - 1) as r:
                for u in (0, 1):
                    q = 2 * r + u
                    settled(sp, xn_ready, q + 1)
                    load_x(q + 2, u)
                    store(q, u, q)
            for q in range(NP - 3, NP):
                if q + 2 < NP:
                    settled(sp, xn_ready, q + 1)
                    load_x(q + 2, q % 2)
                store(q, q % 2, q)
            for s in (0, 1):
                sp.wait_ge(tab_out[s], 16 * (R2 + 1 - s))
                sp.wait_ge(xt_out[s], 16 * (R2 + 1 - s))
                sp.wait_ge(idx_stored[s], 32 * ((NG + 1 - s) // 2))
            sp.wait_ge(d16_stored, 16)
            barrier(sp, 1)
            def load_rows(c, s):
                sp.dma_start(sidx[:, s, :], srcE_d[:, ds(c * CT, CT)]).then_inc(idx_ld[s], 16)
                for h in range(HG):
                    win = dst[ds(c * (CT * P), CT * P)]
                    rowap = bass.AP(tensor=win.tensor, offset=win.offset, ap=[[P, CT], [1, P + 2]])
                    sp.dma_start(drow[h * CT:(h + 1) * CT, s, :], rowap).then_inc(drow_in[s], 16)

            def load_dst(c, s):
                sp.dma_start(dstE[:, s, :], dstE_d[:, ds(c * CT, CT)]).then_inc(dste_in[s], 16)

            def load_all_dst(c):
                sp.dma_start(dbc, dst16_d.rearrange("p t -> (p t)")[ds(c * (CT * P), CT * P)][None, :].to_broadcast([P, CT * P])).then_inc(dbc_in, 16)

            def load_xt(c):
                sp.dma_start(xtk, xnT_d[ds(c, 1)].rearrange("a p (k n) -> p (a k) n", k=2)).then_inc(xtk_in, 16)

            def feed(c, s, summed=True, rows=True):
                if summed:
                    settled(sp, dste_used, c)
                    load_dst(c + 1, 1 - s)
                settled(sp, d_read, c + 2)
                load_xt(c)
                settled(sp, kv_acc, c + 2)
                load_all_dst(c + 1)
                settled(sp, one0_ready, c + 1)
                if rows:
                    load_rows(c + 2, s)

            for c in (0, 1):
                load_rows(c, c)
                load_dst(c, c)
            load_all_dst(0)
            feed(0, 0, summed=False)
            with sp.Fori(0, R2 - 1) as r:
                feed(2 * r + 1, 1)
                feed(2 * r + 2, 0)
            feed(NCH - 2, 1, rows=False)
            settled(sp, d_read, NCH + 1)
            load_xt(NCH - 1)
            barrier(sp, 2)
            load_mix(sp)
            barrier(sp, 3)
            node_loads(sp)
            barrier(sp, 4)
            ffn_dma(sp)

        @block.gpsimd
        def _(pool):
            nc.gpsimd.iota(iotaI, [[1, 512]], base=0, channel_multiplier=0).then_inc(iota_done, 1)
            nc.gpsimd.iota(pcolI, [[0, 1]], base=0, channel_multiplier=1).then_inc(iota_done, 1)
            barrier(pool, 1)
            def gather(c, s, users, wait_free):
                pool.wait_ge(idx_ld[s], 16 * users)
                pool.sem_inc(pace, 1)
                for t in range(CT):
                    if wait_free and t % ST_T == 0:
                        pool.wait_ge(oe_used, SC * (c - 2) + t // ST_T + 3)
                        pool.sem_inc(pace, 1)
                    nc.gpsimd.indirect_dma_start(
                        out=G[:, s, t, :], out_offset=None, in_=tab_d,
                        in_offset=bass.IndirectOffsetOnAxis(ap=sidx[:, s, t:t + 1], axis=0)).then_inc(rows_in[s], 16)

            gather(0, 0, 1, False)
            gather(1, 1, 1, False)
            with pool.Fori(1, R2) as r:
                gather(2 * r, 0, r + 1, True)
                gather(2 * r + 1, 1, r + 1, True)
            gather(NCH - 1, 0, R2 + 1, True)
            barrier(pool, 2)
            barrier(pool, 3)
            node_pool(pool)
            barrier(pool, 4)

        @block.vector
        def _(dve):
            v = nc.vector
            lk = Chain(dve, vch)
            dve.wait_ge(iota_done, 2)
            lk(v.tensor_copy(iota_w, iotaI))
            lk(v.tensor_copy(iota_f[:, :], iotaI[:, 0:P]))
            lk(v.tensor_copy(pcol[:, :], pcolI))
            v.memset(ones[:, :], 1.0)
            v.memset(zb[:, :], 0.0)
            lk(v.tensor_scalar(ident[:, :], iota_f[:, 0:P], pcol[:, :], None, ALU.is_equal))
            lk(v.tensor_scalar(valid_last[:, :], pcol[:, :], float(TAIL), None, ALU.is_lt))
            dve.wait_ge(ld_i, 16)
            lk(v.tensor_copy(sampF[0:1, 0:NST - 1], samp[0:1, 0:NST - 1].bitcast(I32)))
            v.sem_inc(prep_dve, 1)
            T, pos, inv, p128 = (small[:, i:i + 1] for i in range(4))
            lk(v.tensor_scalar(p128, pcol[:, :], float(P), None, ALU.mult))
            lk(v.tensor_scalar(inv, pcol[:, :], 1.0, None, ALU.is_lt))
            lk(v.tensor_scalar(pos, pcol[:, :], float(NB - 1), None, ALU.is_gt))
            lk(v.tensor_tensor(inv, inv, pos, ALU.add))
            dve.wait_ge(prep_mm, 1)
            lk(v.tensor_scalar(tmp512[:, 0:NST - 1], bank[0][:, 0:NST - 1], p128, None, ALU.is_lt))
            lk(v.tensor_reduce(T, tmp512[:, 0:NST - 1], AX, ALU.add))
            lk(v.scalar_tensor_tensor(T, inv, 1e6, T, ALU.mult, ALU.add))
            lk(v.tensor_scalar(tmp512[:, 0:NST + 1], iota_w[:, 0:NST + 1], T, None, ALU.is_gt))
            lk(v.tensor_scalar(diagT, ident[:, :], T, None, ALU.mult))
            lk(v.tensor_scalar(block_base[:, :], iota_w[:, 0:NB], float(P), None, ALU.mult))
            v.sem_inc(prep_dve, 1)
            dve.wait_ge(prep_mm, 2)
            lk(v.tensor_scalar(first_base[:, :], bank[0][:, 0:NST + 1], float(P), None, ALU.mult))
            lk(v.tensor_copy(first_block, bank[0][32:33, 0:NST + 1]))
            for table in (extra_tile, extra_at):
                row = slice(64, 65) if table is extra_tile else slice(96, 97)
                lk(v.tensor_copy(table, bank[1][row, 1:NB]))
                lk(v.tensor_scalar(table, table, SC - 1, None, ALU.bitwise_and))
            at_f, hi_f = sampF[96:97, 0:NB - 1], tmp512[96:97, 0:NB - 1]
            lk(v.tensor_copy(at_f, extra_at))
            lk(v.tensor_scalar(hi_f, at_f, float(SC // 2), float(512 - SC // 2 * ST_T * NV), ALU.is_ge, ALU.mult))
            lk(v.scalar_tensor_tensor(extra_at, at_f, float(ST_T * NV), hi_f, ALU.mult, ALU.add))
            dve.wait_ge(ld_w, 80)
            for c in range(2):
                for a in range(2):
                    lk(v.tensor_tensor(wtmp[:, a, :], wcat[:, c, 0:D], attb[:, a, :], ALU.mult))
                lk(v.tensor_reduce(wcat[:, c, D:ROW], wtmp.rearrange("p a (h n) -> p (a h) n", h=HG), AX, ALU.add))

            def centre(dst_ap, raw):
                parts = raw.rearrange("p (h n) -> p h n", h=HM)
                for kind in (0, 1):
                    a = parts[:, :, CM * (1 + kind):CM * (2 + kind)]
                    m = wmean[:, 8 * kind:8 * kind + 8]
                    lk(v.tensor_reduce(m, a, AX, ALU.add))
                    lk(v.tensor_scalar(m, m, 1.0 / CM, None, ALU.mult))
                    lk(v.tensor_tensor(dst_ap[:, D * kind:D * (kind + 1)].rearrange("p (h n) -> p h n", h=HM), a,
                                       m[:, :, None].to_broadcast([P, HM, CM]), ALU.subtract))

            centre(kvw[:, 0, :], wraw[:, 0, :])
            centre(kvw[:, 1, :], wraw[:, 1, :])
            centre(bkv[:, :], braw)
            for g in range(NG):
                n = grp(g)
                dve.wait_ge(idx_in[g % 2], 32 * (g // 2 + 1))
                if g:
                    dve.wait_ge(idx_t, g)
                lk(v.tensor_copy(idxF[0:n, :, :], idxI[0:n, g % 2, :, :]))
                v.sem_inc(idx_f, 1)
                dve.wait_ge(idx_t, g + 1)
                if g >= 2:
                    dve.wait_ge(idx_stored[g % 2], 32 * (g // 2))
                v.tensor_copy(idxO[:, g % 2, 0, 0:n].bitcast(I32), bank[2][:, 0:n])
                lk(v.tensor_copy(idxO[:, g % 2, 1, 0:n], bank[2][:, P:P + n]))
                v.sem_inc(idx_out, 1)
            for k in range(DQ):
                n = min(1024, NT - k * 1024)
                dve.wait_ge(d32_in, 16 * (k + 1))
                lk(v.tensor_copy(d16[:, k * 1024:k * 1024 + n], d32[:, 0:n]))
                v.sem_inc(d16_ready, 1)
            KLN, KSP = 7, 7

            def ln1(q, s, r, first=False):
                ln = Chain(dve, vln, KLN * q)
                dve.wait_ge(x_in[s], 16 * r + 16)
                for t in (0, 1):
                    last = v.bn_stats(bst[:, 6 * t:6 * t + 6], xin[:, s, t, :])
                ln(last)
                v.sem_inc(pace, 1)
                for t in (0, 1):
                    last = v.bn_aggr(mv[:, t, :], bst[:, 6 * t:6 * t + 6])
                ln(last)
                ln(v.tensor_scalar(var[:, 0:2], mv[:, :, 1], EPS, None, ALU.add))
                v.sem_inc(x_var, 1)
                dve.wait_ge(x_std, q + 1)
                ln(v.reciprocal(mv[:, :, 1], var[:, 2:4]))
                if not first:
                    dve.wait_ge(xn_T, q - 1)
                for t in (0, 1):
                    ln(v.tensor_scalar(xn[:, s, t, :], xin[:, s, t, :], mv[:, t, 0:1], mv[:, t, 1:2],
                                       ALU.subtract, ALU.mult))
                ln(v.tensor_copy(stat[:, ds(2 * q, 2), :], mv))
                v.sem_inc(xn_ready, 1)
                assert ln.n == KLN

            def split(q, s):
                ln = Chain(dve, row_split, KSP * q)
                dve.wait_ge(row_ready, q + 1)
                r0, r1 = res[:, 0, :, :], res[:, 1, :, :]
                ln(v.tensor_copy(r0[:, :, 0:HG], xrow[:, s, :, D + HG:ROW]))
                ln(v.tensor_copy(r0[:, :, HG:2 * HG], xrow[:, s, :, D:D + HG]))
                for k in range(3):
                    part = nodeval[:, ds(2 * q, 2), k, :]
                    ln(v.tensor_copy(part, r0))
                    if k < 2:
                        ln(v.tensor_tensor(r0, r0, part, ALU.subtract))
                assert ln.n == KSP

            ln1(0, 0, 0, first=True)
            ln1(1, 1, 0, first=True)
            split(0, 0)
            ln1(2, 0, 1)
            split(1, 1)
            with dve.Fori(1, R2) as r:
                ln1(2 * r + 1, 1, r)
                split(2 * r, 0)
                ln1(2 * r + 2, 0, r + 1)
                split(2 * r + 1, 1)
            split(NP - 1, 0)
            barrier(dve, 1)

            GW = HG * (CT + 1)

            def ghv(i):
                return gh[:, i * GW:(i + 1) * GW]

            def ghh(i):
                return ghv(i).rearrange("p (h t) -> p h t", h=HG)

            lk(v.memset(accf, 0.0))
            lk(v.memset(gh, -BIG))
            for i in (0, 3):
                lk(v.memset(ghv(i), -3.0 * BIG))
            lk(v.memset(r8, 1.0))
            s3 = s_e.rearrange("p (h t) -> p t h", h=HG)
            dn3 = dn.rearrange("p (t k) -> p t k", k=8)
            U3 = U.rearrange("p (a t h) -> p a t h", a=3, h=HG)
            UA = U.rearrange("p (a n) -> p a n", a=3)
            W3 = We.rearrange("p (a t h) -> p a t h", a=2, h=HG)
            KCHUNK = 27
            H2 = CT // 2
            v.sem_inc(d_read, 1)
            v.sem_inc(kv_var, 1)
            v.sem_inc(vx, 1)

            def node_onehots(c, k0):
                for k in range(k0, k0 + 4):
                    if k0:
                        dve.wait_ge(ot_used, SC * c + k - 2)
                    v.tensor_scalar(oneT[k % 4], dbc[:, k * 512:k * 512 + 512],
                                    cb[:, k:k + 1], pcol[:, :], ALU.subtract, ALU.is_equal).then_inc(ot_ready, 1)

            def prep0(c, s, u, ck):
                dve.wait_ge(dste_in[s], 16 * u + 16)
                ck(v.tensor_copy(cb[:, :], first_base[:, ds(c * SC, SC)]))
                ck(v.tensor_tensor(dl[:, s], dstE[:, s].rearrange("p (k t) -> p k t", t=ST_T),
                                   cb[:, :, None].to_broadcast([P, SC, ST_T]), ALU.subtract))
                dve.wait_ge(dbc_in, 16 * c + 16)
                dve.wait_ge(a_scaled, c + 1)
                node_onehots(c, 0)

            def prep1(c, s, u, ck):
                node_onehots(c, 4)

            def prep2(c, s, u, ck, lo, hi):
                settled(dve, ot_used, SC * c + SC + 1)
                with dve.Fori(lo, hi) as e:
                    tl = dve.value_load(extra_tile[0:1, ds(e, 1)], min_val=0, max_val=SC - 1)
                    dve.wait_ge(xo_used, e + 1)
                    v.tensor_scalar(oneT[0], dbc[:, ds(tl * 512, 512)], block_base[:, ds(e + 1, 1)], pcol[:, :],
                                    ALU.subtract, ALU.is_equal).then_inc(xo_ready, 1)
                dve.wait_ge(drow_in[s], 64 * u + 64)
                ck(v.tensor_tensor(neq, drow[:, s, 0:P + 1], drow[:, s, 1:P + 2], ALU.not_equal))
                ck(v.tensor_tensor(sng, drow[:, s, 1:2], drow[:, s, P:P + 1], ALU.not_equal))
                dve.wait_ge(xo_used, hi + 1)
                for a in (0, 1):
                    last = v.tensor_reduce(dn3[:, a * H2:a * H2 + H2, :],
                                           one[:, a, 0:H2 * NV].rearrange("p (t j k) -> p t k j", j=3, k=8), AX, ALU.add)
                ck(last)
                v.sem_inc(d_read, 1)
                dve.wait_ge(rows_in[s], 16 * CT * u + 16 * CT)
                v.tensor_tensor(s3, G[:, s, :, D:D + HG], dn3[:, :, HG:2 * HG], ALU.max).then_inc(s_ready, 1)
                v.tensor_scalar(pen, neq, -BIG, None, ALU.mult)
                ck(v.tensor_scalar(sng, sng, -BIG, None, ALU.mult))
                ck(v.tensor_scalar(x4[:, 2:3], pen[:, 0:1], sng, None, ALU.add))
                ck(v.tensor_scalar(x4[:, 3:4], pen[:, P:P + 1], sng, None, ALU.add))

            def add_bias(c, t, ck):
                dve.wait_ge(kv_mm, 2 * c + t + 1)
                v.tensor_tensor(kv[:, t, :], bank[7][:, :], bkv[:, :], ALU.add).then_inc(kv_biased, 1)

            def reduce_squares(c, t, ck):
                dve.wait_ge(kv_sq, 2 * c + t + 1)
                ck(v.tensor_reduce(rs[:, t, :], sq.rearrange("p (g n) -> p g n", n=CM), AX, ALU.add))
                v.sem_inc(kv_var, 1)

            def prep3(c, s, u, ck):
                dve.wait_ge(sT_ready, c + 1)
                v.tensor_copy(sT, bank[1][:, 0:P])
                ck(v.tensor_copy(first, bank[1][:, P:2 * P]))
                ck(v.tensor_tensor_scan(fw, pen[:, 0:P], sT, -BIG, ALU.add, ALU.max))
                ck(v.tensor_tensor_scan(bw[:, ::-1], pen[:, 1:P + 1][:, ::-1], sT[:, ::-1], -BIG, ALU.add, ALU.max))
                v.tensor_copy(x4[:, 0:1], fw[:, P - 1:P])
                v.tensor_copy(x4[:, 1:2], bw[:, 0:1]).then_inc(x4_ready, 1)

            def prep4(c, s, u, ck):
                dve.wait_ge(r_ready, c + 1)
                pr = bank[2][0:1, :].rearrange("p (k h t) -> p k h t", k=4, h=HG)
                v.tensor_copy(ghh(0)[:, :, 1:CT + 1], pr[:, 2])
                v.tensor_copy(ghh(1)[:, :, 1:CT + 1], pr[:, 0])
                v.tensor_copy(ghh(3)[:, :, 0:CT], pr[:, 3])
                ck(v.tensor_copy(ghh(4)[:, :, 0:CT], pr[:, 1]))
                ck(v.tensor_tensor_scan(ghv(2), ghv(0), ghv(1), -BIG, ALU.add, ALU.max))
                ck(v.tensor_tensor_scan(ghv(5)[:, ::-1], ghv(3)[:, ::-1], ghv(4)[:, ::-1], -BIG, ALU.add, ALU.max))
                dve.wait_ge(fac_ready, c + 1)
                v.tensor_copy(cin[:, 0:P].rearrange("p (h t) -> p h t", h=HG), ghh(2)[:, :, 0:CT])
                v.tensor_copy(cin[:, P:2 * P].rearrange("p (h t) -> p h t", h=HG), ghh(5)[:, :, 1:CT + 1]).then_inc(gh_ready, 1)
                dve.wait_ge(kv_acc, c + 1)
                add_bias(c, 0, ck)

            def prep5(c, s, u, ck):
                dve.wait_ge(c_ready, c + 1)
                ck(v.tensor_copy(c2, bank[1][:, 2 * P:2 * P + 2]))
                v.tensor_tensor_scan(fw, pen[:, 0:P], sT, c2[:, 0:1], ALU.add, ALU.max)
                ck(v.tensor_tensor_scan(bw[:, ::-1], pen[:, 1:P + 1][:, ::-1], sT[:, ::-1], c2[:, 1:2], ALU.add, ALU.max))
                v.tensor_tensor(fw, fw, bw, ALU.max).then_inc(mm_ready, 1)
                reduce_squares(c, 0, ck)
                add_bias(c, 1, ck)

            def prep6(c, s, u, ck):
                v.tensor_tensor(U3[:, 0], G[:, s, :, D:D + HG], dn3[:, :, 0:HG], ALU.add)
                v.tensor_tensor(U3[:, 1], dn3[:, :, HG:2 * HG], dn3[:, :, 0:HG], ALU.add)
                dve.wait_ge(m_ready, c + 1)
                ck(v.tensor_tensor(U3[:, 2], bank[1][:, 272:272 + P].rearrange("p (h t) -> p t h", h=HG), dn3[:, :, 0:HG], ALU.add))
                ck(v.scalar_tensor_tensor(U, U, 0.2, U, ALU.mult, ALU.max))
                ck(v.tensor_tensor(UA[:, 0:2], UA[:, 0:2],
                                   U[:, None, 2 * P:3 * P].to_broadcast([P, 2, P]), ALU.subtract))
                ck(v.tensor_tensor(rl, ghh(1)[:, :, 0], dn3[0:1, 0, 0:HG], ALU.add))
                ck(v.scalar_tensor_tensor(rl, rl, 0.2, rl, ALU.mult, ALU.max))
                ck(v.tensor_tensor(rl, rl, U3[0:1, 2, 0, :], ALU.subtract))
                v.tensor_scalar(rl, rl, 0.0, None, ALU.min).then_inc(u_ready, 1)
                v.tensor_copy(ghh(1)[:, :, 0], ghh(2)[:, :, CT])
                v.tensor_scalar(one0, iota_f[0:1, 0:P], cb[0:1, 0:1], dstE[0:1, s, 0:1], ALU.add, ALU.is_equal).then_inc(one0_ready, 1)
                reduce_squares(c, 1, ck)
                v.tensor_scalar(rs[:, :, :], rs[:, :, :], 1.0 / CM, EPS, ALU.mult, ALU.add).then_inc(kv_var, 1)

            def prep7(c, s, u, ck):
                dve.wait_ge(kv_std, c + 1)
                ck(v.tensor_scalar(sng, block_base[:, ds(2 * c + 1, 1)], pcol[:, :], float(n_nodes), ALU.add, ALU.is_lt))
                ck(v.reciprocal(rs[:, :, :], rs[:, :, :]))
                ck(v.tensor_scalar(rs[:, 1, :], rs[:, 1, :], sng, None, ALU.mult))
                for t in (0, 1):
                    last = v.tensor_tensor(kv[:, t, :].rearrange("p (g n) -> p g n", n=CM), kv[:, t, :].rearrange("p (g n) -> p g n", n=CM),
                                           rs[:, t, :][:, :, None].to_broadcast([P, 16, CM]), ALU.mult)
                last.then_inc(kv_norm, 1)
                dve.wait_ge(w_ready, c + 1)
                v.tensor_copy(G[:, s, :, D:D + HG], W3[:, 0])
                v.tensor_tensor(G[:, s, :, D + HG:ROW], W3[:, 1], first.rearrange("p (h t) -> p t h", h=HG), ALU.mult)
                gm = G[:, s, :, 0:D].rearrange("p t (h n) -> p t h n", h=HG)
                for k in range(SC - ACT_ST):
                    q4 = slice(k * ST_T, k * ST_T + ST_T)
                    last = v.tensor_tensor(gm[:, q4], gm[:, q4], W3[:, 0, q4][:, :, :, None].to_broadcast([P, ST_T, HG, CG]), ALU.mult)
                last.then_inc(g_ready, 1)

            preps = (prep0, prep1, prep2, prep3, prep4, prep5, prep6, prep7)

            def sum_extras(c, s, lo, hi):
                dve.wait_ge(sum_added, SC * c + 2)
                dve.wait_ge(fac_ready, c + 2)
                fk = Chain(dve, vfac, 3 * c)
                fk(v.tensor_scalar(fac, bank[1][:, 400 + HG:400 + 2 * HG], -1.0, 1.0, ALU.mult, ALU.add))
                fk(v.tensor_tensor(fac, fac, bank[1][:, 400:400 + HG], ALU.add))
                am = acc[:, ds(lo, 1), 0:D].rearrange("p a (h n) -> p (a h) n", h=HG)
                at = acc[:, ds(lo, 1), D:ROW].rearrange("p a (k h) -> p (a k) h", h=HG)
                v.tensor_tensor(am, am, fac[:, :, None].to_broadcast([P, HG, CG]), ALU.mult)
                fk(v.tensor_tensor(at, at, fac[:, None, :].to_broadcast([P, 2, HG]), ALU.mult))
                v.sem_inc(pace, 1)
                with dve.Fori(lo, hi) as e:
                    tl = dve.value_load(extra_tile[0:1, ds(e, 1)], min_val=0, max_val=SC - 1)
                    dve.wait_ge(vx, e + 1)
                    v.scalar_tensor_tensor(oneE[:, 0], iota_f[:, None, :].to_broadcast([P, ST_T, P]), block_base[:, ds(e + 1, 1)],
                                           dstE[:, s, ds(tl * ST_T, ST_T)][:, :, None].to_broadcast([P, ST_T, P]),
                                           ALU.add, ALU.is_equal).then_inc(xe_ready, 1)
                    dve.wait_ge(xe_done, e + 1)
                    a = acc[:, ds(e + 1, 1), :].rearrange("p a r -> p (a r)")
                    v.tensor_tensor(a, a, bank[3][:, 0:ROW], ALU.add).then_inc(vx, 1)
                dve.wait_ge(vx, hi + 1)
                v.sem_inc(dste_used, 1)

            def edge_onehots(c, s, k):
                dve.wait_ge(oe_used, SC * c + k + 1)
                v.tensor_tensor(oneE[:, k % 2], iota_f[:, None, :].to_broadcast([P, ST_T, P]),
                                dl[:, s, k, :, None].to_broadcast([P, ST_T, P]), ALU.is_equal).then_inc(oe_ready, 1)

            def add_sum(c, k, b):
                dve.wait_ge(oe_used, SC * c + k + 3)
                dve.wait_ge(sum_added, SC * c + k + 2)
                a = acc[:, ds(b, 1), :].rearrange("p a r -> p (a r)")
                v.tensor_tensor(a, a, bank[3 + k % 2][:, 0:ROW], ALU.add).then_inc(sum_added, 1)

            def first_blocks(eng, c, n):
                return [eng.value_load(first_block[0:1, ds((c + j) * SC, 1)], min_val=0, max_val=NB - 1) for j in range(n)]

            def edge_step(c, s, nxt, u):
                ck = Chain(dve, vck, nxt * KCHUNK) if nxt is not None else None
                if c is None:
                    at = [0] + first_blocks(dve, nxt, 2)
                else:
                    at = first_blocks(dve, c, 3 if nxt is not None else 2)
                    sum_extras(c, s, at[0], at[1])
                    edge_onehots(c, s, 0)
                for k in range(SC):
                    if c is not None:
                        b = dve.value_load(first_block[0:1, ds(c * SC + k, 1)], min_val=0, max_val=NB - 1)
                        if k + 1 < SC:
                            edge_onehots(c, s, k + 1)
                    if nxt is not None:
                        preps[k](nxt, 1 - s, u, ck, *(at[1:3] if k == 2 else ()))
                    if c is not None:
                        add_sum(c, k, b)
                assert ck is None or ck.n == KCHUNK, ck.n

            edge_step(None, 1, 0, 0)
            with dve.Fori(0, R2) as r:
                edge_step(2 * r, 0, 2 * r + 1, r)
                edge_step(2 * r + 1, 1, 2 * r + 2, r + 1)
            edge_step(NCH - 1, 0, None, 0)
            dve.wait_ge(sum_added, SC * NCH + 2)
            barrier(dve, 2)
            mix_weights_dve(dve, lk)
            barrier(dve, 3)
            node_dve(dve)
            threshold_dve(dve, lk)
            barrier(dve, 4)
            ffn_dve(dve, lk)

        @block.scalar
        def _(act):
            a = nc.scalar

            def std1(q):
                act.wait_ge(x_var, q + 1)
                a.activation(var[:, 2:4], var[:, 0:2], ACT.Sqrt).then_inc(x_std, 1)

            def rows1(q, s, r):
                act.wait_ge(xn_T, q + 1)
                if r is not None:
                    act.wait_ge(xt_out[s], 16 * r)
                    act.wait_ge(tab_out[s], 16 * r)
                    act.wait_ge(row_split, 7 * (q - 1))
                a.copy(xt[:, s, :, :], bank[3][:, :].rearrange("p (k n) -> p k n", k=2)).then_inc(xt_ready, 1)
                for t in (0, 1):
                    act.wait_ge(xp_ready, 2 * q + t + 1)
                    last = a.copy(xrow[:, s, t, :], bank[4 + t][:, 0:ROW])
                last.then_inc(row_ready, 1)

            std1(0)
            std1(1)
            rows1(0, 0, None)
            std1(2)
            rows1(1, 1, None)
            with act.Fori(1, R2) as r:
                for u in (0, 1):
                    q = 2 * r + u
                    std1(q + 1)
                    rows1(q, u, r)
            rows1(NP - 1, 0, R2)
            barrier(act, 1)

            Wt = We.rearrange("p (a t h) -> p a t h", a=2, h=HG)
            act.sem_inc(a_scaled, 1)

            def edge_act(c, s):
                for k in range(SC):
                    b = act.value_load(first_block[0:1, ds(c * SC + k, 1)], min_val=0, max_val=NB - 1)
                    if k == 0:
                        act.wait_ge(ot_used, SC * c + 1)
                    last = a.copy(nv[:, k, :], nodeval[:, ds(b, 1), :, :].rearrange("p a j k -> p (a j k)"))
                last.then_inc(nv_ready, 1)
                for t in (0, 1):
                    act.wait_ge(kv_biased, 2 * c + t + 1)
                    act.wait_ge(kv_var, 3 * c + t + 1)
                    a.activation(sq, kv[:, t, :], ACT.Square).then_inc(kv_sq, 1)
                act.wait_ge(u_ready, c + 1)
                a.activation(We, U[:, 0:2 * P], ACT.Exp)
                a.activation(r8[:, 0:HG], rl, ACT.Exp).then_inc(w_ready, 1)
                act.wait_ge(kv_var, 3 * c + 4)
                a.activation(rs[:, :, :], rs[:, :, :], ACT.Sqrt).then_inc(kv_std, 1)
                act.wait_ge(w_ready, c + 1)
                for t in range(CT - ACT_ST * ST_T, CT):
                    for h in range(HG):
                        g = G[:, s, t, h * CG:(h + 1) * CG]
                        last = a.activation(g, g, ACT.Copy, scale=Wt[:, 0, t, h:h + 1])
                last.then_inc(a_scaled, 1)

            paired(act, lambda c, s, r: edge_act(c, s))
            barrier(act, 2)
            barrier(act, 3)
            node_act(act)
            barrier(act, 4)
            ffn_act(act)

        @block.tensor
        def _(pe):
            te = nc.tensor
            pe.wait_ge(prep_dve, 1)
            te.matmul(bank[0][:, 0:NST - 1], ones[0:1, :], sampF[0:1, 0:NST - 1], start=True, stop=True).then_inc(prep_mm, 1)
            pe.wait_ge(prep_dve, 2)
            te.matmul(bank[0][:, 0:NST + 1], ones[:, :], tmp512[:, 0:NST + 1], start=True, stop=True)
            te.matmul(bank[1][:, 0:P], ones[:, :], diagT, start=True, stop=True).then_inc(prep_mm, 1)
            for g in range(NG):
                n = grp(g)
                pe.wait_ge(idx_f, g + 1)
                if g:
                    pe.wait_ge(idx_out, g)
                te.transpose(bank[2][:, 0:n], idxF[0:n, 0, :], ident[0:n, 0:n])
                te.transpose(bank[2][:, P:P + n], idxF[0:n, 1, :], ident[0:n, 0:n]).then_inc(idx_t, 1)

            def turn(q, s):
                pe.wait_ge(xn_ready, q + 1)
                for k in (0, 1):
                    for t in (0, 1):
                        last = te.transpose(bank[3][:, k * 256 + t * P:k * 256 + t * P + P], xn[:, s, t, k * P:k * P + P], ident[:, :])
                last.then_inc(xn_T, 1)

            def project(q, s):
                pe.wait_ge(xt_ready, q + 1)
                for t in (0, 1):
                    for k in (0, 1):
                        last = te.matmul(bank[4 + t][:, 0:ROW], xt[:, s, k, t * P:t * P + P], wcat[:, k, :], start=(k == 0), stop=(k == 1))
                    last.then_inc(xp_ready, 1)

            turn(0, 0)
            project(0, 0)
            turn(1, 1)
            pe.wait_ge(row_ready, 1)
            project(1, 1)
            with pe.Fori(1, R2) as r:
                for u in (0, 1):
                    q = 2 * r + u
                    turn(q, u)
                    pe.wait_ge(row_ready, q)
                    project(q, u)
            turn(NP - 1, 0)
            pe.wait_ge(row_ready, NP - 1)
            project(NP - 1, 0)
            barrier(pe, 1)

            pe.sem_inc(ot_used, 1)
            pe.sem_inc(xo_used, 1)
            pe.sem_inc(oe_used, 2)
            pe.sem_inc(sum_added, 2)
            pe.sem_inc(kv_acc, 1)
            pe.sem_inc(fac_ready, 1)
            zr = nodeval[:, :, :, :].rearrange("p b j k -> p (b j k)")
            for kbank in (5, 6):
                for z0 in range(0, 512, P):
                    last = te.matmul(bank[kbank][:, z0:z0 + P], zb[:, :], zr[:, 0:P], start=True, stop=False, skip_group_check=True)

            def node_values(c, k0):
                if k0 == 0:
                    pe.wait_ge(d_read, c + 1)
                    for a in (0, 1):
                        for z0 in (0, SC * NV):
                            te.matmul(one[:, a, z0:z0 + SC * NV], zb[:, :], zr[:, 0:SC * NV], start=True, stop=False, skip_group_check=True)
                    pe.wait_ge(nv_ready, c + 1)
                for k in range(k0, k0 + 4):
                    pe.wait_ge(ot_ready, SC * c + k + 1)
                    for t in range(ST_T):
                        at = (k * ST_T + t) % (CT // 2) * NV
                        last = te.matmul(one[:, 2 * k // SC, at:at + NV], oneT[k % 4][:, t * P:t * P + P], nv[:, k, :],
                                         start=False, stop=False, skip_group_check=True)
                    last.then_inc(ot_used, 1)

            def extra_values(c, lo, hi):
                with pe.Fori(lo, hi) as e:
                    at = pe.value_load(extra_at[0:1, ds(e, 1)], min_val=0, max_val=1024 - ST_T * NV)
                    pe.wait_ge(xo_ready, e + 1)
                    for t in range(ST_T):
                        last = te.matmul(onef[:, ds(at + t * NV, NV)], oneT[0][:, t * P:t * P + P],
                                         nodeval[:, ds(e + 1, 1), :, :].rearrange("p a j k -> p (a j k)"),
                                         start=False, stop=False, skip_group_check=True)
                    last.then_inc(xo_used, 1)

            def kv_product(c, t):
                if t:
                    pe.wait_ge(kv_biased, 2 * c + 1)
                else:
                    pe.wait_ge(xtk_in, 16 * c + 16)
                for k in (0, 1):
                    last = te.matmul(bank[7][:, :], xtk[:, k, t * P:t * P + P], kvw[:, k, :], start=(k == 0), stop=(k == 1))
                last.then_inc(kv_mm, 1)

            def after(c, k):
                if k == 0:
                    node_values(c, 0)
                elif k == 1:
                    node_values(c, 4)
                elif k == 2:
                    pe.wait_ge(s_ready, c + 1)
                    te.transpose(bank[1][:, 0:P], s_e, ident[:, :])
                    te.transpose(bank[1][:, P:2 * P], neq[:, 0:P], ident[:, :]).then_inc(sT_ready, 1)
                elif k == 3:
                    pe.wait_ge(x4_ready, c + 1)
                    for j in range(4):
                        last = te.transpose(bank[2][0:1, j * P:j * P + P], x4[:, j:j + 1], ident[:, :])
                    last.then_inc(r_ready, 1)
                    kv_product(c, 0)
                elif k == 4:
                    pe.wait_ge(gh_ready, c + 1)
                    pe.sem_inc(pace, 1)
                    te.transpose(bank[1][:, 2 * P:2 * P + 1], cin[:, 0:P], ident[0:1, 0:1])
                    te.transpose(bank[1][:, 2 * P + 1:2 * P + 2], cin[:, P:2 * P], ident[0:1, 0:1]).then_inc(c_ready, 1)
                    kv_product(c, 1)
                elif k == 5:
                    pe.wait_ge(mm_ready, c + 1)
                    te.transpose(bank[1][:, 272:272 + P], fw, ident[:, :]).then_inc(m_ready, 1)
                elif k == 7:
                    pe.wait_ge(kv_norm, c + 1)
                    for t in (0, 1):
                        for h2 in (0, 1):
                            te.matmul(bank[5][:, h2 * P:h2 * P + P], kv[:, t, h2 * P:h2 * P + P], kv[:, t, D + h2 * P:D + h2 * P + P],
                                      start=False, stop=False, skip_group_check=True)
                            te.matmul(bank[5][:, 256 + h2:257 + h2], kv[:, t, h2 * P:h2 * P + P], ones[:, 0:1],
                                      start=False, stop=False, skip_group_check=True)
                        last = te.matmul(bank[6][:, 0:D], ones[:, :], kv[:, t, D:2 * D], start=False, stop=False, skip_group_check=True)
                    last.then_inc(kv_acc, 1)
                    pe.wait_ge(w_ready, c + 1)
                    pe.wait_ge(one0_ready, c + 1)
                    te.matmul(bank[1][:, 400:400 + 2 * HG], one0, r8, start=True, stop=True).then_inc(fac_ready, 1)

            def sum_extras(c, s, lo, hi):
                pe.wait_ge(g_ready, c + 1)
                settled(pe, a_scaled, c + 2)
                with pe.Fori(lo, hi) as e:
                    tl = pe.value_load(extra_tile[0:1, ds(e, 1)], min_val=0, max_val=SC - 1)
                    rows = G[:, s, ds(tl * ST_T, ST_T), :]
                    pe.wait_ge(xe_ready, e + 1)
                    for k in range(ST_T):
                        last = te.matmul(bank[3][:, 0:ROW], oneE[:, 0, k, :], rows[:, k, :],
                                         start=(k == 0), stop=(k == ST_T - 1))
                    last.then_inc(xe_done, 1)
                pe.wait_ge(vx, hi + 1)

            def sum_rows(c, s, k):
                pe.wait_ge(oe_ready, SC * c + k + 1)
                pe.wait_ge(sum_added, SC * c + k + 1)
                for t in range(ST_T):
                    last = te.matmul(bank[3 + k % 2][:, 0:ROW], oneE[:, k % 2, t, :], G[:, s, k * ST_T + t, :],
                                     start=(t == 0), stop=(t == ST_T - 1))
                last.then_inc(oe_used, 1)

            def edge_step(c, s, nxt):
                start = nxt if c is None else c
                at = [pe.value_load(first_block[0:1, ds((start + j) * SC, 1)], min_val=0, max_val=NB - 1)
                      for j in range(2 + (c is not None and nxt is not None))]
                if c is not None:
                    sum_extras(c, s, at[0], at[1])
                for k in range(SC):
                    if nxt is not None and k == 2:
                        extra_values(nxt, at[-2], at[-1])
                    if c is not None:
                        sum_rows(c, s, k)
                    if nxt is not None:
                        after(nxt, k)

            edge_step(None, 1, 0)
            with pe.Fori(0, R2) as r:
                edge_step(2 * r, 0, 2 * r + 1)
                edge_step(2 * r + 1, 1, 2 * r + 2)
            edge_step(NCH - 1, 0, None)
            barrier(pe, 2)
            mix_weights_pe(pe)
            barrier(pe, 3)
            node_pe(pe)
            threshold_pe(pe)
            barrier(pe, 4)
            ffn_pe(pe)


_F32 = ["L0_gnn_W", "L0_gnn_att_src", "L0_gnn_att_dst", "L0_gnn_bias", "L0_mix_w_qkv", "L0_mix_b_qkv", "L0_mix_kln_g",
        "L0_mix_kln_b", "L0_mix_vln_g", "L0_mix_vln_b", "L0_mix_w1", "L0_mix_b1", "L0_mix_w2", "L0_mix_b2", "L0_ffn_wr",
        "L0_ffn_br", "L0_ffn_w1", "L0_ffn_b1", "L0_ffn_w2", "L0_ffn_b2"]


def kernel(**inputs):
    import concourse.bacc as bacc
    from concourse.bass_utils import run_bass_kernel_spmd

    nc = bacc.Bacc("TRN2", target_bir_lowering=False, num_devices=1)
    x = np.asarray(inputs["x"])
    src, dst = np.asarray(inputs["src"]), np.asarray(inputs["dst"])
    n, e = x.shape[0], src.shape[0]
    npad = -(-n // P) * P
    ep = -(-e // (P * CT)) * (P * CT)
    arrays = {"x_in": np.zeros((npad, x.shape[1]), x.dtype), "src_in": np.zeros((ep,), src.dtype),
              "dst_in": np.full((ep + 2,), npad - 1, dst.dtype)}
    arrays["x_in"][:n] = x
    arrays["src_in"][:e] = src
    arrays["dst_in"][1:1 + e] = dst
    arrays["dst_in"][0] = -1
    for name in _F32:
        arrays[name] = np.ascontiguousarray(inputs[name])
    args = [nc.dram_tensor(k, a.shape, mybir.dt.from_np(a.dtype), kind="ExternalInput").ap() for k, a in arrays.items()]
    out = nc.dram_tensor("out", (npad, x.shape[1]), FP32, kind="ExternalOutput").ap()
    gps_kernel(nc, n, e, *args, out)
    r = run_bass_kernel_spmd(nc, [arrays], core_ids=[0])
    return r.results[0]["out"][:n]
```

```python
import numpy as np
import concourse.bass as bass
from concourse import mybir
from contextlib import ExitStack

FP32 = mybir.dt.float32
BF16 = mybir.dt.bfloat16
I32 = mybir.dt.int32
I16 = mybir.dt.int16
ALU = mybir.AluOpType
ACT = mybir.ActivationFunctionType
AX = mybir.AxisListType.X
P = 128
CT = 32
ST_T = 4
ACT_ST = 3
BIG = 1e38


def ds(start, size):
    return bass.ds(start, size)


class Chain:

    def __init__(self, eng, sem, base=0):
        self.eng, self.sem, self.base, self.n = eng, sem, base, 0

    def __call__(self, ins):
        ins.then_inc(self.sem, 1)
        self.n += 1
        self.eng.wait_ge(self.sem, self.base + self.n)


def gps_kernel(nc, n_nodes, n_edges, x, src, dst, Wg, att_src, att_dst, g_bias, w_qkv, b_qkv, kln_g, kln_b,
               vln_g, vln_b, m_w1, m_b1, m_w2, m_b2, f_wr, f_br, f_w1, f_b1, f_w2, f_b2, out):
    D, HG, HM = 256, 4, 8
    CG, CM = D // HG, D // HM
    FH = 4 * D
    FC = FH // P
    NPAD = x.shape[0]
    NB = NPAD // P
    NP = NB // 2
    EP = src.shape[0]
    NT = EP // P
    NST = NT // ST_T
    SC = CT // ST_T
    NCH = NT // CT
    ROW = D + 2 * HG
    K_SEL = max(1, int(0.5 * n_nodes)) - 1
    NQ = -(-K_SEL // (2 * P))
    EPS = 1e-5
    TAIL = n_nodes - (NB - 1) * P
    assert NB == 2 * NP and NP == NCH and NP % 2 == 1 and NQ % 2 == 1 and NST < 512 and n_edges <= EP

    ctx = ExitStack()
    with ctx:
        def sb(name, shape, dt=FP32):
            return ctx.enter_context(nc.sbuf_tensor(name, shape, dt))

        def sem(name):
            return ctx.enter_context(nc.semaphore(name))

        tab_d = nc.dram_tensor("tab_d", [NPAD, ROW], FP32).ap()
        xnT_d = nc.dram_tensor("xnT_d", [NP, P, 2 * 2 * P], FP32).ap()
        srcE_d = nc.dram_tensor("srcE_d", [P, NT], I32).ap()
        dstE_d = nc.dram_tensor("dstE_d", [P, NT], FP32).ap()
        dst16_d = nc.dram_tensor("dst16_d", [P, NT], I16).ap()
        z_d = nc.dram_tensor("z_d", [NPAD, D], FP32).ap()
        base_d = nc.dram_tensor("base_d", [NPAD, D], FP32).ap()
        perm_d = nc.dram_tensor("perm_d", [NPAD, 2], FP32).ap()

        one = ctx.enter_context(nc.psum_tensor("values", [P, 2, 512], FP32))
        bank = [ctx.enter_context(nc.psum_tensor(f"bank{i}", [P, 512], FP32)) for i in range(1, 7)]
        bank = [one[:, 0, :], bank[0], one[:, 1, :]] + bank[1:]
        onef = one[:, :, :].rearrange("p a n -> p (a n)")

        accf = sb("acc", [P, max(NB * ROW, 6400)])[:, :]
        acc = accf[:, 0:NB * ROW].rearrange("p (b r) -> p b r", r=ROW)
        iota_f = sb("iota_f", [P, P])
        pcol = sb("pcol", [P, 1])
        ident = sb("ident", [P, P])
        ones = sb("ones", [P, P])
        stat = sb("stat", [P, NB, 2])
        wnode = sb("wnode", [P, NB])
        kvw = sb("kvw", [P, 2, 2 * D])
        bkv = sb("bkv", [P, 2 * D])
        valid_last = sb("valid_last", [P, 1])
        first_base = sb("first_base", [P, NST + 1])
        block_base = sb("block_base", [P, NB])
        nodeval = sb("nodeval", [P, NB, 3, 2 * HG], BF16)

        G = sb("G", [P, 2, CT, ROW])
        sidx = sb("sidx", [P, 2, CT], I32)
        dstE = sb("dstE", [P, 2, CT])
        drow = sb("drow", [P, 2, P + 2], I32)
        shared = sb("shared", [P, CT * P // 2])
        dbc = shared[:, :].bitcast(I16)
        kv = shared[:, 0:4 * D].rearrange("p (a n) -> p a n", a=2)
        sq = shared[:, 4 * D:6 * D]
        xtk = shared[:, 6 * D:8 * D].rearrange("p (k n) -> p k n", k=2)
        oneT2 = sb("oneT2", [P, 2, ST_T * P], BF16)
        zb = sb("zb", [P, P], BF16)
        oneE = sb("oneE", [P, 2, ST_T, P])
        NV = 3 * 2 * HG
        nv = sb("nv", [P, SC, NV], BF16)
        cb = sb("cb", [P, SC])
        dl = sb("dl", [P, 2, SC, ST_T])
        work = sb("work", [P, 2236])
        o = [0]

        def piece(n, p=P):
            a = work[0:p, o[0]:o[0] + n]
            o[0] += n
            return a

        dn = piece(CT * 8)
        U = piece(3 * P)
        s_e, sT, bw = (U[:, k * P:(k + 1) * P] for k in range(3))
        pn = piece(2 * (P + 1))
        We = pn[:, 0:2 * P]
        oneT = [oneT2[:, 0, :], oneT2[:, 1, :], U[:, 0:2 * P].bitcast(BF16), We.bitcast(BF16)]
        pen, neq = pn[:, 0:P + 1], pn[:, P + 1:]
        sng = piece(1)
        x4 = piece(4)
        first = piece(P)
        fw = piece(P)
        c2 = piece(2)
        fac = piece(HG)
        g0 = o[0]
        gh = piece(6 * HG * (CT + 1), 1)
        first_block = work[32:33, g0:g0 + NST + 1].bitcast(I32)
        extra_tile = work[64:65, g0:g0 + NB - 1].bitcast(I32)
        extra_at = work[96:97, g0:g0 + NB - 1].bitcast(I32)
        cin = piece(2 * P, 1)
        rl = piece(HG, 1)
        r8 = piece(2 * HG, 1)
        one0 = cin[:, 0:P]
        rs = sb("rs", [P, 2, 16])

        Gf = G[:, :, :, :].rearrange("p a t r -> p (a t r)")
        go = [0]

        def gpiece(n):
            a = Gf[:, go[0]:go[0] + n]
            go[0] += n
            return a

        bar = sem("bar")
        phase = [0]
        d32_in = sem("d32_in")
        ld_w, ld_i, iota_done = sem("ld_w"), sem("ld_i"), sem("iota_done")
        prep_mm, prep_dve, vch = sem("prep_mm"), sem("prep_dve"), sem("vch")
        idx_in = [sem("idx_in0"), sem("idx_in1")]
        idx_f, idx_t, idx_out = sem("idx_f"), sem("idx_t"), sem("idx_out")
        idx_stored = [sem("idx_stored0"), sem("idx_stored1")]
        d16_ready, d16_stored = sem("d16_ready"), sem("d16_stored")
        x_in = [sem("x_in0"), sem("x_in1")]
        vnm = sem("vnm")
        x_var, x_std, xn_ready, xn_T, xt_ready, xp_ready, row_ready = (
            sem("x_var"), sem("x_std"), sem("xn_ready"), sem("xn_T"), sem("xt_ready"), sem("xp_ready"), sem("row_ready"))
        row_split, vln = sem("row_split"), sem("vln")
        tab_out = [sem("tab_out0"), sem("tab_out1")]
        xt_out = [sem("xt_out0"), sem("xt_out1")]
        idx_ld = [sem("idx_ld0"), sem("idx_ld1")]
        rows_in = [sem("rows_in0"), sem("rows_in1")]
        drow_in = [sem("drow_in0"), sem("drow_in1")]
        dste_in = [sem("dste_in0"), sem("dste_in1")]
        nv_ready, xo_ready, xo_used = sem("nv_ready"), sem("xo_ready"), sem("xo_used")
        g_ready, a_scaled, vfac = sem("g_ready"), sem("a_scaled"), sem("vfac")
        xe_ready, xe_done, vx, dste_used = sem("xe_ready"), sem("xe_done"), sem("vx"), sem("dste_used")
        dbc_in, xtk_in = sem("dbc_in"), sem("xtk_in")
        ot_ready, ot_used, d_read, s_ready, sT_ready = (
            sem("ot_ready"), sem("ot_used"), sem("d_read"), sem("s_ready"), sem("sT_ready"))
        x4_ready, r_ready, gh_ready, c_ready, mm_ready, m_ready = (
            sem("x4_ready"), sem("r_ready"), sem("gh_ready"), sem("c_ready"), sem("mm_ready"), sem("m_ready"))
        u_ready, w_ready, one0_ready, fac_ready = sem("u_ready"), sem("w_ready"), sem("one0_ready"), sem("fac_ready")
        oe_ready, oe_used, sum_added = sem("oe_ready"), sem("oe_used"), sem("sum_added")
        vck = sem("vck")
        kv_mm, kv_biased, kv_sq, kv_var, kv_std, kv_norm, kv_acc = (
            sem("kv_mm"), sem("kv_biased"), sem("kv_sq"), sem("kv_var"), sem("kv_std"), sem("kv_norm"), sem("kv_acc"))
        pace = sem("pace")
        mw_in, mw_pe, mw_dve = sem("mw_in"), sem("mw_pe"), sem("mw_dve")
        n_in = [sem("n_in0"), sem("n_in1")]
        h_mm, h_act, o_mm, e_out, rec_ready, u_scaled, t_ready, sc_ready, x_scaled, x_read = (
            sem("h_mm"), sem("h_act"), sem("o_mm"), sem("e_out"), sem("rec_ready"), sem("u_scaled"), sem("t_ready"),
            sem("sc_ready"), sem("x_scaled"), sem("x_read"))
        x_ready = sem("x_ready")
        v_var, v_std = sem("v_var"), sem("v_std")
        z_ready, b_ready, vna, vnp, vns, vpl = (
            sem("z_ready"), sem("b_ready"), sem("vna"), sem("vnp"), sem("vns"), sem("vpl"))
        b_out = [sem("b_out0"), sem("b_out1")]
        vth, cnt_ready, cnt_sum = sem("vth"), sem("cnt_ready"), sem("cnt_sum")
        y_stored = sem("y_stored")
        f_in, perm_out, perm_in, z_turned, zt_ready = (
            sem("f_in"), sem("perm_out"), sem("perm_in"), sem("z_turned"), sem("zt_ready"))
        z_in = [sem("z_in0"), sem("z_in1")]
        b_in = [sem("b_in0"), sem("b_in1")]
        f_up, f_act, f_down, f_y, f_out, vff = (
            sem("f_up"), sem("f_act"), sem("f_down"), sem("f_y"), [sem("f_out0"), sem("f_out1")], sem("vff"))

        block = ctx.enter_context(nc.Block())

        def settled(eng, semaphore, value):
            eng.wait_ge(semaphore, value)
            eng.sem_inc(pace, 1)

        def barrier(eng, n):
            eng.drain().then_inc(bar, 1)
            eng.wait_ge(bar, 5 * n)

        go[0] = 0
        wcat = gpiece(2 * ROW).rearrange("p (c n) -> p c n", c=2)
        attb = gpiece(2 * D).rearrange("p (a n) -> p a n", a=2)
        wtmp = gpiece(2 * D).rearrange("p (a n) -> p a n", a=2)
        wraw = gpiece(2 * 3 * D).rearrange("p (c n) -> p c n", c=2)
        braw = gpiece(3 * D)
        wmean = gpiece(48)
        iotaI = gpiece(512).bitcast(I32)
        pcolI = gpiece(1).bitcast(I32)
        iota_w = gpiece(512)
        samp = gpiece(NST)
        sampF = gpiece(NST)
        tmp512 = gpiece(512)
        small = gpiece(16)
        diagT = gpiece(P)
        go[0] += go[0] % 2
        idxI = gpiece(2 * 2 * P).bitcast(I32).rearrange("p (a k n) -> p a k n", a=2, k=2)
        idxF = gpiece(2 * 2 * P).rearrange("p (a k n) -> p a k n", a=2, k=2)
        idxO = gpiece(2 * 2 * P).rearrange("p (a k n) -> p a k n", a=2, k=2)
        ao = [0]

        def apiece(n):
            a = accf[:, ao[0]:ao[0] + n]
            ao[0] += n
            return a

        d32 = gpiece(1024).bitcast(I32)
        d16 = dbc[:, 0:NT]
        xin = apiece(2 * 2 * D).rearrange("p (a t n) -> p a t n", a=2, t=2)
        xn = apiece(2 * 2 * D).rearrange("p (a t n) -> p a t n", a=2, t=2)
        xt = apiece(2 * 4 * P).rearrange("p (a k n) -> p a k n", a=2, k=2)
        xrow = apiece(2 * 2 * ROW).rearrange("p (a t n) -> p a t n", a=2, t=2)
        bst = apiece(16)
        var = apiece(8).rearrange("p (a k) -> p a k", a=2)
        mv = apiece(8).rearrange("p (a t k) -> p a t k", a=2, t=2)
        res = apiece(2 * 2 * 8).rearrange("p (a t n) -> p a t n", a=2, t=2)
        DQ = (NT + 1023) // 1024

        x_v = x.rearrange("(q t p) n -> q p t n", t=2, p=P)
        tab_v = tab_d.rearrange("(q t p) n -> q p t n", t=2, p=P)
        z_v = z_d.rearrange("(q t p) n -> q p t n", t=2, p=P)
        base_v = base_d.rearrange("(q t p) n -> q p t n", t=2, p=P)
        out_v = out.rearrange("(q t p) n -> q p t n", t=2, p=P)
        src_t = src.rearrange("(t e) -> t e", e=P)
        dst_t = dst[1:1 + EP].rearrange("(t e) -> t e", e=P)
        NG = (NT + P - 1) // P

        def grp(g):
            return min(P, NT - g * P)

        R2 = (NP - 1) // 2

        def first_steps(eng, step):
            step(0, 0, 0)
            with eng.Fori(0, R2 - 1) as r:
                step(2 * r + 1, 1, r)
                step(2 * r + 2, 0, r + 1)
            step(NP - 2, 1, R2 - 1, True, False)
            step(NP - 1, 0, R2, False, False)

        def paired(eng, body):
            with eng.Fori(0, R2) as r:
                body(2 * r, 0, r)
                body(2 * r + 1, 1, r)
            body(NP - 1, 0, R2)

        go[0] = 0
        wq = gpiece(2 * D).rearrange("p (c n) -> p c n", c=2)
        wqT = gpiece(2 * D).rearrange("p (c n) -> p c n", c=2)
        kvd = gpiece(2 * P).rearrange("p (c n) -> p c n", c=2)
        m1T = gpiece(2 * D).rearrange("p (c n) -> p c n", c=2)
        w1m = gpiece(2 * D).rearrange("p (c n) -> p c n", c=2)
        wm = gpiece(2 * D).rearrange("p (c n) -> p c n", c=2)
        w2m = gpiece(2 * D).rearrange("p (c n) -> p c n", c=2)
        b1m = gpiece(2)
        bm = gpiece(2)
        bq = gpiece(2)
        kqb = gpiece(2)
        kcol = gpiece(2)
        vrow = gpiece(2 * CM).rearrange("p (k n) -> p k n", k=2)
        svk = gpiece(4)
        mt1 = gpiece(P)
        mt2 = gpiece(P)
        gbr = gpiece(D)
        b2r = gpiece(D)
        wrr = gpiece(D)
        brc = gpiece(1)
        go[0] += go[0] % 2

        def two_slots():
            return gpiece(2 * 2 * D).rearrange("p (s t n) -> p s t n", s=2, t=2)

        xl, xpl, t1, t2, t3, uu, x2, zz, bb = (two_slots() for _ in range(9))
        xtl = gpiece(2 * 2 * D).rearrange("p (s k n) -> p s k n", s=2, k=2)
        hT = gpiece(2 * D).rearrange("p (k n) -> p k n", k=2)
        junk = gpiece(D)
        var2 = gpiece(4)
        bst2 = gpiece(12)
        mv2 = gpiece(4).rearrange("p (t k) -> p t k", t=2)
        sc1 = gpiece(8).rearrange("p (s t k) -> p s t k", s=2, t=2)
        dsum, flg, wsp = (gpiece(2 * HG).rearrange("p (t h) -> p t h", t=2) for _ in range(3))
        rec, wrc = (gpiece(4 * HG).rearrange("p (s t h) -> p s t h", s=2, t=2) for _ in range(2))
        assert go[0] <= 2 * CT * ROW

        def load_mix(sp):
            wv = w_qkv.rearrange("(c p) (h n) -> p c h n", p=P, h=HM)
            for c in (0, 1):
                sp.dma_start(wq[:, c, :].rearrange("p (h n) -> p h n", h=HM), wv[:, c, :, 0:CM]).then_inc(mw_in, 16)
            sp.dma_start(w1m, m_w1.rearrange("(c p) n -> p c n", p=P)).then_inc(mw_in, 16)
            sp.dma_start(w2m, m_w2.rearrange("(c p) n -> p c n", p=P)).then_inc(mw_in, 16)
            bqv = b_qkv.rearrange("(c h n) -> c h n", c=2, n=3 * CM)[:, :, 0:CM]
            for c in (0, 1):
                sp.dma_start(b1m[:, c:c + 1], m_b1[c * P:(c + 1) * P][:, None]).then_inc(mw_in, 16)
                for h in range(P // CM):
                    sp.dma_start(bq[h * CM:(h + 1) * CM, c:c + 1], bqv[c, h][:, None]).then_inc(mw_in, 16)
            for k, a in ((0, kln_g), (1, kln_b)):
                for h in range(P // CM):
                    sp.dma_start(kcol[h * CM:(h + 1) * CM, k:k + 1], a[:, None]).then_inc(mw_in, 16)
            for k, a in ((0, vln_g), (1, vln_b)):
                sp.dma_start(vrow[:, k, :], a[None, :].to_broadcast([P, CM])).then_inc(mw_in, 16)
            sp.dma_start(gbr, g_bias[None, :].to_broadcast([P, D])).then_inc(mw_in, 16)
            sp.dma_start(b2r, m_b2[None, :].to_broadcast([P, D])).then_inc(mw_in, 16)
            sp.dma_start(wrr, f_wr.rearrange("d o -> o d").to_broadcast([P, D])).then_inc(mw_in, 16)
            sp.dma_start(brc, f_br[None, :].to_broadcast([P, 1])).then_inc(mw_in, 16)

        MW = 16 * (4 + 2 * (1 + P // CM) + 2 * (P // CM) + 2 + 4)

        def mix_weights_dve(dve, lk):
            v = nc.vector
            dve.wait_ge(mw_in, MW)
            lk(v.tensor_scalar(b2r, b2r, -1.0, None, ALU.add))
            lk(v.memset(kvd, 0.0))
            v.sem_inc(mw_dve, 1)
            gain = vrow[:, None, 0, :].to_broadcast([P, P // CM, CM])
            bias = vrow[:, None, 1, :].to_broadcast([P, P // CM, CM])

            def hv(a):
                return a.rearrange("p (h n) -> p h n", n=CM)

            for c in (0, 1):
                lk(v.tensor_scalar(mt1, bank[5][:, c * P:c * P + P], kcol[:, 0:1], None, ALU.mult))
                lk(v.tensor_tensor(hv(mt1), hv(mt1), gain, ALU.mult))
                lk(v.tensor_scalar(mt2, bank[6][:, c * P:c * P + P], kcol[:, 1:2], None, ALU.mult))
                lk(v.tensor_tensor(hv(mt2), hv(mt2), gain, ALU.mult))
                lk(v.tensor_tensor(mt1, mt1, mt2, ALU.add))
                lk(v.tensor_scalar(svk[:, 0:1], bank[5][:, 256 + c:257 + c], kcol[:, 0:1], None, ALU.mult))
                lk(v.scalar_tensor_tensor(svk[:, 0:1], kcol[:, 1:2], float(n_nodes), svk[:, 0:1], ALU.mult, ALU.add))
                lk(v.tensor_scalar(hv(mt2), bias, svk[:, 0:1], None, ALU.mult))
                lk(v.tensor_tensor(mt1, mt1, mt2, ALU.add))
                for h in range(P // CM):
                    r = slice(h * CM, (h + 1) * CM)
                    lk(v.tensor_scalar(kvd[r, c, r], mt1[r, r], 1.0 / n_nodes, None, ALU.mult))
            v.sem_inc(mw_dve, 1)
            dve.wait_ge(mw_pe, 1)
            for c in (0, 1):
                lk(v.tensor_copy(wqT[:, c, :], bank[c][:, 0:D]))
            v.sem_inc(mw_dve, 1)
            dve.wait_ge(mw_pe, 2)
            for c in (0, 1):
                lk(v.tensor_copy(m1T[:, c, :], bank[3 + c][:, 0:D]))
                lk(v.tensor_tensor(m1T[:, c, c * P:c * P + P], m1T[:, c, c * P:c * P + P], ident[:, :], ALU.add))
                lk(v.tensor_copy(kqb[:, c:c + 1], bank[2][:, c:c + 1]))
            v.sem_inc(mw_dve, 1)
            dve.wait_ge(mw_pe, 3)
            for c in (0, 1):
                lk(v.tensor_copy(wm[:, c, :], bank[c][:, 0:D]))
                lk(v.tensor_tensor(bm[:, c:c + 1], bank[2][:, 4 + c:5 + c], b1m[:, c:c + 1], ALU.add))

        def mix_weights_pe(pe):
            te = nc.tensor
            pe.wait_ge(mw_dve, 1)
            for c in (0, 1):
                for k in (0, 1):
                    last = te.transpose(bank[c][:, k * P:k * P + P], wq[:, k, c * P:c * P + P], ident[:, :])
            last.then_inc(mw_pe, 1)
            pe.wait_ge(mw_dve, 3)
            for c in (0, 1):
                te.matmul(bank[3 + c][:, 0:D], kvd[:, c, :], wqT[:, c, :], start=True, stop=True)
                last = te.matmul(bank[2][:, c:c + 1], kvd[:, c, :], bq[:, c:c + 1], start=True, stop=True)
            last.then_inc(mw_pe, 1)
            pe.wait_ge(mw_dve, 4)
            for c in (0, 1):
                for k in (0, 1):
                    te.matmul(bank[c][:, 0:D], m1T[:, k, c * P:c * P + P], w1m[:, k, :], start=(k == 0), stop=(k == 1))
            for c in (0, 1):
                for k in (0, 1):
                    last = te.matmul(bank[2][:, 4 + c:5 + c], w1m[:, k, c * P:c * P + P], kqb[:, k:k + 1], start=(k == 0), stop=(k == 1))
            last.then_inc(mw_pe, 1)

        def node_loads(sp):
            def load(q, s):
                sp.dma_start(xl[:, s, :, :], x_v[ds(q, 1)].rearrange("a p t n -> p (a t) n")).then_inc(n_in[s], 16)
                sp.dma_start(xpl[:, s, :, :], tab_v[ds(q, 1)].rearrange("a p t n -> p (a t) n")[:, :, 0:D]).then_inc(n_in[s], 16)
                sp.dma_start(xtl[:, s, :, :], xnT_d[ds(q, 1)].rearrange("a p (k n) -> p (a k) n", k=2)).then_inc(n_in[s], 16)

            def store(q, s):
                settled(sp, b_ready, q + 3)
                for view, rows in ((z_v, zz), (base_v, bb), (out_v, bb)):
                    sp.dma_start(view[ds(q, 1)].rearrange("a p t n -> p (a t) n"), rows[:, s, :, :]).then_inc(b_out[s], 16)

            def step(q, s):
                settled(sp, h_mm, q + 1)
                settled(sp, t_ready, q + 1)
                settled(sp, x_scaled, q + 1)
                load(q + 2, s)
                store(q, s)

            load(0, 0)
            load(1, 1)
            with sp.Fori(0, R2 - 1) as r:
                step(2 * r, 0)
                step(2 * r + 1, 1)
            step(NP - 3, 0)
            store(NP - 2, 1)
            store(NP - 1, 0)
            for s in (0, 1):
                sp.wait_ge(b_out[s], 48 * (R2 + 2 - s))

        def node_steps(eng, step):
            with eng.Fori(0, R2 - 1) as r:
                step(2 * r, 0, r, True)
                step(2 * r + 1, 1, r, True)
            step(NP - 3, 0, R2 - 1, True)
            step(NP - 2, 1, R2 - 1, True, False)
            step(NP - 1, 0, R2, False, False)

        def heads(a):
            return a.rearrange("p t (h n) -> p t h n", h=HG)

        def wide(a):
            return a[:, :, :, None].to_broadcast([P, 2, HG, CG])

        def node_dve(dve):
            v = nc.vector
            KNA, KNB = 7, 9

            def weights_of(q, s, r):
                ck = Chain(dve, vna, KNA * q)
                aq = acc[:, ds(2 * q, 2), D:ROW]
                ck(v.tensor_tensor(dsum, aq[:, :, 0:HG], aq[:, :, HG:2 * HG], ALU.add))
                ck(v.tensor_scalar(flg, dsum, 0.5, None, ALU.is_lt))
                v.tensor_tensor(wsp, aq[:, :, HG:2 * HG], flg, ALU.add)
                ck(v.tensor_tensor(dsum, dsum, flg, ALU.add))
                v.tensor_copy(sc1[:, s], stat[:, ds(2 * q, 2), :]).then_inc(sc_ready, 1)
                ck(v.reciprocal(rec[:, s], dsum))
                v.sem_inc(rec_ready, 1)
                ck(v.tensor_tensor(wrc[:, s], wsp, rec[:, s], ALU.mult))
                return ck

            def attention_of(q, s, r, ck):
                dve.wait_ge(n_in[s], 48 * r + 48)
                ck(v.tensor_tensor(heads(t1[:, s]), heads(xpl[:, s]), wide(wrc[:, s]), ALU.mult))
                dve.wait_ge(u_scaled, q + 1)
                ck(v.tensor_tensor(t1[:, s], t1[:, s], uu[:, s], ALU.add))
                v.sem_inc(t_ready, 1)
                assert ck.n == KNA, ck.n

            def step(q, s, r, more, more2=True):
                if more:
                    nxt = (q + 1, 1 - s, r + s)
                    na = weights_of(*nxt)
                ck = Chain(dve, vnp, KNB * q)
                dve.wait_ge(e_out, q + 1)
                dve.wait_ge(o_mm, q + 1)
                dve.wait_ge(b_ready, q + 1)
                ck(v.scalar_tensor_tensor(x2[:, s], t2[:, s], 1.0, bank[3 + s][:, :].rearrange("p (t n) -> p t n", t=2), ALU.min, ALU.add))
                ck(v.scalar_tensor_tensor(x2[:, s], t1[:, s], 0.0, x2[:, s], ALU.max, ALU.add))
                dve.wait_ge(x_ready, q + 1)
                ck(v.tensor_tensor(x2[:, s], x2[:, s], t3[:, s], ALU.add))
                v.sem_inc(x_read, 1)
                for t in (0, 1):
                    last = v.bn_stats(bst2[:, 6 * t:6 * t + 6], x2[:, s, t, :])
                ck(last)
                v.sem_inc(pace, 1)
                for t in (0, 1):
                    last = v.bn_aggr(mv2[:, t, :], bst2[:, 6 * t:6 * t + 6])
                ck(last)
                v.tensor_scalar(var2[:, 0:2], mv2[:, :, 1], EPS, None, ALU.add).then_inc(v_var, 1)
                if more:
                    attention_of(*nxt, na)
                dve.wait_ge(v_std, q + 1)
                ck(v.reciprocal(mv2[:, :, 1], var2[:, 2:4]))
                dve.wait_ge(b_out[s], 48 * r + 48)
                for t in (0, 1):
                    last = v.tensor_scalar(zz[:, s, t, :], x2[:, s, t, :], mv2[:, t, 0:1], mv2[:, t, 1:2], ALU.subtract, ALU.mult)
                ck(last)
                v.sem_inc(z_ready, 1)
                for t in (0, 1):
                    ck(v.scalar_tensor_tensor(junk, zz[:, s, t, :], 1.0, wrr, ALU.mult, ALU.mult, accum_out=wnode[:, ds(2 * q + t, 1)]))
                assert ck.n == KNB, ck.n

            lk = Chain(dve, vns)
            lk(v.scalar_tensor_tensor(stat[:, :, 0], stat[:, :, 0], -1.0, stat[:, :, 1], ALU.mult, ALU.mult))
            lk(v.tensor_scalar(stat[:, :, 1], stat[:, :, 1], 1.0, None, ALU.add))
            attention_of(0, 0, 0, weights_of(0, 0, 0))
            node_steps(dve, step)

        def node_pool(pool):
            g = nc.gpsimd
            pool.sem_inc(b_ready, 2)

            def scale_sums(q, s):
                pool.wait_ge(rec_ready, q + 1)
                g.tensor_tensor(heads(uu[:, s]), heads(acc[:, ds(2 * q, 2), 0:D]), wide(rec[:, s]), ALU.mult).then_inc(vpl, 1)
                pool.wait_ge(vpl, q + 1)
                g.tensor_tensor(uu[:, s], uu[:, s], gbr[:, None, :].to_broadcast([P, 2, D]), ALU.add).then_inc(u_scaled, 1)

            def add_b2(q, s):
                pool.wait_ge(x_scaled, q + 1)
                g.tensor_tensor(t3[:, s], t3[:, s], b2r[:, None, :].to_broadcast([P, 2, D]), ALU.add).then_inc(x_ready, 1)

            def step(q, s, r, more, more2=True):
                if more:
                    scale_sums(q + 1, 1 - s)
                    add_b2(q + 1, 1 - s)
                pool.wait_ge(z_ready, q + 1)
                pool.wait_ge(b_out[s], 48 * r + 48)
                g.tensor_tensor(bb[:, s], x2[:, s], zz[:, s], ALU.add).then_inc(b_ready, 1)

            scale_sums(0, 0)
            add_b2(0, 0)
            node_steps(pool, step)

        def node_act(act):
            a = nc.scalar
            act.sem_inc(b_out[0], 48)
            act.sem_inc(b_out[1], 48)

            def scale_x(q, s, r):
                act.wait_ge(n_in[s], 48 * r + 48)
                act.wait_ge(sc_ready, q + 1)
                act.wait_ge(x_read, q + 1)
                for t in (0, 1):
                    last = a.activation(t3[:, s, t, :], xl[:, s, t, :], ACT.Identity, bias=sc1[:, s, t, 0:1], scale=sc1[:, s, t, 1:2])
                last.then_inc(x_scaled, 1)

            def hidden(q):
                act.wait_ge(h_mm, q + 1)
                for k in (0, 1):
                    last = a.activation(hT[:, k, :], bank[0][:, k * D:k * D + D], ACT.Gelu, bias=bm[:, k:k + 1])
                last.then_inc(h_act, 1)

            def step(q, s, r, more, more2=True):
                if more:
                    hidden(q + 1)
                act.wait_ge(v_var, q + 1)
                a.activation(var2[:, 2:4], var2[:, 0:2], ACT.Sqrt).then_inc(v_std, 1)
                if more:
                    scale_x(q + 1, 1 - s, r + s)
                    exponent(q + 1, 1 - s)

            def exponent(q, s):
                act.wait_ge(t_ready, q + 1)
                a.activation(t2[:, s], t1[:, s], ACT.Exp).then_inc(e_out, 1)

            scale_x(0, 0, 0)
            hidden(0)
            exponent(0, 0)
            node_steps(act, step)

        def node_pe(pe):
            te = nc.tensor
            pe.sem_inc(x_read, 2)

            def up(q, s, r):
                pe.wait_ge(n_in[s], 48 * r + 48)
                for f in (0, 1):
                    for k in (0, 1):
                        last = te.matmul(bank[0][:, f * D:f * D + D], wm[:, k, f * P:f * P + P], xtl[:, s, k, :], start=(k == 0), stop=(k == 1))
                last.then_inc(h_mm, 1)

            def down(q, s):
                pe.wait_ge(x_read, q + 1)
                pe.wait_ge(h_act, q + 1)
                for t in (0, 1):
                    for k in (0, 1):
                        last = te.matmul(bank[3 + s][:, t * D:t * D + D], hT[:, k, t * P:t * P + P], w2m[:, k, :], start=(k == 0), stop=(k == 1))
                last.then_inc(o_mm, 1)

            def step(q, s, r, more, more2=True):
                if more:
                    down(q + 1, 1 - s)
                    if more2:
                        up(q + 2, s, r + 1)

            up(0, 0, 0)
            down(0, 0)
            up(1, 1, 0)
            node_steps(pe, step)

        o[0] = 0
        wp, cmpb, rank, sel, eqm = (piece(NB) for _ in range(5))
        wcnt = piece(8)
        lower = piece(P)
        bits = piece(4)
        bits_i = piece(4).bitcast(I32)
        place = piece(NB)
        place_i = piece(NB).bitcast(I32)
        entry = piece(2 * NB).rearrange("p (b k) -> p b k", k=2)

        def threshold_dve(dve, lk):
            v = nc.vector
            cnt, c0, sg, kp, pen_l, need = (wcnt[:, i:i + 1] for i in range(6))
            cur, cand, bi = bits_i[:, 0:1], bits_i[:, 1:2], bits_i[:, 2:3]
            bit, keep, thr = bits[:, 0:1], bits[:, 1:2], bits[:, 2:3]
            lastcol = slice(NB - 1, NB)
            lk(v.tensor_scalar(wnode[:, :], wnode[:, :], brc, None, ALU.add))
            lk(v.tensor_scalar(pen_l, valid_last[:, :], -1.0, 3.0 * BIG, ALU.add, ALU.mult))
            lk(v.tensor_scalar(wnode[:, lastcol], wnode[:, lastcol], valid_last[:, :], pen_l, ALU.mult, ALU.add))
            lk(v.tensor_scalar(lower, iota_f[:, 0:P], pcol[:, :], None, ALU.is_gt))
            lk(v.tensor_scalar(cmpb, wnode[:, :], 0.0, None, ALU.is_ge))
            lk(v.tensor_reduce(cnt, cmpb, AX, ALU.add))
            v.sem_inc(cnt_ready, 1)
            dve.wait_ge(cnt_sum, 1)
            lk(v.tensor_scalar(c0, bank[3][:, 0:1], float(K_SEL), None, ALU.is_ge))
            lk(v.tensor_scalar(sg, c0, 2.0, -1.0, ALU.mult, ALU.add))
            lk(v.tensor_scalar(kp, c0, float(2 * K_SEL - n_nodes - 1), float(n_nodes - K_SEL + 1), ALU.mult, ALU.add))
            lk(v.tensor_scalar(wp, wnode[:, :], sg, None, ALU.mult))
            lk(v.tensor_scalar(wp[:, lastcol], wp[:, lastcol], valid_last[:, :], pen_l, ALU.mult, ALU.add))
            lk(v.memset(bits_i, 0))
            lk(v.memset(bit, float(2 ** 30)))
            KTH = 8
            with dve.Fori(0, 31) as j:
                ck = Chain(dve, vth, KTH * j)
                ck(v.tensor_copy(bi, bit))
                ck(v.tensor_tensor(cand, cur, bi, ALU.bitwise_or))
                ck(v.tensor_scalar(cmpb, wp, cand.bitcast(FP32), None, ALU.is_ge))
                ck(v.tensor_reduce(cnt, cmpb, AX, ALU.add))
                v.sem_inc(cnt_ready, 1)
                dve.wait_ge(cnt_sum, j + 2)
                ck(v.tensor_tensor(keep, bank[3][:, 0:1], kp, ALU.is_ge))
                ck(v.tensor_tensor(bi, keep, bit, ALU.mult))
                ck(v.tensor_tensor(cur, cur, bi, ALU.bitwise_or))
                ck(v.tensor_scalar(bit, bit, 0.5, None, ALU.mult))
                assert ck.n == KTH
            lk(v.tensor_tensor(thr, cur.bitcast(FP32), sg, ALU.mult))
            lk(v.tensor_scalar(sel, wnode[:, :], thr, None, ALU.is_gt))
            lk(v.tensor_scalar(eqm, wnode[:, :], thr, None, ALU.is_equal))
            lk(v.tensor_reduce(cnt, sel, AX, ALU.add))
            v.sem_inc(cnt_ready, 1)
            dve.wait_ge(cnt_sum, 33)
            lk(v.tensor_scalar(need, bank[3][:, 0:1], -1.0, float(K_SEL), ALU.mult, ALU.add))
            tot = bank[4][:, 0:NB]
            lk(v.tensor_copy(cmpb, tot))
            lk(v.memset(wp, 0.0))
            lk(v.tensor_tensor_scan(rank, cmpb, wp, 0.0, ALU.add, ALU.add))
            lk(v.tensor_tensor(rank, rank, cmpb, ALU.subtract))
            lk(v.tensor_tensor(rank, rank, bank[5][:, 0:NB], ALU.add))
            lk(v.tensor_scalar(rank, rank, need, None, ALU.is_lt))
            lk(v.tensor_tensor(eqm, eqm, rank, ALU.mult))
            lk(v.tensor_tensor(sel, sel, eqm, ALU.add))
            v.sem_inc(cnt_ready, 1)
            dve.wait_ge(cnt_sum, 34)
            node_id, before = eqm, rank
            lk(v.tensor_scalar(node_id, block_base[:, :], pcol[:, :], None, ALU.add))
            lk(v.tensor_copy(cmpb, bank[4][:, 0:NB]))
            lk(v.tensor_tensor_scan(before, cmpb, wp, 0.0, ALU.add, ALU.add))
            lk(v.tensor_tensor(before, before, cmpb, ALU.subtract))
            lk(v.tensor_tensor(before, before, bank[5][:, 0:NB], ALU.add))
            lk(v.tensor_tensor(cmpb, node_id, before, ALU.subtract))
            lk(v.tensor_scalar(cmpb, cmpb, float(K_SEL), None, ALU.add))
            lk(v.tensor_tensor(before, before, cmpb, ALU.subtract))
            lk(v.tensor_tensor(before, before, sel, ALU.mult))
            lk(v.tensor_tensor(place, before, cmpb, ALU.add))
            lk(v.tensor_copy(place_i, place))
            lk(v.tensor_copy(entry[:, :, 0].bitcast(I32), node_id))
            lk(v.tensor_tensor(entry[:, :, 1], wnode[:, :], sel, ALU.mult))

        def threshold_pe(pe):
            te = nc.tensor
            pe.wait_ge(cnt_ready, 1)
            te.matmul(bank[3][:, 0:1], ones[:, :], wcnt[:, 0:1], start=True, stop=True).then_inc(cnt_sum, 1)
            with pe.Fori(0, 31) as j:
                pe.wait_ge(cnt_ready, j + 2)
                te.matmul(bank[3][:, 0:1], ones[:, :], wcnt[:, 0:1], start=True, stop=True).then_inc(cnt_sum, 1)
            pe.wait_ge(cnt_ready, 33)
            te.matmul(bank[4][:, 0:NB], ones[:, :], eqm, start=True, stop=True)
            te.matmul(bank[5][:, 0:NB], lower, eqm, start=True, stop=True)
            te.matmul(bank[3][:, 0:1], ones[:, :], wcnt[:, 0:1], start=True, stop=True).then_inc(cnt_sum, 1)
            pe.wait_ge(cnt_ready, 34)
            te.matmul(bank[4][:, 0:NB], ones[:, :], sel, start=True, stop=True)
            te.matmul(bank[5][:, 0:NB], lower, sel, start=True, stop=True).then_inc(cnt_sum, 1)

        go[0] = 0
        w1f = gpiece(2 * FH).rearrange("p (k n) -> p k n", k=2)
        w2f = gpiece(FC * D).rearrange("p (k n) -> p k n", k=FC)
        b1f = gpiece(FC)
        b2f = gpiece(D)
        hf = gpiece(2 * FC * D).rearrange("p (s f n) -> p s f n", s=2, f=FC)
        zl, bl, yo = (gpiece(2 * 2 * D).rearrange("p (s t n) -> p s t n", s=2, t=2) for _ in range(3))
        zt = gpiece(2 * 2 * D).rearrange("p (s k n) -> p s k n", s=2, k=2)
        ty = gpiece(2 * D).rearrange("p (t n) -> p t n", t=2)
        perm = gpiece(4 * NQ).rearrange("p (t k) -> p t k", k=2)
        assert go[0] <= 2 * CT * ROW

        def ffn_dma(sp):
            sp.dma_start(w1f, f_w1.rearrange("(k p) n -> p k n", p=P)).then_inc(f_in, 16)
            sp.dma_start(w2f, f_w2.rearrange("(k p) n -> p k n", p=P)).then_inc(f_in, 16)
            sp.dma_start(b1f, f_b1.rearrange("(k p) -> p k", p=P), allow_slow_non_contiguous=True).then_inc(f_in, 16)
            sp.dma_start(b2f, f_b2[None, :].to_broadcast([P, D])).then_inc(f_in, 16)

            sp.wait_ge(perm_out, 16 * NB)
            sp.dma_start(perm, perm_d[0:2 * NQ * P].rearrange("(t p) k -> p t k", p=P),
                         allow_slow_non_contiguous=True).then_inc(perm_in, 16)

        RF = (NQ - 1) // 2

        def rows_at(q, t):
            return bass.IndirectOffsetOnAxis(ap=perm[:, 2 * q + t, 0:1].bitcast(I32), axis=0)

        def ffn_pool(pool):
            g = nc.gpsimd
            for b in range(NB):
                g.indirect_dma_start(out=perm_d, out_offset=bass.IndirectOffsetOnAxis(ap=place_i[:, b:b + 1], axis=0),
                                     in_=entry[:, b, :], in_offset=None).then_inc(perm_out, 16)

            def gather(rows, table, q, signal):
                for t in (0, 1):
                    g.indirect_dma_start(out=rows[:, q % 2, t, :], out_offset=None, in_=table, in_offset=rows_at(q, t)).then_inc(signal[q % 2], 16)

            pool.sem_inc(y_stored, 2)
            pool.wait_ge(perm_in, 16)
            for q in (0, 1):
                gather(zl, z_d, q, z_in)
                gather(bl, base_d, q, b_in)
            pool.wait_ge(z_turned, 1)
            gather(zl, z_d, 2, z_in)
            for q in range(NQ):
                if q + 3 < NQ:
                    pool.wait_ge(z_turned, q + 2)
                    gather(zl, z_d, q + 3, z_in)
                pool.wait_ge(f_y, q + 1)
                if q:
                    pool.wait_ge(f_out[1 - q % 2], 32 * ((q + 1) // 2))
                    pool.sem_inc(y_stored, 1)
                for t in (0, 1):
                    g.indirect_dma_start(out=out, out_offset=rows_at(q, t), in_=yo[:, q % 2, t, :], in_offset=None).then_inc(f_out[q % 2], 16)
                if q + 2 < NQ:
                    gather(bl, base_d, q + 2, b_in)
            for s in (0, 1):
                pool.wait_ge(f_out[s], 32 * (RF + 1 - s))

        def ffn_pe(pe):
            te = nc.tensor
            pe.wait_ge(f_in, 64)

            def turn(q, s, u):
                pe.wait_ge(z_in[s], 32 * u + 32)
                if not isinstance(q, int) or q:
                    pe.wait_ge(zt_ready, q)
                for k in (0, 1):
                    for t in (0, 1):
                        last = te.transpose(bank[7][:, k * D + t * P:k * D + t * P + P], zl[:, s, t, k * P:k * P + P], ident[:, :])
                last.then_inc(z_turned, 1)

            def up(q, s, first=False):
                pe.wait_ge(zt_ready, q + 1)
                for j in range(FC // 2):
                    if not first:
                        pe.wait_ge(f_act, 4 * q - 3 + j)
                    for f in (2 * j, 2 * j + 1):
                        for k in (0, 1):
                            last = te.matmul(bank[j][:, (f % 2) * D:(f % 2) * D + D], w1f[:, k, f * P:f * P + P], zt[:, s, k, :],
                                             start=(k == 0), stop=(k == 1))
                    last.then_inc(f_up, 1)

            def down(q, s):
                pe.wait_ge(f_act, 4 * q + 4)
                for t in (0, 1):
                    for f in range(FC):
                        last = te.matmul(bank[5 + s][:, t * D:t * D + D], hf[:, s, f, t * P:t * P + P], w2f[:, f, :],
                                         start=(f == 0), stop=(f == FC - 1))
                last.then_inc(f_down, 1)

            turn(0, 0, 0)
            turn(1, 1, 0)
            up(0, 0, True)
            turn(2, 0, 1)
            up(1, 1)
            down(0, 0)
            with pe.Fori(1, RF) as r:
                turn(2 * r + 1, 1, r)
                up(2 * r, 0)
                down(2 * r - 1, 1)
                turn(2 * r + 2, 0, r + 1)
                up(2 * r + 1, 1)
                down(2 * r, 0)
            up(NQ - 1, 0)
            down(NQ - 2, 1)
            pe.wait_ge(f_y, NQ - 2)
            down(NQ - 1, 0)

        def ffn_act(act):
            a = nc.scalar
            act.wait_ge(f_in, 64)

            def body(q, s, first):
                for j in range(FC // 2):
                    act.wait_ge(f_up, 4 * q + j + 1)
                    if j == 0 and not first:
                        act.wait_ge(f_down, q - 1)
                    for f in (2 * j, 2 * j + 1):
                        last = a.activation(hf[:, s, f, :], bank[j][:, (f % 2) * D:(f % 2) * D + D], ACT.Gelu_apprx_tanh,
                                            bias=b1f[:, f:f + 1])
                    last.then_inc(f_act, 1)

            body(0, 0, True)
            body(1, 1, True)
            with act.Fori(1, RF) as r:
                body(2 * r, 0, False)
                body(2 * r + 1, 1, False)
            body(NQ - 1, 0, False)

        def ffn_dve(dve, lk):
            v = nc.vector
            dve.wait_ge(f_in, 64)
            KFF = 3

            def keep_z(q, s):
                dve.wait_ge(z_turned, q + 1)
                if not isinstance(q, int) or q >= 2:
                    dve.wait_ge(f_up, 4 * q - 4)
                v.tensor_copy(zt[:, s], bank[7][:, :].rearrange("p (k n) -> p k n", k=2)).then_inc(zt_ready, 1)

            def body(q, s, r, more=True):
                if more:
                    keep_z(q + 2, s)
                ck = Chain(dve, vff, KFF * q)
                dve.wait_ge(f_down, q + 1)
                ck(v.tensor_tensor(ty, bank[5 + s][:, :].rearrange("p (t n) -> p t n", t=2),
                                   b2f[:, None, :].to_broadcast([P, 2, D]), ALU.add))
                dve.wait_ge(b_in[s], 32 * r + 32)
                dve.wait_ge(y_stored, q + 1)
                for t in (0, 1):
                    ck(v.scalar_tensor_tensor(yo[:, s, t, :], ty[:, t, :], perm[:, ds(2 * q + t, 1), 1], bl[:, s, t, :], ALU.mult, ALU.add))
                v.sem_inc(f_y, 1)
                assert ck.n == KFF

            keep_z(0, 0)
            keep_z(1, 1)
            body(0, 0, 0)
            with dve.Fori(1, RF) as r:
                body(2 * r - 1, 1, r - 1)
                body(2 * r, 0, r)
            body(NQ - 2, 1, RF - 1, False)
            body(NQ - 1, 0, RF, False)
        @block.sync
        def _(sp):
            sp.dma_start(wcat[:, :, 0:D], Wg.rearrange("(c p) n -> p c n", p=P)).then_inc(ld_w, 16)
            sp.dma_start(attb[:, 0, :], att_src.rearrange("h c -> (h c)")[None, :].to_broadcast([P, D])).then_inc(ld_w, 16)
            sp.dma_start(attb[:, 1, :], att_dst.rearrange("h c -> (h c)")[None, :].to_broadcast([P, D])).then_inc(ld_w, 16)
            sp.dma_start(wraw, w_qkv.rearrange("(c p) n -> p c n", p=P)).then_inc(ld_w, 16)
            sp.dma_start(braw, b_qkv[None, :].to_broadcast([P, 3 * D])).then_inc(ld_w, 16)
            sp.dma_start(samp[0:1, 0:NST - 1].bitcast(I32),
                         dst[0:EP].rearrange("(a t s) -> a t s", a=1, s=ST_T * P)[:, 1:, 0],
                         allow_slow_non_contiguous=True).then_inc(ld_i, 16)
            def load_group(g):
                n = grp(g)
                sp.dma_start(idxI[0:n, g % 2, 0, :], src_t[g * P:g * P + n, :]).then_inc(idx_in[g % 2], 16)
                sp.dma_start(idxI[0:n, g % 2, 1, :], dst_t[g * P:g * P + n, :]).then_inc(idx_in[g % 2], 16)

            for g in range(min(2, NG)):
                load_group(g)
            for g in range(NG):
                n = grp(g)
                if g + 2 < NG:
                    sp.wait_ge(idx_f, g + 1)
                    load_group(g + 2)
                sp.wait_ge(idx_out, g + 1)
                sp.dma_start(srcE_d[:, g * P:g * P + n], idxO[:, g % 2, 0, 0:n].bitcast(I32)).then_inc(idx_stored[g % 2], 16)
                sp.dma_start(dstE_d[:, g * P:g * P + n], idxO[:, g % 2, 1, 0:n]).then_inc(idx_stored[g % 2], 16)
            for k in range(DQ):
                n = min(1024, NT - k * 1024)
                if k:
                    sp.wait_ge(d16_ready, k)
                sp.dma_start(d32[:, 0:n], dst[1:1 + EP].rearrange("(p t) -> p t", p=P)[:, k * 1024:k * 1024 + n]).then_inc(d32_in, 16)
            sp.wait_ge(d16_ready, DQ)
            sp.dma_start(dst16_d, d16).then_inc(d16_stored, 16)
            def load_x(q, s):
                sp.dma_start(xin[:, s, :, :], x_v[q]).then_inc(x_in[s], 16)

            def store(q, s, tick):
                settled(sp, row_ready, tick + 1)
                sp.dma_start(tab_v[q], xrow[:, s, :, :]).then_inc(tab_out[s], 16)
                sp.dma_start(xnT_d[q].rearrange("p (k n) -> p k n", k=2), xt[:, s, :, :]).then_inc(xt_out[s], 16)

            load_x(0, 0)
            load_x(1, 1)
            with sp.Fori(0, R2 - 1) as r:
                for u in (0, 1):
                    q = 2 * r + u
                    settled(sp, xn_ready, q + 1)
                    load_x(q + 2, u)
                    store(q, u, q)
            for q in range(NP - 3, NP):
                if q + 2 < NP:
                    settled(sp, xn_ready, q + 1)
                    load_x(q + 2, q % 2)
                store(q, q % 2, q)
            for s in (0, 1):
                sp.wait_ge(tab_out[s], 16 * (R2 + 2 - s))
                sp.wait_ge(xt_out[s], 16 * (R2 + 2 - s))
                sp.wait_ge(idx_stored[s], 32 * ((NG + 1 - s) // 2))
            sp.wait_ge(d16_stored, 16)
            barrier(sp, 1)
            def load_rows(c, s):
                sp.dma_start(sidx[:, s, :], srcE_d[:, ds(c * CT, CT)]).then_inc(idx_ld[s], 16)
                for h in range(HG):
                    win = dst[ds(c * (CT * P), CT * P)]
                    rowap = bass.AP(tensor=win.tensor, offset=win.offset, ap=[[P, CT], [1, P + 2]])
                    sp.dma_start(drow[h * CT:(h + 1) * CT, s, :], rowap).then_inc(drow_in[s], 16)

            def load_dst(c, s):
                sp.dma_start(dstE[:, s, :], dstE_d[:, ds(c * CT, CT)]).then_inc(dste_in[s], 16)

            def load_all_dst(c):
                sp.dma_start(dbc, dst16_d.rearrange("p t -> (p t)")[ds(c * (CT * P), CT * P)][None, :].to_broadcast([P, CT * P])).then_inc(dbc_in, 16)

            def load_xt(c):
                sp.dma_start(xtk, xnT_d[ds(c, 1)].rearrange("a p (k n) -> p (a k) n", k=2)).then_inc(xtk_in, 16)

            def feed(c, s, summed=True, rows=True):
                if summed:
                    settled(sp, dste_used, c)
                    load_dst(c + 1, 1 - s)
                settled(sp, d_read, c + 2)
                load_xt(c)
                settled(sp, kv_acc, c + 2)
                load_all_dst(c + 1)
                settled(sp, one0_ready, c + 1)
                if rows:
                    load_rows(c + 2, s)

            for c in (0, 1):
                load_rows(c, c)
                load_dst(c, c)
            load_all_dst(0)
            feed(0, 0, summed=False)
            with sp.Fori(0, R2 - 1) as r:
                feed(2 * r + 1, 1)
                feed(2 * r + 2, 0)
            feed(NCH - 2, 1, rows=False)
            settled(sp, d_read, NCH + 1)
            load_xt(NCH - 1)
            barrier(sp, 2)
            load_mix(sp)
            barrier(sp, 3)
            node_loads(sp)
            barrier(sp, 4)
            ffn_dma(sp)

        @block.gpsimd
        def _(pool):
            nc.gpsimd.iota(iotaI, [[1, 512]], base=0, channel_multiplier=0).then_inc(iota_done, 1)
            nc.gpsimd.iota(pcolI, [[0, 1]], base=0, channel_multiplier=1).then_inc(iota_done, 1)
            barrier(pool, 1)
            def gather(c, s, users, wait_free):
                pool.wait_ge(idx_ld[s], 16 * users)
                pool.sem_inc(pace, 1)
                for t in range(CT):
                    if wait_free and t % ST_T == 0:
                        pool.wait_ge(oe_used, SC * (c - 2) + t // ST_T + 3)
                        pool.sem_inc(pace, 1)
                    nc.gpsimd.indirect_dma_start(
                        out=G[:, s, t, :], out_offset=None, in_=tab_d,
                        in_offset=bass.IndirectOffsetOnAxis(ap=sidx[:, s, t:t + 1], axis=0)).then_inc(rows_in[s], 16)

            gather(0, 0, 1, False)
            gather(1, 1, 1, False)
            with pool.Fori(1, R2) as r:
                gather(2 * r, 0, r + 1, True)
                gather(2 * r + 1, 1, r + 1, True)
            gather(NCH - 1, 0, R2 + 1, True)
            barrier(pool, 2)
            barrier(pool, 3)
            node_pool(pool)
            barrier(pool, 4)
            ffn_pool(pool)

        @block.vector
        def _(dve):
            v = nc.vector
            lk = Chain(dve, vch)
            dve.wait_ge(iota_done, 2)
            lk(v.tensor_copy(iota_w, iotaI))
            lk(v.tensor_copy(iota_f[:, :], iotaI[:, 0:P]))
            lk(v.tensor_copy(pcol[:, :], pcolI))
            v.memset(ones[:, :], 1.0)
            v.memset(zb[:, :], 0.0)
            lk(v.tensor_scalar(ident[:, :], iota_f[:, 0:P], pcol[:, :], None, ALU.is_equal))
            lk(v.tensor_scalar(valid_last[:, :], pcol[:, :], float(TAIL), None, ALU.is_lt))
            dve.wait_ge(ld_i, 16)
            lk(v.tensor_copy(sampF[0:1, 0:NST - 1], samp[0:1, 0:NST - 1].bitcast(I32)))
            v.sem_inc(prep_dve, 1)
            T, pos, inv, p128 = (small[:, i:i + 1] for i in range(4))
            lk(v.tensor_scalar(p128, pcol[:, :], float(P), None, ALU.mult))
            lk(v.tensor_scalar(inv, pcol[:, :], 1.0, None, ALU.is_lt))
            lk(v.tensor_scalar(pos, pcol[:, :], float(NB - 1), None, ALU.is_gt))
            lk(v.tensor_tensor(inv, inv, pos, ALU.add))
            dve.wait_ge(prep_mm, 1)
            lk(v.tensor_scalar(tmp512[:, 0:NST - 1], bank[0][:, 0:NST - 1], p128, None, ALU.is_lt))
            lk(v.tensor_reduce(T, tmp512[:, 0:NST - 1], AX, ALU.add))
            lk(v.scalar_tensor_tensor(T, inv, 1e6, T, ALU.mult, ALU.add))
            lk(v.tensor_scalar(tmp512[:, 0:NST + 1], iota_w[:, 0:NST + 1], T, None, ALU.is_gt))
            lk(v.tensor_scalar(diagT, ident[:, :], T, None, ALU.mult))
            lk(v.tensor_scalar(block_base[:, :], iota_w[:, 0:NB], float(P), None, ALU.mult))
            v.sem_inc(prep_dve, 1)
            dve.wait_ge(prep_mm, 2)
            lk(v.tensor_scalar(first_base[:, :], bank[0][:, 0:NST + 1], float(P), None, ALU.mult))
            lk(v.tensor_copy(first_block, bank[0][32:33, 0:NST + 1]))
            for table in (extra_tile, extra_at):
                row = slice(64, 65) if table is extra_tile else slice(96, 97)
                lk(v.tensor_copy(table, bank[1][row, 1:NB]))
                lk(v.tensor_scalar(table, table, SC - 1, None, ALU.bitwise_and))
            at_f, hi_f = sampF[96:97, 0:NB - 1], tmp512[96:97, 0:NB - 1]
            lk(v.tensor_copy(at_f, extra_at))
            lk(v.tensor_scalar(hi_f, at_f, float(SC // 2), float(512 - SC // 2 * ST_T * NV), ALU.is_ge, ALU.mult))
            lk(v.scalar_tensor_tensor(extra_at, at_f, float(ST_T * NV), hi_f, ALU.mult, ALU.add))
            dve.wait_ge(ld_w, 80)
            for c in range(2):
                for a in range(2):
                    lk(v.tensor_tensor(wtmp[:, a, :], wcat[:, c, 0:D], attb[:, a, :], ALU.mult))
                lk(v.tensor_reduce(wcat[:, c, D:ROW], wtmp.rearrange("p a (h n) -> p (a h) n", h=HG), AX, ALU.add))

            def centre(dst_ap, raw):
                parts = raw.rearrange("p (h n) -> p h n", h=HM)
                for kind in (0, 1):
                    a = parts[:, :, CM * (1 + kind):CM * (2 + kind)]
                    m = wmean[:, 8 * kind:8 * kind + 8]
                    lk(v.tensor_reduce(m, a, AX, ALU.add))
                    lk(v.tensor_scalar(m, m, 1.0 / CM, None, ALU.mult))
                    lk(v.tensor_tensor(dst_ap[:, D * kind:D * (kind + 1)].rearrange("p (h n) -> p h n", h=HM), a,
                                       m[:, :, None].to_broadcast([P, HM, CM]), ALU.subtract))

            centre(kvw[:, 0, :], wraw[:, 0, :])
            centre(kvw[:, 1, :], wraw[:, 1, :])
            centre(bkv[:, :], braw)
            def cast(g):
                n = grp(g)
                dve.wait_ge(idx_in[g % 2], 32 * (g // 2 + 1))
                v.tensor_copy(idxF[0:n, g % 2, :, :], idxI[0:n, g % 2, :, :]).then_inc(idx_f, 1)

            cast(0)
            for g in range(NG):
                n = grp(g)
                if g + 1 < NG:
                    cast(g + 1)
                dve.wait_ge(idx_t, g + 1)
                if g >= 2:
                    dve.wait_ge(idx_stored[g % 2], 32 * (g // 2))
                turned = bank[2 + 4 * (g % 2)]
                v.tensor_copy(idxO[:, g % 2, 0, 0:n].bitcast(I32), turned[:, 0:n])
                v.tensor_copy(idxO[:, g % 2, 1, 0:n], turned[:, P:P + n]).then_inc(idx_out, 1)
            for k in range(DQ):
                n = min(1024, NT - k * 1024)
                dve.wait_ge(d32_in, 16 * (k + 1))
                lk(v.tensor_copy(d16[:, k * 1024:k * 1024 + n], d32[:, 0:n]))
                v.sem_inc(d16_ready, 1)
            KSP = 7

            def stats(q, s, u):
                dve.wait_ge(x_in[s], 16 * u + 16)
                ln = Chain(dve, vln, 2 * q)
                for t in (0, 1):
                    last = v.bn_stats(bst[:, 6 * t:6 * t + 6], xin[:, s, t, :])
                ln(last)
                v.sem_inc(pace, 1)
                for t in (0, 1):
                    last = v.bn_aggr(mv[:, s, t, :], bst[:, 6 * t:6 * t + 6])
                ln(last)
                v.tensor_scalar(var[:, s, 0:2], mv[:, s, :, 1], EPS, None, ALU.add).then_inc(x_var, 1)

            def norm(q, s, first=False):
                dve.wait_ge(x_std, q + 1)
                Chain(dve, vnm, q)(v.reciprocal(mv[:, s, :, 1], var[:, s, 2:4]))
                if not first:
                    dve.wait_ge(xn_T, q - 1)
                v.tensor_copy(stat[:, ds(2 * q, 2), :], mv[:, s])
                for t in (0, 1):
                    last = v.tensor_scalar(xn[:, s, t, :], xin[:, s, t, :], mv[:, s, t, 0:1], mv[:, s, t, 1:2],
                                           ALU.subtract, ALU.mult)
                last.then_inc(xn_ready, 1)

            def split(q, s):
                ln = Chain(dve, row_split, KSP * (q + 2))
                dve.wait_ge(row_ready, q + 1)
                r0 = res[:, 0, :, :]
                ln(v.tensor_copy(r0[:, :, 0:HG], xrow[:, s, :, D + HG:ROW]))
                ln(v.tensor_copy(r0[:, :, HG:2 * HG], xrow[:, s, :, D:D + HG]))
                for k in range(3):
                    part = nodeval[:, ds(2 * q, 2), k, :]
                    ln(v.tensor_copy(part, r0))
                    if k < 2:
                        ln(v.tensor_tensor(r0, r0, part, ALU.subtract))
                assert ln.n == KSP

            def step(q, s, u, more=True, more2=True):
                if more:
                    norm(q + 1, 1 - s, isinstance(q, int) and q == 0)
                if more2:
                    stats(q + 2, s, u + 1)
                if not isinstance(q, int) or q:
                    split(q - 1, 1 - s)

            v.sem_inc(row_split, 2 * KSP)
            v.sem_inc(tab_out[0], 16)
            v.sem_inc(tab_out[1], 16)
            v.sem_inc(xt_out[0], 16)
            v.sem_inc(xt_out[1], 16)
            stats(0, 0, 0)
            stats(1, 1, 0)
            norm(0, 0, True)
            first_steps(dve, step)
            split(NP - 1, 0)
            barrier(dve, 1)

            GW = HG * (CT + 1)

            def ghv(i):
                return gh[:, i * GW:(i + 1) * GW]

            def ghh(i):
                return ghv(i).rearrange("p (h t) -> p h t", h=HG)

            lk(v.memset(accf, 0.0))
            lk(v.memset(gh, -BIG))
            for i in (0, 3):
                lk(v.memset(ghv(i), -3.0 * BIG))
            lk(v.memset(r8, 1.0))
            s3 = s_e.rearrange("p (h t) -> p t h", h=HG)
            dn3 = dn.rearrange("p (t k) -> p t k", k=8)
            U3 = U.rearrange("p (a t h) -> p a t h", a=3, h=HG)
            UA = U.rearrange("p (a n) -> p a n", a=3)
            W3 = We.rearrange("p (a t h) -> p a t h", a=2, h=HG)
            KCHUNK = 27
            H2 = CT // 2
            v.sem_inc(d_read, 1)
            v.sem_inc(kv_var, 1)
            v.sem_inc(vx, 1)

            def node_onehots(c, k0):
                for k in range(k0, k0 + 4):
                    if k0:
                        dve.wait_ge(ot_used, SC * c + k - 2)
                    v.tensor_scalar(oneT[k % 4], dbc[:, k * 512:k * 512 + 512],
                                    cb[:, k:k + 1], pcol[:, :], ALU.subtract, ALU.is_equal).then_inc(ot_ready, 1)

            def prep0(c, s, u, ck):
                dve.wait_ge(dste_in[s], 16 * u + 16)
                ck(v.tensor_copy(cb[:, :], first_base[:, ds(c * SC, SC)]))
                ck(v.tensor_tensor(dl[:, s], dstE[:, s].rearrange("p (k t) -> p k t", t=ST_T),
                                   cb[:, :, None].to_broadcast([P, SC, ST_T]), ALU.subtract))
                dve.wait_ge(dbc_in, 16 * c + 16)
                dve.wait_ge(a_scaled, c + 1)
                node_onehots(c, 0)

            def prep1(c, s, u, ck):
                node_onehots(c, 4)

            def prep2(c, s, u, ck, lo, hi):
                settled(dve, ot_used, SC * c + SC + 1)
                with dve.Fori(lo, hi) as e:
                    tl = dve.value_load(extra_tile[0:1, ds(e, 1)], min_val=0, max_val=SC - 1)
                    dve.wait_ge(xo_used, e + 1)
                    v.tensor_scalar(oneT[0], dbc[:, ds(tl * 512, 512)], block_base[:, ds(e + 1, 1)], pcol[:, :],
                                    ALU.subtract, ALU.is_equal).then_inc(xo_ready, 1)
                dve.wait_ge(drow_in[s], 64 * u + 64)
                ck(v.tensor_tensor(neq, drow[:, s, 0:P + 1], drow[:, s, 1:P + 2], ALU.not_equal))
                ck(v.tensor_tensor(sng, drow[:, s, 1:2], drow[:, s, P:P + 1], ALU.not_equal))
                dve.wait_ge(xo_used, hi + 1)
                for a in (0, 1):
                    last = v.tensor_reduce(dn3[:, a * H2:a * H2 + H2, :],
                                           one[:, a, 0:H2 * NV].rearrange("p (t j k) -> p t k j", j=3, k=8), AX, ALU.add)
                ck(last)
                v.sem_inc(d_read, 1)
                dve.wait_ge(rows_in[s], 16 * CT * u + 16 * CT)
                v.tensor_tensor(s3, G[:, s, :, D:D + HG], dn3[:, :, HG:2 * HG], ALU.max).then_inc(s_ready, 1)
                v.tensor_scalar(pen, neq, -BIG, None, ALU.mult)
                ck(v.tensor_scalar(sng, sng, -BIG, None, ALU.mult))
                ck(v.tensor_scalar(x4[:, 2:3], pen[:, 0:1], sng, None, ALU.add))
                ck(v.tensor_scalar(x4[:, 3:4], pen[:, P:P + 1], sng, None, ALU.add))

            def add_bias(c, t, ck):
                dve.wait_ge(kv_mm, 2 * c + t + 1)
                v.tensor_tensor(kv[:, t, :], bank[7][:, :], bkv[:, :], ALU.add).then_inc(kv_biased, 1)

            def reduce_squares(c, t, ck):
                dve.wait_ge(kv_sq, 2 * c + t + 1)
                ck(v.tensor_reduce(rs[:, t, :], sq.rearrange("p (g n) -> p g n", n=CM), AX, ALU.add))
                v.sem_inc(kv_var, 1)

            def prep3(c, s, u, ck):
                dve.wait_ge(sT_ready, c + 1)
                v.tensor_copy(sT, bank[1][:, 0:P])
                ck(v.tensor_copy(first, bank[1][:, P:2 * P]))
                ck(v.tensor_tensor_scan(fw, pen[:, 0:P], sT, -BIG, ALU.add, ALU.max))
                ck(v.tensor_tensor_scan(bw[:, ::-1], pen[:, 1:P + 1][:, ::-1], sT[:, ::-1], -BIG, ALU.add, ALU.max))
                v.tensor_copy(x4[:, 0:1], fw[:, P - 1:P])
                v.tensor_copy(x4[:, 1:2], bw[:, 0:1]).then_inc(x4_ready, 1)

            def prep4(c, s, u, ck):
                dve.wait_ge(r_ready, c + 1)
                pr = bank[2][0:1, :].rearrange("p (k h t) -> p k h t", k=4, h=HG)
                v.tensor_copy(ghh(0)[:, :, 1:CT + 1], pr[:, 2])
                v.tensor_copy(ghh(1)[:, :, 1:CT + 1], pr[:, 0])
                v.tensor_copy(ghh(3)[:, :, 0:CT], pr[:, 3])
                ck(v.tensor_copy(ghh(4)[:, :, 0:CT], pr[:, 1]))
                ck(v.tensor_tensor_scan(ghv(2), ghv(0), ghv(1), -BIG, ALU.add, ALU.max))
                ck(v.tensor_tensor_scan(ghv(5)[:, ::-1], ghv(3)[:, ::-1], ghv(4)[:, ::-1], -BIG, ALU.add, ALU.max))
                dve.wait_ge(fac_ready, c + 1)
                v.tensor_copy(cin[:, 0:P].rearrange("p (h t) -> p h t", h=HG), ghh(2)[:, :, 0:CT])
                v.tensor_copy(cin[:, P:2 * P].rearrange("p (h t) -> p h t", h=HG), ghh(5)[:, :, 1:CT + 1]).then_inc(gh_ready, 1)
                dve.wait_ge(kv_acc, c + 1)
                add_bias(c, 0, ck)

            def prep5(c, s, u, ck):
                dve.wait_ge(c_ready, c + 1)
                ck(v.tensor_copy(c2, bank[1][:, 2 * P:2 * P + 2]))
                v.tensor_tensor_scan(fw, pen[:, 0:P], sT, c2[:, 0:1], ALU.add, ALU.max)
                ck(v.tensor_tensor_scan(bw[:, ::-1], pen[:, 1:P + 1][:, ::-1], sT[:, ::-1], c2[:, 1:2], ALU.add, ALU.max))
                v.tensor_tensor(fw, fw, bw, ALU.max).then_inc(mm_ready, 1)
                reduce_squares(c, 0, ck)
                add_bias(c, 1, ck)

            def prep6(c, s, u, ck):
                v.tensor_tensor(U3[:, 0], G[:, s, :, D:D + HG], dn3[:, :, 0:HG], ALU.add)
                v.tensor_tensor(U3[:, 1], dn3[:, :, HG:2 * HG], dn3[:, :, 0:HG], ALU.add)
                dve.wait_ge(m_ready, c + 1)
                ck(v.tensor_tensor(U3[:, 2], bank[1][:, 272:272 + P].rearrange("p (h t) -> p t h", h=HG), dn3[:, :, 0:HG], ALU.add))
                ck(v.scalar_tensor_tensor(U, U, 0.2, U, ALU.mult, ALU.max))
                ck(v.tensor_tensor(UA[:, 0:2], UA[:, 0:2],
                                   U[:, None, 2 * P:3 * P].to_broadcast([P, 2, P]), ALU.subtract))
                ck(v.tensor_tensor(rl, ghh(1)[:, :, 0], dn3[0:1, 0, 0:HG], ALU.add))
                ck(v.scalar_tensor_tensor(rl, rl, 0.2, rl, ALU.mult, ALU.max))
                ck(v.tensor_tensor(rl, rl, U3[0:1, 2, 0, :], ALU.subtract))
                v.tensor_scalar(rl, rl, 0.0, None, ALU.min).then_inc(u_ready, 1)
                v.tensor_copy(ghh(1)[:, :, 0], ghh(2)[:, :, CT])
                v.tensor_scalar(one0, iota_f[0:1, 0:P], cb[0:1, 0:1], dstE[0:1, s, 0:1], ALU.add, ALU.is_equal).then_inc(one0_ready, 1)
                reduce_squares(c, 1, ck)
                v.tensor_scalar(rs[:, :, :], rs[:, :, :], 1.0 / CM, EPS, ALU.mult, ALU.add).then_inc(kv_var, 1)

            def prep7(c, s, u, ck):
                dve.wait_ge(kv_std, c + 1)
                ck(v.tensor_scalar(sng, block_base[:, ds(2 * c + 1, 1)], pcol[:, :], float(n_nodes), ALU.add, ALU.is_lt))
                ck(v.reciprocal(rs[:, :, :], rs[:, :, :]))
                ck(v.tensor_scalar(rs[:, 1, :], rs[:, 1, :], sng, None, ALU.mult))
                for t in (0, 1):
                    last = v.tensor_tensor(kv[:, t, :].rearrange("p (g n) -> p g n", n=CM), kv[:, t, :].rearrange("p (g n) -> p g n", n=CM),
                                           rs[:, t, :][:, :, None].to_broadcast([P, 16, CM]), ALU.mult)
                last.then_inc(kv_norm, 1)
                dve.wait_ge(w_ready, c + 1)
                v.tensor_copy(G[:, s, :, D:D + HG], W3[:, 0])
                v.tensor_tensor(G[:, s, :, D + HG:ROW], W3[:, 1], first.rearrange("p (h t) -> p t h", h=HG), ALU.mult)
                gm = G[:, s, :, 0:D].rearrange("p t (h n) -> p t h n", h=HG)
                for k in range(SC - ACT_ST):
                    q4 = slice(k * ST_T, k * ST_T + ST_T)
                    last = v.tensor_tensor(gm[:, q4], gm[:, q4], W3[:, 0, q4][:, :, :, None].to_broadcast([P, ST_T, HG, CG]), ALU.mult)
                last.then_inc(g_ready, 1)

            preps = (prep0, prep1, prep2, prep3, prep4, prep5, prep6, prep7)

            def sum_extras(c, s, lo, hi):
                dve.wait_ge(sum_added, SC * c + 2)
                dve.wait_ge(fac_ready, c + 2)
                fk = Chain(dve, vfac, 3 * c)
                fk(v.tensor_scalar(fac, bank[1][:, 400 + HG:400 + 2 * HG], -1.0, 1.0, ALU.mult, ALU.add))
                fk(v.tensor_tensor(fac, fac, bank[1][:, 400:400 + HG], ALU.add))
                am = acc[:, ds(lo, 1), 0:D].rearrange("p a (h n) -> p (a h) n", h=HG)
                at = acc[:, ds(lo, 1), D:ROW].rearrange("p a (k h) -> p (a k) h", h=HG)
                v.tensor_tensor(am, am, fac[:, :, None].to_broadcast([P, HG, CG]), ALU.mult)
                fk(v.tensor_tensor(at, at, fac[:, None, :].to_broadcast([P, 2, HG]), ALU.mult))
                v.sem_inc(pace, 1)
                with dve.Fori(lo, hi) as e:
                    tl = dve.value_load(extra_tile[0:1, ds(e, 1)], min_val=0, max_val=SC - 1)
                    dve.wait_ge(vx, e + 1)
                    v.scalar_tensor_tensor(oneE[:, 0], iota_f[:, None, :].to_broadcast([P, ST_T, P]), block_base[:, ds(e + 1, 1)],
                                           dstE[:, s, ds(tl * ST_T, ST_T)][:, :, None].to_broadcast([P, ST_T, P]),
                                           ALU.add, ALU.is_equal).then_inc(xe_ready, 1)
                    dve.wait_ge(xe_done, e + 1)
                    a = acc[:, ds(e + 1, 1), :].rearrange("p a r -> p (a r)")
                    v.tensor_tensor(a, a, bank[3][:, 0:ROW], ALU.add).then_inc(vx, 1)
                dve.wait_ge(vx, hi + 1)
                v.sem_inc(dste_used, 1)

            def edge_onehots(c, s, k):
                dve.wait_ge(oe_used, SC * c + k + 1)
                v.tensor_tensor(oneE[:, k % 2], iota_f[:, None, :].to_broadcast([P, ST_T, P]),
                                dl[:, s, k, :, None].to_broadcast([P, ST_T, P]), ALU.is_equal).then_inc(oe_ready, 1)

            def add_sum(c, k, b):
                dve.wait_ge(oe_used, SC * c + k + 3)
                dve.wait_ge(sum_added, SC * c + k + 2)
                a = acc[:, ds(b, 1), :].rearrange("p a r -> p (a r)")
                v.tensor_tensor(a, a, bank[3 + k % 2][:, 0:ROW], ALU.add).then_inc(sum_added, 1)

            def first_blocks(eng, c, n):
                return [eng.value_load(first_block[0:1, ds((c + j) * SC, 1)], min_val=0, max_val=NB - 1) for j in range(n)]

            def edge_step(c, s, nxt, u):
                ck = Chain(dve, vck, nxt * KCHUNK) if nxt is not None else None
                if c is None:
                    at = [0] + first_blocks(dve, nxt, 2)
                else:
                    at = first_blocks(dve, c, 3 if nxt is not None else 2)
                    sum_extras(c, s, at[0], at[1])
                    edge_onehots(c, s, 0)
                    b = at[0]
                for k in range(SC):
                    if c is not None and k + 1 < SC:
                        edge_onehots(c, s, k + 1)
                    if nxt is not None:
                        preps[k](nxt, 1 - s, u, ck, *(at[1:3] if k == 2 else ()))
                    if c is not None:
                        here = b
                        if k + 1 < SC:
                            v.sem_inc(pace, 1)
                            b = dve.value_load(first_block[0:1, ds(c * SC + k + 1, 1)], min_val=0, max_val=NB - 1)
                        add_sum(c, k, here)
                assert ck is None or ck.n == KCHUNK, ck.n

            edge_step(None, 1, 0, 0)
            with dve.Fori(0, R2) as r:
                edge_step(2 * r, 0, 2 * r + 1, r)
                edge_step(2 * r + 1, 1, 2 * r + 2, r + 1)
            edge_step(NCH - 1, 0, None, 0)
            dve.wait_ge(sum_added, SC * NCH + 2)
            barrier(dve, 2)
            mix_weights_dve(dve, lk)
            barrier(dve, 3)
            node_dve(dve)
            threshold_dve(dve, lk)
            barrier(dve, 4)
            ffn_dve(dve, lk)

        @block.scalar
        def _(act):
            a = nc.scalar

            def std(q, s):
                act.wait_ge(x_var, q + 1)
                a.activation(var[:, s, 2:4], var[:, s, 0:2], ACT.Sqrt).then_inc(x_std, 1)

            def turned(q, s, u):
                act.wait_ge(xn_T, q + 1)
                act.wait_ge(xt_out[s], 16 * u + 16)
                a.copy(xt[:, s, :, :], bank[3][:, :].rearrange("p (k n) -> p k n", k=2)).then_inc(xt_ready, 1)

            def rows(q, s, u):
                act.wait_ge(tab_out[s], 16 * u + 16)
                act.wait_ge(row_split, 7 * (q + 1))
                for t in (0, 1):
                    act.wait_ge(xp_ready, 2 * q + t + 1)
                    last = a.copy(xrow[:, s, t, :], bank[4 + t][:, 0:ROW])
                last.then_inc(row_ready, 1)

            def step(q, s, u, more=True, more2=True):
                rows(q, s, u)
                if more:
                    turned(q + 1, 1 - s, u + s)
                if more2:
                    std(q + 2, s)

            std(0, 0)
            std(1, 1)
            turned(0, 0, 0)
            first_steps(act, step)
            barrier(act, 1)

            Wt = We.rearrange("p (a t h) -> p a t h", a=2, h=HG)
            act.sem_inc(a_scaled, 1)

            def edge_act(c, s):
                for k in range(SC):
                    b = act.value_load(first_block[0:1, ds(c * SC + k, 1)], min_val=0, max_val=NB - 1)
                    if k == 0:
                        act.wait_ge(ot_used, SC * c + 1)
                    last = a.copy(nv[:, k, :], nodeval[:, ds(b, 1), :, :].rearrange("p a j k -> p (a j k)"))
                last.then_inc(nv_ready, 1)
                for t in (0, 1):
                    act.wait_ge(kv_biased, 2 * c + t + 1)
                    act.wait_ge(kv_var, 3 * c + t + 1)
                    a.activation(sq, kv[:, t, :], ACT.Square).then_inc(kv_sq, 1)
                act.wait_ge(u_ready, c + 1)
                a.activation(We, U[:, 0:2 * P], ACT.Exp)
                a.activation(r8[:, 0:HG], rl, ACT.Exp).then_inc(w_ready, 1)
                act.wait_ge(kv_var, 3 * c + 4)
                a.activation(rs[:, :, :], rs[:, :, :], ACT.Sqrt).then_inc(kv_std, 1)
                act.wait_ge(w_ready, c + 1)
                for t in range(CT - ACT_ST * ST_T, CT):
                    for h in range(HG):
                        g = G[:, s, t, h * CG:(h + 1) * CG]
                        last = a.activation(g, g, ACT.Copy, scale=Wt[:, 0, t, h:h + 1])
                last.then_inc(a_scaled, 1)

            paired(act, lambda c, s, r: edge_act(c, s))
            barrier(act, 2)
            barrier(act, 3)
            node_act(act)
            barrier(act, 4)
            ffn_act(act)

        @block.tensor
        def _(pe):
            te = nc.tensor
            pe.wait_ge(prep_dve, 1)
            te.matmul(bank[0][:, 0:NST - 1], ones[0:1, :], sampF[0:1, 0:NST - 1], start=True, stop=True).then_inc(prep_mm, 1)
            pe.wait_ge(prep_dve, 2)
            te.matmul(bank[0][:, 0:NST + 1], ones[:, :], tmp512[:, 0:NST + 1], start=True, stop=True)
            te.matmul(bank[1][:, 0:P], ones[:, :], diagT, start=True, stop=True).then_inc(prep_mm, 1)
            for g in range(NG):
                n = grp(g)
                pe.wait_ge(idx_f, g + 1)
                if g >= 2:
                    pe.wait_ge(idx_out, g - 1)
                turned = bank[2 + 4 * (g % 2)]
                te.transpose(turned[:, 0:n], idxF[0:n, g % 2, 0, :], ident[0:n, 0:n])
                te.transpose(turned[:, P:P + n], idxF[0:n, g % 2, 1, :], ident[0:n, 0:n]).then_inc(idx_t, 1)

            def turn(q, s):
                pe.wait_ge(xn_ready, q + 1)
                for k in (0, 1):
                    for t in (0, 1):
                        last = te.transpose(bank[3][:, k * 256 + t * P:k * 256 + t * P + P], xn[:, s, t, k * P:k * P + P], ident[:, :])
                last.then_inc(xn_T, 1)

            def project(q, s):
                pe.wait_ge(xt_ready, q + 1)
                for t in (0, 1):
                    for k in (0, 1):
                        last = te.matmul(bank[4 + t][:, 0:ROW], xt[:, s, k, t * P:t * P + P], wcat[:, k, :], start=(k == 0), stop=(k == 1))
                    last.then_inc(xp_ready, 1)

            def step(q, s, u, more=True, more2=True):
                if not isinstance(q, int) or q:
                    pe.wait_ge(row_ready, q)
                project(q, s)
                if more:
                    turn(q + 1, 1 - s)

            turn(0, 0)
            first_steps(pe, step)
            barrier(pe, 1)

            pe.sem_inc(ot_used, 1)
            pe.sem_inc(xo_used, 1)
            pe.sem_inc(oe_used, 2)
            pe.sem_inc(sum_added, 2)
            pe.sem_inc(kv_acc, 1)
            pe.sem_inc(fac_ready, 1)
            zr = nodeval[:, :, :, :].rearrange("p b j k -> p (b j k)")
            for kbank in (5, 6):
                for z0 in range(0, 512, P):
                    last = te.matmul(bank[kbank][:, z0:z0 + P], zb[:, :], zr[:, 0:P], start=True, stop=False, skip_group_check=True)

            def node_values(c, k0):
                if k0 == 0:
                    pe.wait_ge(d_read, c + 1)
                    for a in (0, 1):
                        for z0 in (0, SC * NV):
                            te.matmul(one[:, a, z0:z0 + SC * NV], zb[:, :], zr[:, 0:SC * NV], start=True, stop=False, skip_group_check=True)
                    pe.wait_ge(nv_ready, c + 1)
                for k in range(k0, k0 + 4):
                    pe.wait_ge(ot_ready, SC * c + k + 1)
                    for t in range(ST_T):
                        at = (k * ST_T + t) % (CT // 2) * NV
                        last = te.matmul(one[:, 2 * k // SC, at:at + NV], oneT[k % 4][:, t * P:t * P + P], nv[:, k, :],
                                         start=False, stop=False, skip_group_check=True)
                    last.then_inc(ot_used, 1)

            def extra_values(c, lo, hi):
                with pe.Fori(lo, hi) as e:
                    at = pe.value_load(extra_at[0:1, ds(e, 1)], min_val=0, max_val=1024 - ST_T * NV)
                    pe.wait_ge(xo_ready, e + 1)
                    for t in range(ST_T):
                        last = te.matmul(onef[:, ds(at + t * NV, NV)], oneT[0][:, t * P:t * P + P],
                                         nodeval[:, ds(e + 1, 1), :, :].rearrange("p a j k -> p (a j k)"),
                                         start=False, stop=False, skip_group_check=True)
                    last.then_inc(xo_used, 1)

            def kv_product(c, t):
                if t:
                    pe.wait_ge(kv_biased, 2 * c + 1)
                else:
                    pe.wait_ge(xtk_in, 16 * c + 16)
                for k in (0, 1):
                    last = te.matmul(bank[7][:, :], xtk[:, k, t * P:t * P + P], kvw[:, k, :], start=(k == 0), stop=(k == 1))
                last.then_inc(kv_mm, 1)

            def after(c, k):
                if k == 0:
                    node_values(c, 0)
                elif k == 1:
                    node_values(c, 4)
                elif k == 2:
                    pe.wait_ge(s_ready, c + 1)
                    te.transpose(bank[1][:, 0:P], s_e, ident[:, :])
                    te.transpose(bank[1][:, P:2 * P], neq[:, 0:P], ident[:, :]).then_inc(sT_ready, 1)
                elif k == 3:
                    pe.wait_ge(x4_ready, c + 1)
                    for j in range(4):
                        last = te.transpose(bank[2][0:1, j * P:j * P + P], x4[:, j:j + 1], ident[:, :])
                    last.then_inc(r_ready, 1)
                    kv_product(c, 0)
                elif k == 4:
                    pe.wait_ge(gh_ready, c + 1)
                    pe.sem_inc(pace, 1)
                    te.transpose(bank[1][:, 2 * P:2 * P + 1], cin[:, 0:P], ident[0:1, 0:1])
                    te.transpose(bank[1][:, 2 * P + 1:2 * P + 2], cin[:, P:2 * P], ident[0:1, 0:1]).then_inc(c_ready, 1)
                    kv_product(c, 1)
                elif k == 5:
                    pe.wait_ge(mm_ready, c + 1)
                    te.transpose(bank[1][:, 272:272 + P], fw, ident[:, :]).then_inc(m_ready, 1)
                elif k == 7:
                    pe.wait_ge(kv_norm, c + 1)
                    for t in (0, 1):
                        for h2 in (0, 1):
                            te.matmul(bank[5][:, h2 * P:h2 * P + P], kv[:, t, h2 * P:h2 * P + P], kv[:, t, D + h2 * P:D + h2 * P + P],
                                      start=False, stop=False, skip_group_check=True)
                            te.matmul(bank[5][:, 256 + h2:257 + h2], kv[:, t, h2 * P:h2 * P + P], ones[:, 0:1],
                                      start=False, stop=False, skip_group_check=True)
                        last = te.matmul(bank[6][:, 0:D], ones[:, :], kv[:, t, D:2 * D], start=False, stop=False, skip_group_check=True)
                    last.then_inc(kv_acc, 1)
                    pe.wait_ge(w_ready, c + 1)
                    pe.wait_ge(one0_ready, c + 1)
                    te.matmul(bank[1][:, 400:400 + 2 * HG], one0, r8, start=True, stop=True).then_inc(fac_ready, 1)

            def sum_extras(c, s, lo, hi):
                pe.wait_ge(g_ready, c + 1)
                settled(pe, a_scaled, c + 2)
                with pe.Fori(lo, hi) as e:
                    tl = pe.value_load(extra_tile[0:1, ds(e, 1)], min_val=0, max_val=SC - 1)
                    rows = G[:, s, ds(tl * ST_T, ST_T), :]
                    pe.wait_ge(xe_ready, e + 1)
                    for k in range(ST_T):
                        last = te.matmul(bank[3][:, 0:ROW], oneE[:, 0, k, :], rows[:, k, :],
                                         start=(k == 0), stop=(k == ST_T - 1))
                    last.then_inc(xe_done, 1)
                pe.wait_ge(vx, hi + 1)

            def sum_rows(c, s, k):
                pe.wait_ge(oe_ready, SC * c + k + 1)
                pe.wait_ge(sum_added, SC * c + k + 1)
                for t in range(ST_T):
                    last = te.matmul(bank[3 + k % 2][:, 0:ROW], oneE[:, k % 2, t, :], G[:, s, k * ST_T + t, :],
                                     start=(t == 0), stop=(t == ST_T - 1))
                last.then_inc(oe_used, 1)

            def edge_step(c, s, nxt):
                start = nxt if c is None else c
                at = [pe.value_load(first_block[0:1, ds((start + j) * SC, 1)], min_val=0, max_val=NB - 1)
                      for j in range(2 + (c is not None and nxt is not None))]
                if c is not None:
                    sum_extras(c, s, at[0], at[1])
                for k in range(SC):
                    if nxt is not None and k == 2:
                        extra_values(nxt, at[-2], at[-1])
                    if c is not None:
                        sum_rows(c, s, k)
                    if nxt is not None:
                        after(nxt, k)

            edge_step(None, 1, 0)
            with pe.Fori(0, R2) as r:
                edge_step(2 * r, 0, 2 * r + 1)
                edge_step(2 * r + 1, 1, 2 * r + 2)
            edge_step(NCH - 1, 0, None)
            barrier(pe, 2)
            mix_weights_pe(pe)
            barrier(pe, 3)
            node_pe(pe)
            threshold_pe(pe)
            barrier(pe, 4)
            ffn_pe(pe)


_F32 = ["L0_gnn_W", "L0_gnn_att_src", "L0_gnn_att_dst", "L0_gnn_bias", "L0_mix_w_qkv", "L0_mix_b_qkv", "L0_mix_kln_g",
        "L0_mix_kln_b", "L0_mix_vln_g", "L0_mix_vln_b", "L0_mix_w1", "L0_mix_b1", "L0_mix_w2", "L0_mix_b2", "L0_ffn_wr",
        "L0_ffn_br", "L0_ffn_w1", "L0_ffn_b1", "L0_ffn_w2", "L0_ffn_b2"]


def kernel(**inputs):
    import concourse.bacc as bacc
    from concourse.bass_utils import run_bass_kernel_spmd

    nc = bacc.Bacc("TRN2", target_bir_lowering=False, num_devices=1)
    x = np.asarray(inputs["x"])
    src, dst = np.asarray(inputs["src"]), np.asarray(inputs["dst"])
    n, e = x.shape[0], src.shape[0]
    npad = -(-n // P) * P
    ep = -(-e // (P * CT)) * (P * CT)
    arrays = {"x_in": np.zeros((npad, x.shape[1]), x.dtype), "src_in": np.zeros((ep,), src.dtype),
              "dst_in": np.full((ep + 2,), npad - 1, dst.dtype)}
    arrays["x_in"][:n] = x
    arrays["src_in"][:e] = src
    arrays["dst_in"][1:1 + e] = dst
    arrays["dst_in"][0] = -1
    for name in _F32:
        arrays[name] = np.ascontiguousarray(inputs[name])
    args = [nc.dram_tensor(k, a.shape, mybir.dt.from_np(a.dtype), kind="ExternalInput").ap() for k, a in arrays.items()]
    out = nc.dram_tensor("out", (npad, x.shape[1]), FP32, kind="ExternalOutput").ap()
    gps_kernel(nc, n, e, *args, out)
    r = run_bass_kernel_spmd(nc, [arrays], core_ids=[0])
    return r.results[0]["out"][:n]
```
